# Optimizing a Trainium2 kernel written in Bass

```python
import numpy as np
import jax
import jax.numpy as jnp

def _softmax(x, axis=-1):
    return jax.nn.softmax(x, axis=axis)

def _gelu(x):
    return jax.nn.gelu(x, approximate=True)

def _silu(x):
    return jax.nn.silu(x)

def _sigmoid(x):
    return jax.nn.sigmoid(x)

def _layernorm(x, axis=-1, eps=1e-05):
    m = jnp.mean(x, axis=axis, keepdims=True)
    v = jnp.var(x, axis=axis, keepdims=True)
    return (x - m) / jnp.sqrt(v + eps)

def _scatter_add(tgt, idx, src, axis=0):
    return tgt.at[idx].add(src)

def _segment_sum(src, seg, n):
    return jax.ops.segment_sum(src, seg, n)
kernel_name = 'mk_xattn_ffn_d4_seqx_r8_f6d955'

def setup_inputs(seed: int=0):
    np.random.seed(seed)
    _w = jnp.asarray

    def _rec_inputs():
        import jax
        import jax.numpy as jnp
        _rk = jax.random.key(seed)
        x = -0.0002928 + 1 * jax.random.normal(jax.random.fold_in(_rk, 1), (4, 512, 128), jnp.float32)
        _lenS = 512 - jax.random.randint(jax.random.fold_in(_rk, 7), (4,), 0, max(1, 512 // 4) + 1, jnp.int32)
        _lenS2 = 32 - jax.random.randint(jax.random.fold_in(_rk, 8), (4,), 0, max(1, 32 // 4) + 1, jnp.int32)
        _ctx_1024P = jax.random.normal(jax.random.fold_in(_rk, 11), (4, 16, 128), jnp.float32)
        _ctx_1024c = jax.random.dirichlet(jax.random.fold_in(_rk, 511), 0.3 * jnp.ones((16,), jnp.float32), (4, 32))
        _ctx_1024t = jnp.einsum('bsk,bkd->bsd', _ctx_1024c, _ctx_1024P)
        _ctx_1024t = _ctx_1024t * jax.lax.rsqrt(jnp.mean(jnp.square(_ctx_1024t)) + 1e-12) * 0.953939
        ctx_1024 = -1.39393e-06 + 0.999914 * (_ctx_1024t + 0.3 * jax.random.normal(jax.random.fold_in(_rk, 611), (4, 32, 128), jnp.float32))
        _validS = jnp.arange(512)[None, :] < _lenS[:, None]
        _validS2 = jnp.arange(32)[None, :] < _lenS2[:, None]
        _causal = jnp.tril(jnp.ones((512, 512), dtype=bool))
        mask_Bx1xS2_if1 = jnp.where(jnp.ones((4, 1, 32), dtype=bool), 1, 0).astype(jnp.int32)
        mask_BxSxS2_if1 = jnp.where(jnp.ones((4, 512, 32), dtype=bool), 1, 0).astype(jnp.int32)
        return (x, ctx_1024, mask_Bx1xS2_if1, mask_BxSxS2_if1)
    x, ctx_1024, mask_Bx1xS2_if1, mask_BxSxS2_if1 = _rec_inputs()

    def _L0_xattn_setup():
        import jax, jax.numpy as jnp
        import numpy as np
        D_MODEL = 128
        H = 16
        D_K = D_MODEL // H
        key = jax.random.key(seed)
        ks = jax.random.split(key, 8)
        B, S = (2, 256)
        q = jax.random.normal(ks[0], (B, S, D_MODEL), dtype=jnp.float32)
        k = jax.random.normal(ks[1], (B, S, D_MODEL), dtype=jnp.float32)
        v = jax.random.normal(ks[2], (B, S, D_MODEL), dtype=jnp.float32)
        mask = jnp.ones((B, 1, S), dtype=jnp.int32)
        sc = 1.0 / np.sqrt(D_MODEL)
        Wq = jax.random.normal(ks[3], (D_MODEL, D_MODEL), dtype=jnp.float32) * sc
        Wk = jax.random.normal(ks[4], (D_MODEL, D_MODEL), dtype=jnp.float32) * sc
        Wv = jax.random.normal(ks[5], (D_MODEL, D_MODEL), dtype=jnp.float32) * sc
        Wo = jax.random.normal(ks[6], (D_MODEL, D_MODEL), dtype=jnp.float32) * sc
        return {'q': q, 'k': k, 'v': v, 'mask': mask, 'Wq': Wq, 'Wk': Wk, 'Wv': Wv, 'Wo': Wo}
    _L0_xattn_all = _L0_xattn_setup()
    _L0_xattn_in = {k: v for k, v in _L0_xattn_all.items() if k in ('Wq', 'Wk', 'Wv', 'Wo')}
    del _L0_xattn_all

    def _L0_ffn_setup():
        import jax, jax.numpy as jnp
        import numpy as np
        E = 8
        K = 2
        D = 128
        key = jax.random.key(seed)
        k0, k1, k2, k3 = jax.random.split(key, 4)
        x = jax.random.normal(k0, (2, 256, D), dtype=jnp.float32)
        gate_w = jax.random.normal(k1, (D, E), dtype=jnp.float32) * 0.02
        fc_w = jax.random.normal(k2, (E, D, 4 * D), dtype=jnp.float32) * 0.02
        proj_w = jax.random.normal(k3, (E, 4 * D, D), dtype=jnp.float32) * 0.02
        return {'x': x, 'gate_w': gate_w, 'fc_w': fc_w, 'proj_w': proj_w}
    _L0_ffn_all = _L0_ffn_setup()
    _L0_ffn_in = {k: v for k, v in _L0_ffn_all.items() if k in ('gate_w', 'fc_w', 'proj_w')}
    del _L0_ffn_all

    def _L1_xattn_setup():
        import jax, jax.numpy as jnp
        import numpy as np
        EMBED = 128
        B, S = (4, 512)
        INV_SCALE = float(EMBED ** 0.5)
        key = jax.random.key(seed)
        ks = jax.random.split(key, 6)
        std = 1.0 / np.sqrt(EMBED)
        return {'query': jax.random.normal(ks[0], (B, S, EMBED), jnp.float32), 'key': jax.random.normal(ks[1], (B, S, EMBED), jnp.float32), 'value': jax.random.normal(ks[2], (B, S, EMBED), jnp.float32), 'Wq': jax.random.normal(ks[3], (EMBED, EMBED), jnp.float32) * std, 'bq': jnp.zeros((EMBED,), jnp.float32), 'Wk': jax.random.normal(ks[4], (EMBED, EMBED), jnp.float32) * std, 'bk': jnp.zeros((EMBED,), jnp.float32), 'Wv': jax.random.normal(ks[5], (EMBED, EMBED), jnp.float32) * std, 'bv': jnp.zeros((EMBED,), jnp.float32)}
    _L1_xattn_all = _L1_xattn_setup()
    _L1_xattn_in = {k: v for k, v in _L1_xattn_all.items() if k in ('Wq', 'bq', 'Wk', 'bk', 'Wv', 'bv')}
    del _L1_xattn_all

    def _L1_ffn_setup():
        import jax, jax.numpy as jnp
        import numpy as np
        HIDDEN = 128
        NUM_EXPERTS = 8
        TOP_K = 2
        B, S = (4, 128)
        key = jax.random.key(seed)
        ks = jax.random.split(key, 8)
        H, E = (HIDDEN, NUM_EXPERTS)
        sc = lambda fan_in: 1.0 / np.sqrt(fan_in)
        x = jax.random.normal(ks[0], (B, S, H), dtype=jnp.float32)
        Wr = jax.random.uniform(ks[1], (H, E), minval=-sc(H), maxval=sc(H), dtype=jnp.float32)
        br = jax.random.uniform(ks[2], (E,), minval=-sc(H), maxval=sc(H), dtype=jnp.float32)
        W1 = jax.random.uniform(ks[3], (E, H, 2 * H), minval=-sc(H), maxval=sc(H), dtype=jnp.float32)
        b1 = jax.random.uniform(ks[4], (E, 2 * H), minval=-sc(H), maxval=sc(H), dtype=jnp.float32)
        W2 = jax.random.uniform(ks[5], (E, 2 * H, H), minval=-sc(2 * H), maxval=sc(2 * H), dtype=jnp.float32)
        b2 = jax.random.uniform(ks[6], (E, H), minval=-sc(2 * H), maxval=sc(2 * H), dtype=jnp.float32)
        return {'x': x, 'Wr': Wr, 'br': br, 'W1': W1, 'b1': b1, 'W2': W2, 'b2': b2}
    _L1_ffn_all = _L1_ffn_setup()
    _L1_ffn_in = {k: v for k, v in _L1_ffn_all.items() if k in ('Wr', 'br', 'W1', 'b1', 'W2', 'b2')}
    del _L1_ffn_all

    def _L2_xattn_setup():
        import jax, jax.numpy as jnp
        import numpy as np
        key = jax.random.key(seed)
        ks = jax.random.split(key, 5)
        b, n_q, n_kv = (16, 128, 512)
        query_dim, context_dim, heads, dim_head = (128, 128, 16, 64)
        inner = heads * dim_head
        x = jax.random.normal(ks[0], (b, n_q, query_dim), dtype=jnp.float32)
        context = jax.random.normal(ks[1], (b, n_kv, context_dim), dtype=jnp.float32)
        Wq = jax.random.normal(ks[2], (query_dim, inner), dtype=jnp.float32) * query_dim ** (-0.5)
        Wkv = jax.random.normal(ks[3], (context_dim, 2 * inner), dtype=jnp.float32) * context_dim ** (-0.5)
        Wout = jax.random.normal(ks[4], (inner, query_dim), dtype=jnp.float32) * inner ** (-0.5)
        bout = jnp.zeros((query_dim,), dtype=jnp.float32)
        return {'x': x, 'context': context, 'Wq': Wq, 'Wkv': Wkv, 'Wout': Wout, 'bout': bout}
    _L2_xattn_all = _L2_xattn_setup()
    _L2_xattn_in = {k: v for k, v in _L2_xattn_all.items() if k in ('Wq', 'Wkv', 'Wout', 'bout')}
    del _L2_xattn_all

    def _L2_ffn_setup():
        import jax, jax.numpy as jnp
        import numpy as np
        B, S, D_MODEL, D_HIDDEN = (4, 256, 128, 512)

        def act_quant(x):
            scale = 127.0 / jnp.clip(jnp.max(jnp.abs(x), axis=-1, keepdims=True), 1e-05)
            return jnp.clip(jnp.round(x * scale), -128, 127) / scale

        def weight_quant(w):
            scale = 1.0 / jnp.clip(jnp.mean(jnp.abs(w)), 1e-05)
            return jnp.clip(jnp.round(w * scale), -1, 1) / scale

        def bit_linear(x, w):
            xq = x + jax.lax.stop_gradient(act_quant(x) - x)
            wq = w + jax.lax.stop_gradient(weight_quant(w) - w)
            return jnp.einsum('bsd,hd->bsh', xq, wq)

        def depthwise_conv1d(x_bcl, w, b):
            y = jax.lax.conv_general_dilated(x_bcl, w, window_strides=(1,), padding=[(1, 1)], dimension_numbers=('NCH', 'OIH', 'NCH'), feature_group_count=x_bcl.shape[1])
            return y + b[None, :, None]
        key = jax.random.key(seed)
        ks = jax.random.split(key, 5)
        lim1 = 1.0 / np.sqrt(D_MODEL)
        lim2 = 1.0 / np.sqrt(D_HIDDEN)
        limc = 1.0 / np.sqrt(3.0)
        return {'x': jax.random.normal(ks[0], (B, S, D_MODEL), dtype=jnp.float32), 'w1': jax.random.uniform(ks[1], (D_HIDDEN, D_MODEL), jnp.float32, -lim1, lim1), 'conv_w': jax.random.uniform(ks[2], (D_HIDDEN, 1, 3), jnp.float32, -limc, limc), 'conv_b': jax.random.uniform(ks[3], (D_HIDDEN,), jnp.float32, -limc, limc), 'w2': jax.random.uniform(ks[4], (D_MODEL, D_HIDDEN), jnp.float32, -lim2, lim2)}
    _L2_ffn_all = _L2_ffn_setup()
    _L2_ffn_in = {k: v for k, v in _L2_ffn_all.items() if k in ('w1', 'conv_w', 'conv_b', 'w2')}
    del _L2_ffn_all

    def _L3_xattn_setup():
        import jax, jax.numpy as jnp
        import numpy as np
        N_HEAD = 16
        N_EMBD = 128
        DIM_K = N_EMBD // N_HEAD

        def _split_heads(x):
            B, S, _ = x.shape
            return x.reshape(B, S, N_HEAD, DIM_K).transpose(0, 2, 1, 3)
        key = jax.random.key(seed)
        ks = jax.random.split(key, 11)
        B, S, D = (2, 256, N_EMBD)
        s = 1.0 / np.sqrt(D)
        inp = {'q': jax.random.normal(ks[0], (B, S, D), jnp.float32), 'k': jax.random.normal(ks[1], (B, S, D), jnp.float32), 'v': jax.random.normal(ks[2], (B, S, D), jnp.float32), 'mask': jnp.ones((B, S, S), jnp.int32), 'Wq': jax.random.normal(ks[3], (D, D), jnp.float32) * s, 'bq': jnp.zeros((D,), jnp.float32), 'Wk': jax.random.normal(ks[4], (D, D), jnp.float32) * s, 'bk': jnp.zeros((D,), jnp.float32), 'Wv': jax.random.normal(ks[5], (D, D), jnp.float32) * s, 'bv': jnp.zeros((D,), jnp.float32), 'Wo': jax.random.normal(ks[6], (D, D), jnp.float32) * s, 'bo': jnp.zeros((D,), jnp.float32)}
        return inp
    _L3_xattn_all = _L3_xattn_setup()
    _L3_xattn_in = {k: v for k, v in _L3_xattn_all.items() if k in ('Wq', 'bq', 'Wk', 'bk', 'Wv', 'bv', 'Wo', 'bo')}
    del _L3_xattn_all

    def _L3_ffn_setup():
        import jax, jax.numpy as jnp
        import numpy as np
        B, S, D = (2, 256, 128)
        F = 512
        E, K = (8, 2)
        EPS = 1e-09
        key = jax.random.key(seed)
        k1, k2, k3, k4 = jax.random.split(key, 4)
        x = jax.random.normal(k1, (B, S, D), dtype=jnp.float32)
        w_gate = jax.random.normal(k2, (D, E), dtype=jnp.float32) * 0.02
        w_gate_up = jax.random.normal(k3, (E, D, 2 * F), dtype=jnp.float32) * 0.02
        w_down = jax.random.normal(k4, (E, F, D), dtype=jnp.float32) * 0.02
        return {'x': x, 'w_gate': w_gate, 'w_gate_up': w_gate_up, 'w_down': w_down}
    _L3_ffn_all = _L3_ffn_setup()
    _L3_ffn_in = {k: v for k, v in _L3_ffn_all.items() if k in ('w_gate', 'w_gate_up', 'w_down')}
    del _L3_ffn_all
    return {'x': x, 'ctx_1024': ctx_1024, 'mask_Bx1xS2_if1': mask_Bx1xS2_if1, 'mask_BxSxS2_if1': mask_BxSxS2_if1, 'L0_xattn_Wq': _L0_xattn_in['Wq'], 'L0_xattn_Wk': _L0_xattn_in['Wk'], 'L0_xattn_Wv': _L0_xattn_in['Wv'], 'L0_xattn_Wo': _L0_xattn_in['Wo'], 'L0_ffn_gate_w': _L0_ffn_in['gate_w'], 'L0_ffn_fc_w': _L0_ffn_in['fc_w'], 'L0_ffn_proj_w': _L0_ffn_in['proj_w'], 'L1_xattn_Wq': _L1_xattn_in['Wq'], 'L1_xattn_bq': _L1_xattn_in['bq'], 'L1_xattn_Wk': _L1_xattn_in['Wk'], 'L1_xattn_bk': _L1_xattn_in['bk'], 'L1_xattn_Wv': _L1_xattn_in['Wv'], 'L1_xattn_bv': _L1_xattn_in['bv'], 'L1_ffn_Wr': _L1_ffn_in['Wr'], 'L1_ffn_br': _L1_ffn_in['br'], 'L1_ffn_W1': _L1_ffn_in['W1'], 'L1_ffn_b1': _L1_ffn_in['b1'], 'L1_ffn_W2': _L1_ffn_in['W2'], 'L1_ffn_b2': _L1_ffn_in['b2'], 'L2_xattn_Wq': _L2_xattn_in['Wq'], 'L2_xattn_Wkv': _L2_xattn_in['Wkv'], 'L2_xattn_Wout': _L2_xattn_in['Wout'], 'L2_xattn_bout': _L2_xattn_in['bout'], 'L2_ffn_w1': _L2_ffn_in['w1'], 'L2_ffn_conv_w': _L2_ffn_in['conv_w'], 'L2_ffn_conv_b': _L2_ffn_in['conv_b'], 'L2_ffn_w2': _L2_ffn_in['w2'], 'L3_xattn_Wq': _L3_xattn_in['Wq'], 'L3_xattn_bq': _L3_xattn_in['bq'], 'L3_xattn_Wk': _L3_xattn_in['Wk'], 'L3_xattn_bk': _L3_xattn_in['bk'], 'L3_xattn_Wv': _L3_xattn_in['Wv'], 'L3_xattn_bv': _L3_xattn_in['bv'], 'L3_xattn_Wo': _L3_xattn_in['Wo'], 'L3_xattn_bo': _L3_xattn_in['bo'], 'L3_ffn_w_gate': _L3_ffn_in['w_gate'], 'L3_ffn_w_gate_up': _L3_ffn_in['w_gate_up'], 'L3_ffn_w_down': _L3_ffn_in['w_down']}

def reference(x, ctx_1024, mask_Bx1xS2_if1, mask_BxSxS2_if1, L0_xattn_Wq, L0_xattn_Wk, L0_xattn_Wv, L0_xattn_Wo, L0_ffn_gate_w, L0_ffn_fc_w, L0_ffn_proj_w, L1_xattn_Wq, L1_xattn_bq, L1_xattn_Wk, L1_xattn_bk, L1_xattn_Wv, L1_xattn_bv, L1_ffn_Wr, L1_ffn_br, L1_ffn_W1, L1_ffn_b1, L1_ffn_W2, L1_ffn_b2, L2_xattn_Wq, L2_xattn_Wkv, L2_xattn_Wout, L2_xattn_bout, L2_ffn_w1, L2_ffn_conv_w, L2_ffn_conv_b, L2_ffn_w2, L3_xattn_Wq, L3_xattn_bq, L3_xattn_Wk, L3_xattn_bk, L3_xattn_Wv, L3_xattn_bv, L3_xattn_Wo, L3_xattn_bo, L3_ffn_w_gate, L3_ffn_w_gate_up, L3_ffn_w_down):
    import jax
    import jax.numpy as jnp

    def _L0_xattn_ref(q, k, v, mask, Wq, Wk, Wv, Wo):
        import jax, jax.numpy as jnp
        import numpy as np
        D_MODEL = 128
        H = 16
        D_K = D_MODEL // H
        B, Sq, _ = q.shape
        Sk = k.shape[1]

        def split_heads(x, W, S):
            return (x @ W.T).reshape(B, S, H, D_K).transpose(0, 2, 1, 3)
        qh = split_heads(q, Wq, Sq)
        kh = split_heads(k, Wk, Sk)
        vh = split_heads(v, Wv, Sk)
        scores = jnp.einsum('bhqd,bhkd->bhqk', qh, kh) / jnp.sqrt(jnp.asarray(D_K, qh.dtype))
        m = mask[:, None, :, :]
        scores = jnp.where(m == 0, jnp.asarray(-1000000000.0, scores.dtype), scores)
        p = jax.nn.softmax(scores, axis=-1)
        out = jnp.einsum('bhqk,bhkd->bhqd', p, vh)
        out = out.transpose(0, 2, 1, 3).reshape(B, Sq, H * D_K)
        return out @ Wo.T

    def _L0_ffn_ref(x, gate_w, fc_w, proj_w):
        import jax, jax.numpy as jnp
        import numpy as np
        E = 8
        K = 2
        D = 128
        orig_shape = x.shape
        d = orig_shape[-1]
        xt = x.reshape(-1, d)
        gates = jax.nn.softmax(xt @ gate_w, axis=-1)
        top_v, top_i = jax.lax.top_k(gates, K)
        top_v = top_v / jnp.sum(top_v, axis=-1, keepdims=True)
        h = jnp.einsum('nd,edf->enf', xt, fc_w)
        h = jax.nn.gelu(h, approximate=False)
        eo = jnp.einsum('enf,efd->end', h, proj_w)
        eo_nt = jnp.swapaxes(eo, 0, 1)
        sel = jnp.take_along_axis(eo_nt, top_i[:, :, None], axis=1)
        out = jnp.sum(sel * top_v[:, :, None], axis=1)
        return out.reshape(orig_shape)

    def _L1_xattn_ref(query, key, value, Wq, bq, Wk, bk, Wv, bv):
        import jax, jax.numpy as jnp
        import numpy as np
        EMBED = 128
        B, S = (4, 512)
        INV_SCALE = float(EMBED ** 0.5)
        q = jnp.einsum('bsd,ed->bse', query, Wq) + bq
        k = jnp.einsum('bsd,ed->bse', key, Wk) + bk
        v = jnp.einsum('bsd,ed->bse', value, Wv) + bv
        scores = jnp.einsum('bqe,bke->bqk', q, k) / INV_SCALE
        probs = jax.nn.softmax(scores, axis=-1)
        return jnp.einsum('bqk,bke->bqe', probs, v)

    def _L1_ffn_ref(x, Wr, br, W1, b1, W2, b2):
        import jax, jax.numpy as jnp
        import numpy as np
        HIDDEN = 128
        NUM_EXPERTS = 8
        TOP_K = 2
        B, S = (4, 128)
        B_, S_, H = x.shape
        xf = x.reshape(-1, H)
        logits = xf @ Wr + br
        topk_w, topk_idx = jax.lax.top_k(logits, TOP_K)
        topk_w = jax.nn.softmax(topk_w, axis=-1)
        gate = jnp.sum(jax.nn.one_hot(topk_idx, NUM_EXPERTS, dtype=xf.dtype) * topk_w[..., None], axis=1)
        h = jax.nn.relu(jnp.einsum('th,ehf->etf', xf, W1) + b1[:, None, :])
        y = jnp.einsum('etf,efh->eth', h, W2) + b2[:, None, :]
        out = jnp.einsum('te,eth->th', gate, y)
        return out.reshape(B_, S_, H)

    def _L2_xattn_ref(x, context, Wq, Wkv, Wout, bout):
        import jax, jax.numpy as jnp
        import numpy as np
        heads, dim_head = (16, 64)
        b, n_q, _ = x.shape
        n_kv = context.shape[1]
        scale = dim_head ** (-0.5)
        q = x @ Wq
        kv = context @ Wkv
        k, v = jnp.split(kv, 2, axis=-1)

        def split_heads(t):
            bb, n, _ = t.shape
            return t.reshape(bb, n, heads, dim_head).transpose(0, 2, 1, 3)
        q, k, v = map(split_heads, (q, k, v))
        i_idx = jnp.arange(n_q)[:, None]
        j_idx = jnp.arange(n_kv)[None, :]
        mask = j_idx % n_q == i_idx
        sim = jnp.einsum('bhid,bhjd->bhij', q, k) * scale
        max_neg = -jnp.finfo(sim.dtype).max
        sim = jnp.where(mask[None, None, :, :], sim, max_neg)
        attn = jax.nn.softmax(sim, axis=-1)
        out = jnp.einsum('bhij,bhjd->bhid', attn, v)
        out = out.transpose(0, 2, 1, 3).reshape(b, n_q, heads * dim_head)
        return out @ Wout + bout

    def _L2_ffn_ref(x, w1, conv_w, conv_b, w2):
        import jax, jax.numpy as jnp
        import numpy as np
        B, S, D_MODEL, D_HIDDEN = (4, 256, 128, 512)

        def act_quant(x):
            scale = 127.0 / jnp.clip(jnp.max(jnp.abs(x), axis=-1, keepdims=True), 1e-05)
            return jnp.clip(jnp.round(x * scale), -128, 127) / scale

        def weight_quant(w):
            scale = 1.0 / jnp.clip(jnp.mean(jnp.abs(w)), 1e-05)
            return jnp.clip(jnp.round(w * scale), -1, 1) / scale

        def bit_linear(x, w):
            xq = x + jax.lax.stop_gradient(act_quant(x) - x)
            wq = w + jax.lax.stop_gradient(weight_quant(w) - w)
            return jnp.einsum('bsd,hd->bsh', xq, wq)

        def depthwise_conv1d(x_bcl, w, b):
            y = jax.lax.conv_general_dilated(x_bcl, w, window_strides=(1,), padding=[(1, 1)], dimension_numbers=('NCH', 'OIH', 'NCH'), feature_group_count=x_bcl.shape[1])
            return y + b[None, :, None]
        h = bit_linear(x, w1)
        h = depthwise_conv1d(h.transpose(0, 2, 1), conv_w, conv_b)
        h = h.transpose(0, 2, 1)
        h = jax.nn.silu(h)
        return bit_linear(h, w2)

    def _L3_xattn_ref(q, k, v, mask, Wq, bq, Wk, bk, Wv, bv, Wo, bo):
        import jax, jax.numpy as jnp
        import numpy as np
        N_HEAD = 16
        N_EMBD = 128
        DIM_K = N_EMBD // N_HEAD

        def _split_heads(x):
            B, S, _ = x.shape
            return x.reshape(B, S, N_HEAD, DIM_K).transpose(0, 2, 1, 3)
        Q = _split_heads(q @ Wq + bq)
        K = _split_heads(k @ Wk + bk)
        V = _split_heads(v @ Wv + bv)
        scale = 1.0 / jnp.sqrt(jnp.asarray(DIM_K, Q.dtype))
        score = jnp.einsum('bhqd,bhkd->bhqk', Q, K) * scale
        score = jnp.where(mask[:, None, :, :] == 0, jnp.asarray(-1000000000.0, score.dtype), score)
        attn = jax.nn.softmax(score, axis=-1)
        out = jnp.einsum('bhqk,bhkd->bhqd', attn, V)
        B, _, S, _ = out.shape
        out = out.transpose(0, 2, 1, 3).reshape(B, S, N_EMBD)
        return out @ Wo + bo

    def _L3_ffn_ref(x, w_gate, w_gate_up, w_down):
        import jax, jax.numpy as jnp
        import numpy as np
        B, S, D = (2, 256, 128)
        F = 512
        E, K = (8, 2)
        EPS = 1e-09
        gate_logits = x @ w_gate
        gate_probs = jax.nn.softmax(gate_logits, axis=-1)
        topk_vals, topk_idx = jax.lax.top_k(gate_probs, K)
        masked = jnp.sum(jax.nn.one_hot(topk_idx, E, dtype=gate_probs.dtype) * topk_vals[..., None], axis=-2)
        denom = jnp.maximum(jnp.sum(masked, axis=-1, keepdims=True), EPS)
        gate_probs = masked / denom
        gu = jnp.einsum('bsd,edh->ebsh', x, w_gate_up)
        g, u = jnp.split(gu, 2, axis=-1)
        act = jax.nn.silu(g) * u
        expert_out = jnp.einsum('ebsf,efd->ebsd', act, w_down)
        return jnp.einsum('bse,ebsd->bsd', gate_probs, expert_out)
    x = x + _L0_xattn_ref(_layernorm(x, axis=-1), ctx_1024, ctx_1024, mask_Bx1xS2_if1, L0_xattn_Wq, L0_xattn_Wk, L0_xattn_Wv, L0_xattn_Wo)
    x = x + _L0_ffn_ref(_layernorm(x, axis=-1), L0_ffn_gate_w, L0_ffn_fc_w, L0_ffn_proj_w)
    x = x + _L1_xattn_ref(_layernorm(x, axis=-1), ctx_1024, ctx_1024, L1_xattn_Wq, L1_xattn_bq, L1_xattn_Wk, L1_xattn_bk, L1_xattn_Wv, L1_xattn_bv)
    x = x + _L1_ffn_ref(_layernorm(x, axis=-1), L1_ffn_Wr, L1_ffn_br, L1_ffn_W1, L1_ffn_b1, L1_ffn_W2, L1_ffn_b2)
    x = x + _L2_xattn_ref(_layernorm(x, axis=-1), ctx_1024, L2_xattn_Wq, L2_xattn_Wkv, L2_xattn_Wout, L2_xattn_bout)
    x = x + _L2_ffn_ref(_layernorm(x, axis=-1), L2_ffn_w1, L2_ffn_conv_w, L2_ffn_conv_b, L2_ffn_w2)
    x = x + _L3_xattn_ref(_layernorm(x, axis=-1), ctx_1024, ctx_1024, mask_BxSxS2_if1, L3_xattn_Wq, L3_xattn_bq, L3_xattn_Wk, L3_xattn_bk, L3_xattn_Wv, L3_xattn_bv, L3_xattn_Wo, L3_xattn_bo)
    x = x + _L3_ffn_ref(_layernorm(x, axis=-1), L3_ffn_w_gate, L3_ffn_w_gate_up, L3_ffn_w_down)
    return x

_drawn_inputs = setup_inputs


def setup_inputs(seed=0):
    import zlib

    import numpy as np

    out = dict(_drawn_inputs(seed))
    spreads = {'L1_xattn_bq': (0.0, 0.326),
     'L1_xattn_bk': (0.0, 0.8),
     'L1_xattn_bv': (0.0, 0.1),
     'L2_xattn_bout': (0.0, 0.1),
     'L3_xattn_bq': (0.0, 0.426),
     'L3_xattn_bk': (0.0, 0.8),
     'L3_xattn_bv': (0.0, 0.1),
     'L3_xattn_bo': (0.0, 0.1)}
    factors = {'L1_ffn_b1': 5.63,
     'L1_ffn_b2': 3.073,
     'L3_ffn_w_gate': 8.0,
     'L3_ffn_w_gate_up': 8.0,
     'L3_ffn_w_down': 8.0}
    for name, (base, spread) in spreads.items():
        noise = np.random.default_rng([zlib.crc32(name.encode()), seed]).standard_normal(out[name].shape)
        drawn = base * np.exp(spread * noise) if base else spread * noise
        out[name] = jnp.asarray(drawn.astype(out[name].dtype))
    for name, factor in factors.items():
        out[name] = (out[name] * factor).astype(out[name].dtype)
    return out
```

```python
from contextlib import ExitStack

import concourse.bass as bass
from concourse import mybir

F32 = mybir.dt.float32
F32R = mybir.dt.float32r
BF16 = mybir.dt.bfloat16
I32 = mybir.dt.int32
ACT = mybir.ActivationFunctionType
ALU = mybir.AluOpType
AX = mybir.AxisListType

P = 128
B, S, D = 4, 512, 128
K = 32
H = 16
DK = D // H
HK = H * K
TILES = B * S // P
BT = S // P
GROUPS = 2
GT = TILES // GROUPS
GB = B // GROUPS
E, TOPK = 8, 2
HPC = P // K
HC = H // HPC
VW = HPC * DK + HPC
NT = (GT * P * TOPK + E * (P - 1)) // P
RAW = 6
RING = 4
STEPS = NT - 3
EPS = 1e-5
FILL = -float(2 ** 100)
ROUND = 1.5 * 2.0 ** 23
NEG = -3.4028234663852886e38
HL, DL = 16, 64
INNER = HL * DL
IC = INNER // P
F2, F2C, TAPS = 512, 4, 3
RSQRT_SEED = float(0x5F3759DF)
assert STEPS % RING == 0

MOE = [
    dict(up=512, f=512, act=ACT.Gelu, bias=False),
    dict(up=256, f=256, act=ACT.Relu, bias=True),
    dict(up=1024, f=512, act=ACT.Silu, bias=False),
]


def build(nc, p0, p1, p3, cols, rows, bias, x, mask0, mask3, fc0, pj0, fc1, pj1, fc3, pj3, wkv, wq2, wout2, w1t, w2t, cw,
          out):
    ctx = ExitStack()
    with ctx:
        def sb(name, shape, dt):
            return ctx.enter_context(nc.sbuf_tensor(name, shape, dt))

        def sem(name):
            return ctx.enter_context(nc.semaphore(name))

        xs_dram = [nc.dram_tensor(f"xs{g}", (NT * P, D), F32, kind="Internal").ap() for g in range(GROUPS)]
        ys_dram = [nc.dram_tensor(f"ys{g}", (NT * P, D), F32, kind="Internal").ap() for g in range(GROUPS)]
        xs_tiles = [a.rearrange("(t p) d -> t p d", p=P) for a in xs_dram]
        ys_tiles = [a.rearrange("(t p) d -> t p d", p=P) for a in ys_dram]

        bank = [ctx.enter_context(nc.psum_tensor(f"bank{i}", [P, 512], F32)) for i in range(8)]

        ident = sb("ident", [P, P], F32)
        ones_row = sb("ones_row", [1, P], F32)
        ones_row_bf = sb("ones_row_bf", [1, P], BF16)
        ones_bf = sb("ones_bf", [P, P], BF16)
        before_bf = sb("before_bf", [P, P], BF16)
        head_mask = sb("head_mask", [P, H], F32)
        chunk_mask = sb("chunk_mask", [P, HPC], F32)
        expert_i = sb("expert_i", [P, E], I32)
        prefer = sb("prefer", [P, E], F32)
        tile_i = sb("tile_i", [1, NT, E], I32)
        tile_no = sb("tile_no", [1, NT, E], F32)
        zeros = sb("zeros", [P, P], F32)
        ones_f = sb("ones_f", [P, P], F32)
        ident_bf = sb("ident_bf", [P, P], BF16)

        X = sb("X", [P, TILES, D], F32)
        w0 = sb("w0", [P, 5 * P + E], F32)
        ctxT, wk0, wq0, wv0, wo0 = (w0[:, i * P:(i + 1) * P] for i in range(5))
        gate0 = w0[:, 5 * P:5 * P + E]
        mask0_i = sb("mask0_i", [1, B, K], I32)
        w1 = sb("w1", [P, 3 * P + E], F32)
        wk1, wq1, wv1 = (w1[:, i * P:(i + 1) * P] for i in range(3))
        gate1 = w1[:, 3 * P:3 * P + E]
        w3 = sb("w3", [P, 4 * P + E], F32)
        wk3, wq3, wv3, wo3 = (w3[:, i * P:(i + 1) * P] for i in range(4))
        gate3 = w3[:, 4 * P:4 * P + E]
        col = sb("col", [P, 4 + F2C], F32)
        bq1, bk1, bq3, bk3 = (col[:, i:i + 1] for i in range(4))
        row = sb("row", [1, 4 * P + E], F32)
        bv1, bv3, bo3, bout2 = (row[:, i * P:(i + 1) * P] for i in range(4))
        br1 = row[:, 4 * P:4 * P + E]
        part_no = sb("part_no", [3, 1], I32)
        part_f = sb("part_f", [3, 1], F32)
        minus_12 = sb("minus_12", [3, 1], F32)
        minus_2 = sb("minus_2", [3, 1], F32)
        brow = sb("brow", [3, B, HK], BF16)
        sel = sb("sel", [K, H, K], BF16)
        sel_f = sb("sel_f", [K, K], F32)
        vo = sb("vo", [P, D], F32)
        M1 = sb("M1", [P, B, K], F32)
        r1 = sb("r1", [1, B, K], F32)
        V1 = sb("V1", [K, B, D], F32)
        batch_mask = sb("batch_mask", [P, P], F32)
        late = sb("late", [P, 1], F32)

        ctx4 = sb("ctx4", [P, B, HPC, K], F32)
        kT = sb("kT", [P, B, K], F32)
        with nc.sbuf_tensor("bias1", [3, E, 256], BF16) as bias1, nc.sbuf_tensor("bias2", [3, E, D], BF16) as bias2:
            pass
        M = sb("M", [P, B, HK], F32)
        VB = sb("VB", [P, B, HC, VW], F32)
        mfill = sb("mfill", [K, B * S], BF16)
        mrow = mfill[0:1, :].rearrange("p (b h k) -> p b h k", b=B, h=H)
        stats = sb("stats", [P, GT, 6], F32)
        mv = sb("mv", [P, GT, 2], F32)
        ve = sb("ve", [P, GT], F32)
        ti = sb("ti", [P, GT], I32)
        yi = sb("yi", [P, GT], I32)
        ya = sb("ya", [P, GT], F32)
        yb = sb("yb", [P, GT], F32)
        rstd = sb("rstd", [P, GT], F32)
        XNR = sb("XNR", [P, GROUPS, GT, D], F32)
        smax = sb("smax", [P, 2, H], F32)
        rsum = sb("rsum", [P, 2, H], F32)
        ON = sb("ON", [P, 2, D], F32)
        OT = sb("OT", [P, 2, P], F32)

        lg = sb("lg", [P, GT, E], F32)
        l2 = sb("l2", [P, GT, E], F32)
        cand = sb("cand", [P, GT, E], F32)
        m1 = sb("m1", [P, GT], F32)
        m2 = sb("m2", [P, GT], F32)
        c1 = sb("c1", [P, GT], F32)
        oh1 = sb("oh1", [P, GT, E], F32)
        oh2 = sb("oh2", [P, GT, E], F32)
        both = sb("both", [P, GT, E], BF16)
        dl = sb("dl", [P, GT, E], F32)
        de = sb("de", [P, GT], F32)
        ex = sb("ex", [P, GT, E], F32)
        e2 = sb("e2", [P, GT], F32)
        es = sb("es", [P, GT], F32)
        pr1 = sb("pr1", [P, GT], F32)
        pr2 = sb("pr2", [P, GT], F32)
        den = sb("den", [P, GT], F32)
        gates = sb("gates", [P, GROUPS, TOPK, GT], F32)
        cnt = sb("cnt", [P, E], F32)
        inc_a = sb("inc_a", [P, 4 + E], F32)
        inc_b = sb("inc_b", [P, 4 + E], F32)
        start_f = sb("start_f", [P, E], F32)
        place = sb("place", [P, GT, E], F32)
        pick = sb("pick", [P, GT, E], F32)
        slot_f = sb("slot_f", [P, TOPK, GT], F32)
        slot_i = sb("slot_i", [P, GROUPS, TOPK, GT], I32)
        le = sb("le", [1, NT, E], F32)
        eid_f = sb("eid_f", [1, NT], F32)
        eid_c = sb("eid_c", [1, NT], F32)
        eid_i = sb("eid_i", [1, GROUPS, NT + 1], I32)

        with ExitStack() as l2f_tiles:
            def l2f(name, shape, dt=F32):
                return l2f_tiles.enter_context(nc.sbuf_tensor(name, shape, dt))

            w1c_h = l2f("w1c_h", [P, TAPS, F2], F32R)
            w1c_l = l2f("w1c_l", [P, TAPS, F2], F32R)
            w1_s = l2f("w1_s", [P, F2])
            w2_s = l2f("w2_s", [P, F2C, D])
            w2q = l2f("w2q", [P, F2C, D], BF16)
            cw_s = l2f("cw_s", [TAPS, F2])
            U = l2f("U", [P, B, D])
            Z = l2f("Z", [P, F2C, S])
            zq = l2f("zq", [P, 2, F2], BF16)
        WA = sb("WA", [P, E, 2, 512], F32R)
        with ExitStack() as l2_tiles:
            def l2x(name, shape, dt=F32):
                return l2_tiles.enter_context(nc.sbuf_tensor(name, shape, dt))

            wkv_s = l2x("wkv_s", [P, 2 * INNER])
            wq_s = l2x("wq_s", [P, INNER])
            wout_s = l2x("wout_s", [P, IC, D])
            kall = l2x("kall", [P, INNER])
            vall = l2x("vall", [P, INNER])
            vsum = l2x("vsum", [P, INNER])
            attn2 = l2x("attn2", [P, INNER])
        WB = sb("WB", [P, E, 2, 512], F32R)
        WC = sb("WC", [P, E, 2, 512], F32R)
        wmean = sb("wmean", [P, 2, 4], F32)
        raw = sb("raw", [P, RAW, 512], F32)
        xrow = [sb(f"xrow{i}", [P, D], F32) for i in range(RING)]
        with ExitStack() as attention_tiles:
            def at(name, shape, dt):
                return attention_tiles.enter_context(nc.sbuf_tensor(name, shape, dt))

            XN = at("XN", [P, GT, D], F32)
            XT = at("XT", [P, GT, P], F32)
            PR = at("PR", [P, 2, HK], F32)
            PT = at("PT", [P, 2, HC, P], F32)
            rrow = at("rrow", [3, HK], F32)
        with ExitStack() as ffn_tiles:
            def ff(name, shape, dt):
                return ffn_tiles.enter_context(nc.sbuf_tensor(name, shape, dt))

            XQ = ff("XQ", [P, GT, D], F32)
            xqh = ff("xqh", [P, S + 2], F32R)
            xql = ff("xql", [P, S + 2], F32R)
            zt = ff("zt", [P, 2, F2], F32)
            zqT = ff("zqT", [P, 2, F2C, P], BF16)
        xh = [sb(f"xh{i}", [P, P], F32R) for i in range(2)]
        xl = [sb(f"xl{i}", [P, P], F32R) for i in range(2)]
        hb = [sb(f"hb{i}", [P, 512], F32) for i in range(2)]
        hh = [sb(f"hh{i}", [P, 4, P], F32R) for i in range(2)]
        gb = [sb(f"gb{i}", [P, 512], F32) for i in range(2)]
        hl = [sb(f"hl{i}", [P, 4, P], F32R) for i in range(2)]
        with nc.sbuf_tensor("kbd", [P, B, H, K], F32) as kbd:
            pass
        with nc.sbuf_tensor("bias1_raw", [3, E, 256], F32) as bias1_raw:
            pass
        Y = sb("Y", [P, NT, D], F32)
        YG = sb("YG", [P, GT, D], F32)
        XL = sb("XL", [P, P], F32)
        s16 = sb("s16", [P, HL], F32)
        m16 = sb("m16", [P, HL], F32)
        e16 = sb("e16", [P, 2, HL], F32)
        sum16 = sb("sum16", [P, HL], F32)
        amax = sb("amax", [P, GT], F32)
        qscale = sb("qscale", [P, GT], F32)
        qinv = sb("qinv", [P, GT], F32)
        zmax = sb("zmax", [P, GT], F32)
        zscale = sb("zscale", [P, GT], F32)
        zinv = sb("zinv", [P, GT], F32)

        in_w0, in_mask0 = sem("in_w0"), sem("in_mask0")
        in_x = [sem(f"in_x{g}") for g in range(GROUPS)]
        in_raw = [sem(f"in_raw{i}") for i in range(RAW)]
        zeroed, const_ready, pool_chain, dve_chain = sem("zeroed"), sem("const_ready"), sem("pool_chain"), sem("dve_chain")
        zeros_ready, xn_ready, xnr_ready = sem("zeros_ready"), sem("xn_ready"), sem("xnr_ready")
        setup_mm, setup_evac, m_evac, ctx4_ready, mrow_ready = sem("setup_mm"), sem("setup_evac"), sem("m_evac"), sem("ctx4_ready"), sem("mrow_ready")
        xt_mm, xt_ready = sem("xt_mm"), sem("xt_ready")
        s_mm, s_sub, s_exp, pt_mm, pt_ready = sem("s_mm"), sem("s_sub"), sem("s_exp"), sem("pt_mm"), sem("pt_ready")
        o_mm, o_norm, ot_mm, ot_ready, wo_mm, x_added = sem("o_mm"), sem("o_norm"), sem("ot_mm"), sem("ot_ready"), sem("wo_mm"), sem("x_added")
        lg_mm, both_ready, rank_mm, routed, dl_ready, ex_ready = sem("lg_mm"), sem("both_ready"), sem("rank_mm"), sem("routed"), sem("dl_ready"), sem("ex_ready")
        scattered, gathered, y_stored = ([sem(f"{n}{g}") for g in range(GROUPS)] for n in ("scattered", "gathered", "y_stored"))
        x_loaded = [sem(f"x_loaded{i}") for i in range(RING)]
        w_split = sem("w_split")
        ex_t, ex_xh, ex_xl, ex_up, ex_act = sem("ex_t"), sem("ex_xh"), sem("ex_xl"), sem("ex_up"), sem("ex_act")
        ex_ht, ex_hh, ex_hl, ex_dn, ex_y = sem("ex_ht"), sem("ex_hh"), sem("ex_hl"), sem("ex_dn"), sem("ex_y")
        stored = sem("stored")
        in_w1, in_w3, in_col, in_row, in_b1, in_b2, in_mask3, in_l2, in_ff2 = (
            sem(n) for n in ("in_w1", "in_w3", "in_col", "in_row", "in_b1", "in_b2", "in_mask3", "in_l2", "in_ff2"))
        s1_mm, s1_evac, s2_mm, s2_evac, s2_act, r_mm, r_evac = (
            sem(n) for n in ("s1_mm", "s1_evac", "s2_mm", "s2_evac", "s2_act", "r_mm", "r_evac"))
        a1_s, a1_sub, a1_exp, a1_p, a1_pt, a1_ptc, a1_o, a1_added = (
            sem(n) for n in ("a1_s", "a1_sub", "a1_exp", "a1_p", "a1_pt", "a1_ptc", "a1_o", "a1_added"))
        x2_n, x2_t, x2_xl, x2_q, x2_m, x2_e, x2_o, x2_ot, x2_otc, x2_mm = (
            sem(n) for n in ("x2_n", "x2_t", "x2_xl", "x2_q", "x2_m", "x2_e", "x2_o", "x2_ot", "x2_otc", "x2_mm"))
        fs_sum, fs_mm, fs_ready = (sem(n) for n in ("fs_sum", "fs_mm", "fs_ready"))
        f2_xq, f2_xt, f2_xh, f2_xl, f2_h, f2_z, f2_tt, f2_zr, f2_zq, f2_qt, f2_qtc, f2_dn, f2_added = (
            sem(n) for n in ("f2_xq", "f2_xt", "f2_xh", "f2_xl", "f2_h", "f2_z", "f2_tt", "f2_zr", "f2_zq", "f2_qt", "f2_qtc",
                             "f2_dn", "f2_added"))
        ex_mul = sem("ex_mul")
        combined = sem("combined")

        N_W1, N_W3 = 2 * E, 4 * E
        N_D3 = N_W3 + 2 * E
        mask3_i = XNR[0:K, :, :, :].rearrange("p g t d -> p (g t d)").bitcast(I32)
        oT = wkv_s[:, INNER:2 * INNER].rearrange("p (c r) -> p c r", c=IC)
        kq = wkv_s[:, 0:INNER]

        LN_ORDER = {k: i for i, k in enumerate(
            [(f"{kind}{layer}", g) for layer in (0, 1, 3) for g in range(GROUPS) for kind in "ar"])}

        block = ctx.enter_context(nc.Block())

        @block.sync
        def _(sp):
            sp.dma_start(w0[:, :], p0).then_inc(in_w0, 16)
            sp.dma_start(mask0_i[:, :, :], mask0).then_inc(in_mask0, 16)
            x_v = x.rearrange("(g t p) d -> g p t d", g=GROUPS, p=P)
            for g in range(GROUPS):
                sp.dma_start(X[:, g * GT:(g + 1) * GT, :], x_v[g]).then_inc(in_x[g], 16)
            sp.dma_start(col[:, :], cols).then_inc(in_col, 16)
            sp.dma_start(row[:, :], rows).then_inc(in_row, 16)
            sp.dma_start(w1[:, :], p1).then_inc(in_w1, 16)
            sp.dma_start(w3[:, :], p3).then_inc(in_w3, 16)
            def load_weights(n0, matrices):
                for i, (src, width) in enumerate(matrices):
                    n = n0 + i
                    if n >= RAW:
                        sp.wait_ge(w_split, n - RAW + 1)
                    dst = raw[:, n % RAW, 0:width]
                    if src.shape[0] != P:
                        src = src.rearrange("(c p) d -> p c d", p=P)
                        dst = dst.rearrange("p (c d) -> p c d", d=D)
                    sp.dma_start(dst, src).then_inc(in_raw[n % RAW], 16)

            sp.wait_ge(zeros_ready, 1)
            for g in range(GROUPS):
                sp.dma_start(xs_tiles[g].rearrange("t p d -> p t d"),
                             zeros[:, :].unsqueeze(1).broadcast_to([P, NT, D])).then_inc(zeroed, 16)
            load_weights(0, [(w[e], 512) for e in range(E) for w in (fc0, pj0)])

            def experts(m):
                g = m % GROUPS
                xs_t, ys_t = xs_tiles[g], ys_tiles[g]
                base = m * NT

                def load(t, s):
                    sp.dma_start(xrow[s][:, :], xs_t[bass.ds(t, 1)].rearrange("a p d -> p (a d)")).then_inc(x_loaded[s], 16)

                def store(t):
                    sp.wait_ge(ex_y, t + base + 1)
                    sp.dma_start(ys_t[bass.ds(t, 1)].rearrange("a p d -> p (a d)"),
                                 Y[:, bass.ds(t, 1), :].rearrange("p a d -> p (a d)")).then_inc(y_stored[g], 16)

                sp.wait_ge(scattered[g], 16 * TOPK * GT * (m // GROUPS + 1))
                if m:
                    sp.wait_ge(ex_t, base)
                for s in range(RING):
                    load(s, s)
                for s in range(RING):
                    sp.wait_ge(ex_t, base + s + 1)
                    load(RING + s, s)
                with sp.Fori(2, NT // RING) as i:
                    for s in range(RING):
                        sp.wait_ge(ex_t, i * RING + (base - RING + s + 1))
                        load(i * RING + s, s)
                        store((i - 2) * RING + s)
                for t in range(NT // RING * RING, NT):
                    sp.wait_ge(ex_t, base + t - RING + 1)
                    load(t, t % RING)
                    store(t - 2 * RING)
                for t in range(NT - 2 * RING, NT):
                    store(t)

            sp.wait_ge(m_evac, B)
            for i in range(3):
                sp.dma_start(bias1_raw[i:i + 1, :, :].rearrange("p e f -> p (e f)"), bias[:, 0:E * 256]).then_inc(in_b1, 16)
                sp.dma_start(YG[i:i + 1, :, :].rearrange("p e f -> p (e f)"), bias[:, E * 256:]).then_inc(in_b2, 16)
            sp.wait_ge(w_split, N_W1 - RAW + 2)
            load_weights(N_W1, [(w[e], 256) for e in range(E) for w in (fc1, pj1)])
            for g in range(GROUPS):
                experts(g)
            sp.wait_ge(ex_dn, 2 * NT)
            sp.dma_start(wkv_s[:, :], wkv).then_inc(in_l2, 16)
            sp.dma_start(wq_s[:, :], wq2).then_inc(in_l2, 16)
            sp.dma_start(wout_s[:, :, :], wout2.rearrange("(c p) d -> p c d", p=P)).then_inc(in_l2, 16)
            sp.dma_start(w1_s[:, :], w1t).then_inc(in_ff2, 16)
            sp.dma_start(w2_s[:, :, :], w2t.rearrange("(c p) d -> p c d", p=P)).then_inc(in_ff2, 16)
            sp.dma_start(cw_s[:, :], cw).then_inc(in_ff2, 16)
            for g in range(GROUPS):
                experts(GROUPS + g)
            load_weights(N_W3, [(fc3[e, :, 0:512], 512) for e in range(E)])
            sp.wait_ge(combined, 2 * GROUPS)
            sp.dma_start(mask3_i, mask3).then_inc(in_mask3, 16)
            load_weights(N_W3 + E, [(fc3[e, :, 512:1024], 512) for e in range(E)])
            load_weights(N_D3, [(pj3[e], 512) for e in range(E)])
            for g in range(GROUPS):
                experts(2 * GROUPS + g)
            out_v = out.rearrange("(g t p) d -> g p t d", g=GROUPS, p=P)
            for g in range(GROUPS):
                sp.wait_ge(combined, 2 * GROUPS + g + 1)
                sp.dma_start(out_v[g], X[:, g * GT:(g + 1) * GT, :]).then_inc(stored, 16)
            sp.wait_ge(stored, 16 * GROUPS)

        @block.gpsimd
        def _(pool):
            n = [0]

            def link(ins):
                n[0] += 1
                ins.then_inc(pool_chain, 1)
                pool.wait_ge(pool_chain, n[0])

            link(pool.memset(zeros[:, :], 0.0))
            pool.sem_inc(zeros_ready, 1)
            link(pool.affine_select(out=ident[:, :], in_=zeros[:, :], compare_op=ALU.not_equal, fill=1.0,
                                    base=0, pattern=[[-1, P]], channel_multiplier=1))
            pool.memset(ones_row[:, :], 1.0)
            pool.memset(ones_row_bf[:, :], 1.0)
            pool.memset(ones_bf[:, :], 1.0)
            pool.memset(ones_f[:, :], 1.0)
            pool.memset(batch_mask[:, :], 1.0)
            pool.memset(late[:, :], 1.0)
            pool.memset(head_mask[:, :], 1.0)
            link(pool.memset(chunk_mask[:, :], 1.0))
            link(pool.affine_select(out=head_mask[:, :], in_=head_mask[:, :], compare_op=ALU.is_ge, fill=0.0,
                                    base=0, pattern=[[-DK, H]], channel_multiplier=1))
            link(pool.affine_select(out=head_mask[:, :], in_=head_mask[:, :], compare_op=ALU.is_ge, fill=0.0,
                                    base=DK - 1, pattern=[[DK, H]], channel_multiplier=-1))
            link(pool.affine_select(out=chunk_mask[:, :], in_=chunk_mask[:, :], compare_op=ALU.is_ge, fill=0.0,
                                    base=0, pattern=[[-K, HPC]], channel_multiplier=1))
            link(pool.affine_select(out=chunk_mask[:, :], in_=chunk_mask[:, :], compare_op=ALU.is_ge, fill=0.0,
                                    base=K - 1, pattern=[[K, HPC]], channel_multiplier=-1))
            link(pool.affine_select(out=before_bf[:, :], in_=ones_bf[:, :], compare_op=ALU.is_ge, fill=0.0,
                                    base=-1, pattern=[[1, P]], channel_multiplier=-1))
            bm = batch_mask[:, :].rearrange("p (b k) -> p b k", b=B)
            link(pool.affine_select(out=bm, in_=bm, compare_op=ALU.is_ge, fill=0.0,
                                    base=0, pattern=[[-K, B], [0, K]], channel_multiplier=1))
            link(pool.affine_select(out=bm, in_=bm, compare_op=ALU.is_ge, fill=0.0,
                                    base=K - 1, pattern=[[K, B], [0, K]], channel_multiplier=-1))
            link(pool.affine_select(out=late[:, :], in_=late[:, :], compare_op=ALU.is_ge, fill=0.0,
                                    base=-K, pattern=[[0, 1]], channel_multiplier=1))
            pool.iota(part_no[:, :], [[0, 1]], base=0, channel_multiplier=1)
            pool.iota(expert_i[:, :], [[-1, E]], base=E, channel_multiplier=0)
            pool.iota(tile_i[:, :, :], [[1, NT], [0, E]], base=0, channel_multiplier=0).then_inc(const_ready, 1)

            def split(n0, matrices):
                for i, dst in enumerate(matrices):
                    n = n0 + i
                    src = raw[:, n % RAW, 0:dst.shape[2]]
                    pool.wait_ge(in_raw[n % RAW], 16 * (n // RAW + 1))
                    link(pool.tensor_copy(dst[:, 0, :], src))
                    pool.tensor_tensor(dst[:, 1, :], src, dst[:, 0, :].bitcast(F32),
                                       ALU.subtract).then_inc(w_split, 1)

            def scatter(r):
                g = r % GROUPS
                if r == 0:
                    pool.wait_ge(zeroed, 16 * GROUPS)
                pool.wait_ge(routed, r + 1)
                for k in range(TOPK):
                    for j in range(GT):
                        pool.indirect_dma_start(
                            out=xs_dram[g], out_offset=bass.IndirectOffsetOnAxis(ap=slot_i[:, g, k, j:j + 1], axis=0),
                            in_=XNR[:, g, j, :], in_offset=None).then_inc(scattered[g], 16)

            def gather(m):
                g = m % GROUPS
                pool.wait_ge(y_stored[g], 16 * NT * (m // GROUPS + 1))
                if m:
                    pool.wait_ge(combined, m)
                for j in range(GT):
                    for k, dst in enumerate((XNR[:, g, j, :], YG[:, j, :])):
                        pool.indirect_dma_start(
                            out=dst, out_offset=None, in_=ys_dram[g],
                            in_offset=bass.IndirectOffsetOnAxis(ap=slot_i[:, g, k, j:j + 1], axis=0)).then_inc(gathered[g], 16)

            split(0, [w[:, e, :, :] for e in range(E) for w in (WA, WB)])
            scatter(0)
            split(N_W1, [WC[:, e, :, c:c + 256] for e in range(E) for c in (0, 256)])
            scatter(1)
            gather(0)
            gather(1)
            scatter(2)
            scatter(3)
            gather(2)
            gather(3)
            pool.wait_ge(ex_dn, 4 * NT)
            split(N_W3, [WC[:, e, :, :] for e in range(E)])
            pool.wait_ge(f2_added, TILES)
            split(N_W3 + E, [WA[:, e, :, :] for e in range(E)])
            split(N_D3, [WB[:, e, :, :] for e in range(E)])
            scatter(4)
            scatter(5)
            gather(4)
            gather(5)

        @block.scalar
        def _(act):
            def evac_xt(n):
                for q in range(GB):
                    act.wait_ge(xt_mm, GB * n + q + 1)
                    act.activation(XT[:, q * BT:(q + 1) * BT, :], bank[6 + q][:, :].rearrange("p (t c) -> p t c", c=P),
                                   ACT.Copy).then_inc(xt_ready, 1)

            def setup(i):
                for b in range(B):
                    act.wait_ge(setup_mm, i * (B + 2) + 2 + b)
                    act.activation(M[:, b, :], bank[1 + b % 2][:, :], ACT.Copy).then_inc(m_evac, 1)

            def attention(a):
                for s in range(GT + 4):
                    if s < GT:
                        act.wait_ge(s_sub, a * GT + s + 1)
                        act.activation(PR[:, s % 2, :], PR[:, s % 2, :], ACT.Exp, scale=float(DK) ** -0.5).then_inc(s_exp, 1)
                    j = s - 1
                    if 0 <= j < GT:
                        act.wait_ge(pt_mm, a * GT + j + 1)
                        act.activation(PT[:, j % 2, :, :], bank[2 + j % 2][:, :].rearrange("p (c t) -> p c t", c=HC),
                                       ACT.Copy).then_inc(pt_ready, 1)
                    j = s - 3
                    if 0 <= j < GT:
                        act.wait_ge(ot_mm, a * GT + j + 1)
                        act.activation(OT[:, j % 2, :], bank[6][:, 0:P], ACT.Copy).then_inc(ot_ready, 1)

            def router(r):
                act.wait_ge(dl_ready, r + 1)
                act.activation(ex[:, :, :], dl[:, :, :], ACT.Exp)
                act.activation(e2[:, :], de[:, :], ACT.Exp).then_inc(ex_ready, 1)

            def experts(m):
                L = MOE[m // GROUPS]
                f = L["f"]
                nc_f = f // P
                base = m * NT

                def x_high(t, s):
                    act.wait_ge(ex_t, t + base + 1)
                    act.activation(xh[s][:, :], bank[6][:, 0:P], ACT.Copy).then_inc(ex_xh, 1)

                def activate(t, s):
                    act.wait_ge(ex_up, t + base + 1)
                    dst = gb if L["up"] > L["f"] else hb
                    act.activation(dst[s][:, 0:f], bank[s][:, 0:f], L["act"]).then_inc(ex_act, 1)

                def h_high(t, s):
                    act.wait_ge(ex_ht, t + base + 1)
                    act.activation(hh[s][:, 0:nc_f, :], bank[4 + s][:, 0:f].rearrange("p (c t) -> p c t", c=nc_f),
                                   ACT.Copy).then_inc(ex_hh, 1)

                x_high(0, 0)
                x_high(1, 1)
                activate(0, 0)
                x_high(2, 0)
                activate(1, 1)
                h_high(0, 0)
                with act.Fori(0, STEPS // 2) as i:
                    for u in range(2):
                        x_high(2 * i + (u + 3), (u + 1) % 2)
                        activate(2 * i + (u + 2), u % 2)
                        h_high(2 * i + (u + 1), (u + 1) % 2)
                activate(NT - 1, (NT - 1) % 2)
                h_high(NT - 2, (NT - 2) % 2)
                h_high(NT - 1, (NT - 1) % 2)

            def attention1(g):
                act.wait_ge(a1_sub, g + 1)
                act.activation(PR[:, 0, 0:GT * K], PR[:, 0, 0:GT * K], ACT.Exp, scale=float(D) ** -0.5).then_inc(a1_exp, 1)
                for q in range(GB):
                    act.wait_ge(a1_pt, GB * g + q + 1)
                    act.activation(PT[0:K, q, :, :], bank[2 + q][0:K, :].rearrange("p (t c) -> p t c", t=BT),
                                   ACT.Copy).then_inc(a1_ptc, 1)

            def setup2():
                for i, dst in enumerate((kall, vall)):
                    act.wait_ge(s2_mm, i + 1)
                    for c in range(2):
                        act.activation(dst[:, c * 512:(c + 1) * 512], bank[2 + 2 * i + c][:, :], ACT.Copy).then_inc(s2_act, 1)
                act.wait_ge(s2_mm, 3)
                for c in range(2):
                    act.activation(vsum[:, c * 512:(c + 1) * 512], bank[2 + c][:, :], ACT.Copy).then_inc(s2_act, 1)
                act.wait_ge(s2_mm, 4)
                for c in range(2):
                    act.activation(attn2[:, c * 512:(c + 1) * 512], bank[4 + c][:, :], ACT.Copy, scale=1.0 / K).then_inc(s2_act, 1)

            def xattn2(g):
                R = GB * K
                act.wait_ge(x2_t, g + 1)
                act.activation(XL[:, g * R:(g + 1) * R].rearrange("p (q k) -> p q k", q=GB),
                               bank[6][:, 0:GB * P].rearrange("p (q t) -> p q t", q=GB)[:, :, 0:K], ACT.Copy).then_inc(x2_xl, 1)
                act.wait_ge(x2_m, g + 1)
                act.activation(e16[g * R:(g + 1) * R, :, :], e16[g * R:(g + 1) * R, :, :], ACT.Exp).then_inc(x2_e, 1)
                for c in range(2):
                    act.wait_ge(x2_ot, 2 * g + c + 1)
                    n = (g + 1) * R
                    act.activation(oT[:, c * 4:(c + 1) * 4, 0:n],
                                   bank[2 + c][:, 0:4 * n].rearrange("p (c r) -> p c r", c=4), ACT.Copy).then_inc(x2_otc, 1)

            def ffn2(g):
                for q in range(GB):
                    n = GB * g + q
                    act.wait_ge(f2_xt, n + 1)
                    act.activation(xqh[:, 1:S + 1], bank[6][:, :], ACT.Copy).then_inc(f2_xh, 1)
                    for c in range(F2C):
                        act.wait_ge(f2_h, n * F2C + c + 1)
                        act.activation(Z[:, c, :], bank[c][:, :], ACT.Silu, bias=col[:, 4 + c:5 + c]).then_inc(f2_z, 1)
                    for j in range(BT):
                        act.wait_ge(f2_qt, n * BT + j + 1)
                        act.activation(zqT[:, j % 2, :, :], bank[7][:, 0:F2 // 2].bitcast(BF16)
                                       .rearrange("p (c t) -> p c t", c=F2C), ACT.Copy).then_inc(f2_qtc, 1)

            setup(0)
            for g in range(GROUPS):
                evac_xt(LN_ORDER["a0", g])
                attention(g)
                evac_xt(LN_ORDER["r0", g])
                router(g)
            for g in range(GROUPS):
                experts(g)
            for g in range(GROUPS):
                evac_xt(LN_ORDER["a1", g])
                attention1(g)
                evac_xt(LN_ORDER["r1", g])
                router(GROUPS + g)
            setup2()
            for g in range(GROUPS):
                experts(GROUPS + g)
            setup(1)
            act.wait_ge(in_col, 16)
            for g in range(GROUPS):
                xattn2(g)
                ffn2(g)
            for g in range(GROUPS):
                evac_xt(LN_ORDER["a3", g])
                attention(GROUPS + g)
                evac_xt(LN_ORDER["r3", g])
                router(2 * GROUPS + g)
            for g in range(GROUPS):
                experts(2 * GROUPS + g)

        @block.vector
        def _(dve):
            n = [0]

            def link(ins):
                n[0] += 1
                ins.then_inc(dve_chain, 1)
                dve.wait_ge(dve_chain, n[0])

            def layer_norm(tiles, dst, done=None):
                nt = len(tiles)
                for j, t in enumerate(tiles):
                    ins = dve.bn_stats(stats[:, j, :], X[:, t, :])
                link(ins)
                for j in range(nt):
                    ins = dve.bn_aggr(mv[:, j, :], stats[:, j, :])
                link(ins)
                link(dve.tensor_scalar(ve[:, :], mv[:, :, 1], EPS, None, ALU.add))
                link(dve.tensor_scalar(ti[:, :], ve[:, :].bitcast(I32), 1, None, ALU.logical_shift_right))
                link(dve.tensor_scalar(yi[:, :], ti[:, :], -1.0, RSQRT_SEED, ALU.mult, ALU.add))
                y = yi[:, :].bitcast(F32)
                for k in range(3):
                    link(dve.tensor_tensor(ya[:, :], y, y, ALU.mult))
                    link(dve.scalar_tensor_tensor(out=yb[:, :], in0=ve[:, :], scalar=-0.5, in1=ya[:, :],
                                                  op0=ALU.mult, op1=ALU.mult))
                    link(dve.scalar_tensor_tensor(out=rstd[:, :], in0=yb[:, :], scalar=1.5, in1=y,
                                                  op0=ALU.add, op1=ALU.mult))
                    y = rstd[:, :]
                for j, t in enumerate(tiles):
                    ins = dve.tensor_scalar(dst[:, j, :], X[:, t, :], mv[:, j, 0:1], rstd[:, j:j + 1],
                                            ALU.subtract, ALU.mult)
                    if done is not None:
                        ins.then_inc(done, 1)
                if done is None:
                    link(ins)

            def half(g):
                return [g * GT + j for j in range(GT)]

            def constants():
                dve.wait_ge(const_ready, 1)
                dve.tensor_copy(prefer[:, :], expert_i[:, :])
                dve.tensor_copy(ident_bf[:, :], ident[:, :])
                link(dve.tensor_copy(tile_no[:, :, :], tile_i[:, :, :]))
                link(dve.memset(inc_a[:, :], 0.0))
                link(dve.memset(inc_b[:, :], 0.0))
                link(dve.memset(eid_i[:, :, :], 0))
                dve.wait_ge(in_w0, 16)
                dve.tensor_copy(ctx4[:, :, :, :], ctxT.rearrange("p (b k) -> p b k", b=B).unsqueeze(2)
                                .broadcast_to([P, B, HPC, K])).then_inc(ctx4_ready, 1)
                dve.wait_ge(in_mask0, 16)
                dve.tensor_scalar(mrow, mask0_i[:, :, :].unsqueeze(2).broadcast_to([1, B, H, K]),
                                  0, FILL, ALU.is_equal, ALU.mult).then_inc(mrow_ready, 1)
                dve.tensor_scalar(part_f[:, :], part_no[:, :], 0.0, None, ALU.is_equal)
                link(dve.tensor_copy(sel_f[:, :], ident[0:K, 0:K]))
                link(dve.tensor_scalar(minus_12[:, :], part_f[:, :], 1.0, None, ALU.subtract))
                dve.tensor_scalar(minus_2[:, :], part_no[:, :], 2.0, -1.0, ALU.is_equal, ALU.mult)
                link(dve.tensor_copy(sel[:, :, :], sel_f[:, :].unsqueeze(1).broadcast_to([K, H, K])))

            def split3(dst, src):
                link(dve.tensor_copy(dst, src))
                link(dve.scalar_tensor_tensor(out=src, in0=dst, scalar=minus_12[:, :], in1=src, op0=ALU.mult, op1=ALU.add))
                link(dve.tensor_copy(dst, src))
                link(dve.scalar_tensor_tensor(out=src, in0=dst, scalar=minus_2[:, :], in1=src, op0=ALU.mult, op1=ALU.add))
                return dve.tensor_copy(dst, src)

            def setup(i):
                dve.wait_ge(setup_mm, i * (B + 2) + 1)
                kps = bank[0][:, 0:P].rearrange("p (b k) -> p b k", b=B)
                if i == 0:
                    link(dve.tensor_copy(kT[:, :, :], kps))
                else:
                    dve.wait_ge(y_stored[1], 16 * NT * 2)
                    link(dve.tensor_scalar(kT[:, :, :], kps, bk3, None, ALU.add))
                for b in range(B):
                    dve.tensor_tensor(kbd[:, b, :, :], kT[:, b, :].unsqueeze(1).broadcast_to([P, H, K]),
                                      head_mask[:, :].unsqueeze(2).broadcast_to([P, H, K]), ALU.mult).then_inc(setup_evac, 1)
                if i == 1:
                    for b in range(B):
                        dve.wait_ge(r_mm, b + 1)
                        if b:
                            dve.wait_ge(r_evac, b)
                        link(dve.tensor_copy(rrow[:, :], bank[4 + b % 2][0:3, :]))
                        split3(brow[:, b, :], rrow[:, :]).then_inc(r_evac, 1)
                dve.wait_ge(setup_mm, (i + 1) * (B + 2))
                for b in range(B):
                    v = bank[3][:, b * P:(b + 1) * P].rearrange("p (c h d) -> p c h d", c=HC, h=HPC)
                    dve.tensor_tensor(VB[:, b, :, 0:HPC * DK].rearrange("p c (h d) -> p c h d", h=HPC), v,
                                      chunk_mask[:, :].unsqueeze(1).unsqueeze(3).broadcast_to([P, HC, HPC, DK]), ALU.mult)
                    ins = dve.tensor_copy(VB[:, b, :, HPC * DK:VW], chunk_mask[:, :].unsqueeze(1).broadcast_to([P, HC, HPC]))
                ins.then_inc(setup_evac, 1)

            def attention(a, g):
                for s in range(GT + 4):
                    if s < GT:
                        dve.wait_ge(s_mm, a * GT + s + 1)
                        sc = bank[s % 2][:, :].rearrange("p (h k) -> p h k", h=H)
                        link(dve.tensor_reduce(smax[:, s % 2, :], sc, AX.X, ALU.max))
                        dve.tensor_tensor(PR[:, s % 2, :].rearrange("p (h k) -> p h k", h=H), sc,
                                          smax[:, s % 2, :].unsqueeze(2).broadcast_to([P, H, K]),
                                          ALU.subtract).then_inc(s_sub, 1)
                    j = s - 2
                    if 0 <= j < GT:
                        dve.wait_ge(o_mm, a * GT + j + 1)
                        o = bank[4 + j % 2][:, 0:HC * VW].rearrange("p (c w) -> p c w", c=HC)
                        link(dve.reciprocal(rsum[:, j % 2, :].rearrange("p (c h) -> p c h", c=HC), o[:, :, HPC * DK:VW]))
                        dve.tensor_tensor(ON[:, j % 2, :].rearrange("p (c h d) -> p c h d", c=HC, h=HPC),
                                          o[:, :, 0:HPC * DK].rearrange("p c (h d) -> p c h d", h=HPC),
                                          rsum[:, j % 2, :].rearrange("p (c h) -> p c h", c=HC).unsqueeze(3)
                                          .broadcast_to([P, HC, HPC, DK]), ALU.mult).then_inc(o_norm, 1)
                    j = s - 4
                    if 0 <= j < GT:
                        dve.wait_ge(wo_mm, a * GT + j + 1)
                        t = g * GT + j
                        dve.tensor_tensor(X[:, t, :], X[:, t, :], bank[7][:, 0:D], ALU.add).then_inc(x_added, 1)
                dve.wait_ge(x_added, (a + 1) * GT)

            def router(r):
                g = r % GROUPS
                flat = [P, GT, E]
                dve.wait_ge(lg_mm, r + 1)
                link(dve.tensor_copy(lg[:, :, :], bank[0][:, 0:GT * E].rearrange("p (t e) -> p t e", e=E)))
                pref = prefer[:, :].unsqueeze(1).broadcast_to(flat)

                def first_of_max(src, mx, onehot):
                    link(dve.tensor_reduce(mx[:, :], src, AX.X, ALU.max))
                    link(dve.tensor_tensor(cand[:, :, :], src, mx[:, :].unsqueeze(2).broadcast_to(flat), ALU.is_equal))
                    link(dve.tensor_tensor(cand[:, :, :], cand[:, :, :], pref, ALU.mult))
                    link(dve.tensor_reduce(c1[:, :], cand[:, :, :], AX.X, ALU.max))
                    link(dve.tensor_tensor(onehot[:, :, :], cand[:, :, :], c1[:, :].unsqueeze(2).broadcast_to(flat),
                                           ALU.is_equal))

                first_of_max(lg[:, :, :], m1, oh1)
                link(dve.scalar_tensor_tensor(out=l2[:, :, :], in0=oh1[:, :, :], scalar=-3.0e38, in1=lg[:, :, :],
                                              op0=ALU.mult, op1=ALU.add))
                first_of_max(l2[:, :, :], m2, oh2)
                dve.tensor_tensor(both[:, :, :], oh1[:, :, :], oh2[:, :, :], ALU.add).then_inc(both_ready, 1)
                link(dve.tensor_tensor(dl[:, :, :], lg[:, :, :], m1[:, :].unsqueeze(2).broadcast_to(flat), ALU.subtract))
                dve.tensor_tensor(de[:, :], m2[:, :], m1[:, :], ALU.subtract).then_inc(dl_ready, 1)
                dve.wait_ge(rank_mm, r + 1)
                link(dve.tensor_scalar(cnt[:, :], bank[1][:, GT * E:GT * E + E], 1.0 / P, (P - 1) / P - 0.5 + 0.5 / P,
                                       ALU.mult, ALU.add))
                link(dve.tensor_scalar(cnt[:, :], cnt[:, :], ROUND, -ROUND, ALU.add, ALU.add))
                link(dve.tensor_tensor(inc_a[:, 5:4 + E], cnt[:, 1:E], cnt[:, 0:E - 1], ALU.add))
                link(dve.tensor_copy(inc_a[:, 4:5], cnt[:, 0:1]))
                link(dve.tensor_tensor(inc_b[:, 4:4 + E], inc_a[:, 4:4 + E], inc_a[:, 2:2 + E], ALU.add))
                link(dve.tensor_tensor(inc_a[:, 4:4 + E], inc_b[:, 4:4 + E], inc_b[:, 0:E], ALU.add))
                inclusive = inc_a[:, 4:4 + E]
                link(dve.tensor_tensor(start_f[:, :], inclusive, cnt[:, :], ALU.subtract))
                link(dve.tensor_scalar(start_f[:, :], start_f[:, :], float(P), None, ALU.mult))
                link(dve.tensor_tensor(place[:, :, :], bank[1][:, 0:GT * E].rearrange("p (t e) -> p t e", e=E),
                                       start_f[:, :].unsqueeze(1).broadcast_to(flat), ALU.add))
                for k, oh in enumerate((oh1, oh2)):
                    link(dve.tensor_tensor(pick[:, :, :], place[:, :, :], oh[:, :, :], ALU.mult))
                    link(dve.tensor_reduce(slot_f[:, k, :], pick[:, :, :], AX.X, ALU.add))
                link(dve.tensor_copy(slot_i[:, g, :, :], slot_f[:, :, :]))
                link(dve.tensor_tensor(le[:, :, :], tile_no[:, :, :], inc_a[0:1, 4:4 + E].unsqueeze(1)
                                       .broadcast_to([1, NT, E]), ALU.is_ge))
                link(dve.tensor_reduce(eid_f[:, :], le[:, :, :], AX.X, ALU.add))
                link(dve.tensor_scalar(eid_c[:, :], eid_f[:, :], float(E - 1), None, ALU.min))
                dve.tensor_copy(eid_i[:, g, 0:NT], eid_c[:, :]).then_inc(routed, 1)
                dve.wait_ge(ex_ready, r + 1)
                link(dve.tensor_reduce(es[:, :], ex[:, :, :], AX.X, ALU.add))
                link(dve.reciprocal(pr1[:, :], es[:, :]))
                link(dve.tensor_tensor(pr2[:, :], e2[:, :], pr1[:, :], ALU.mult))
                link(dve.tensor_tensor(den[:, :], pr1[:, :], pr2[:, :], ALU.add))
                link(dve.tensor_scalar(den[:, :], den[:, :], 1e-9, None, ALU.max))
                link(dve.reciprocal(den[:, :], den[:, :]))
                link(dve.tensor_tensor(gates[:, g, 0, :], pr1[:, :], den[:, :], ALU.mult))
                link(dve.tensor_tensor(gates[:, g, 1, :], pr2[:, :], den[:, :], ALU.mult))

            def experts(m):
                L = MOE[m // GROUPS]
                f = L["f"]
                nc_f = f // P
                base = m * NT

                def x_low(t, s):
                    dve.wait_ge(ex_xh, t + base + 1)
                    dve.tensor_tensor(xl[s][:, :], bank[6][:, 0:P], xh[s][:, :].bitcast(F32), ALU.subtract).then_inc(ex_xl, 1)

                def multiply(t, s):
                    if L["up"] > f:
                        dve.wait_ge(ex_act, t + base + 1)
                        dve.tensor_tensor(hb[s][:, :], gb[s][:, :], bank[2 + s][:, :], ALU.mult).then_inc(ex_mul, 1)

                def h_low(t, s):
                    dve.wait_ge(ex_hh, t + base + 1)
                    dve.tensor_tensor(hl[s][:, 0:nc_f, :], bank[4 + s][:, 0:f].rearrange("p (c t) -> p c t", c=nc_f),
                                      hh[s][:, 0:nc_f, :].bitcast(F32), ALU.subtract).then_inc(ex_hl, 1)

                def y_copy(t):
                    dve.wait_ge(ex_dn, t + base + 1)
                    dve.tensor_reduce(Y[:, bass.ds(t, 1), :].rearrange("p a d -> p (a d)"),
                                      bank[7][:, 0:2 * D].rearrange("p (k d) -> p d k", k=2), AX.X, ALU.add).then_inc(ex_y, 1)

                if m:
                    dve.wait_ge(y_stored[(m - 1) % GROUPS], 16 * NT * ((m - 1) // GROUPS + 1))
                x_low(0, 0)
                x_low(1, 1)
                multiply(0, 0)
                x_low(2, 0)
                multiply(1, 1)
                h_low(0, 0)
                with dve.Fori(0, STEPS // 2) as i:
                    for u in range(2):
                        x_low(2 * i + (u + 3), (u + 1) % 2)
                        multiply(2 * i + (u + 2), u % 2)
                        h_low(2 * i + (u + 1), (u + 1) % 2)
                        y_copy(2 * i + u)
                multiply(NT - 1, (NT - 1) % 2)
                h_low(NT - 2, (NT - 2) % 2)
                y_copy(NT - 3)
                h_low(NT - 1, (NT - 1) % 2)
                y_copy(NT - 2)
                y_copy(NT - 1)

            def combine(m):
                g = m % GROUPS
                dve.wait_ge(gathered[g], 16 * TOPK * GT * (m // GROUPS + 1))
                for k, src in enumerate((XNR[:, g, :, :], YG[:, :, :])):
                    for j in range(GT):
                        t = g * GT + j
                        ins = dve.scalar_tensor_tensor(out=X[:, t, :], in0=src[:, j, :], scalar=gates[:, g, k, j:j + 1],
                                                       in1=X[:, t, :], op0=ALU.mult, op1=ALU.add)
                    if k < TOPK - 1:
                        link(ins)
                ins.then_inc(combined, 1)
                dve.wait_ge(combined, m + 1)

            def setup1():
                dve.wait_ge(in_col, 16)
                dve.wait_ge(s1_mm, 1)
                dve.tensor_scalar(kT[:, :, :], bank[2][:, 0:P].rearrange("p (b k) -> p b k", b=B), bk1, None,
                                  ALU.add).then_inc(s1_evac, 1)
                dve.wait_ge(s1_mm, 4)
                dve.tensor_copy(M1[:, :, :], bank[4][:, 0:P].rearrange("p (b k) -> p b k", b=B))
                dve.tensor_copy(r1[:, :, :], bank[5][0:1, 0:P].rearrange("p (b k) -> p b k", b=B))
                link(dve.tensor_copy(V1[:, :, :], bank[3][0:K, :].rearrange("p (b d) -> p b d", b=B)))
                dve.wait_ge(in_b1, 48)
                link(split3(bias1[:, :, :], bias1_raw[:, :, :]))
                dve.wait_ge(in_b2, 48)
                split3(bias2[:, :, :], YG[0:3, :, :]).then_inc(s1_evac, 1)

            def attention1(g):
                sc = bank[0][:, 0:GT * K].rearrange("p (t k) -> p t k", k=K)
                pr = [PR[:, i, 0:GT * K].rearrange("p (t k) -> p t k", k=K) for i in range(2)]
                dve.wait_ge(a1_s, g + 1)
                link(dve.tensor_reduce(m1[:, :], sc, AX.X, ALU.max))
                dve.tensor_tensor(pr[0], sc, m1[:, :].unsqueeze(2).broadcast_to([P, GT, K]), ALU.subtract).then_inc(a1_sub, 1)
                dve.wait_ge(a1_exp, g + 1)
                link(dve.tensor_reduce(es[:, :], pr[0], AX.X, ALU.add))
                link(dve.reciprocal(es[:, :], es[:, :]))
                dve.tensor_tensor(pr[1], pr[0], es[:, :].unsqueeze(2).broadcast_to([P, GT, K]), ALU.mult).then_inc(a1_p, 1)
                for q in range(GB):
                    dve.wait_ge(a1_o, GB * g + q + 1)
                    xv = X[:, g * GT + q * BT:g * GT + (q + 1) * BT, :]
                    dve.tensor_tensor(xv, xv, bank[4 + q][:, :].rearrange("p (t d) -> p t d", d=D), ALU.add).then_inc(a1_added, 1)
                dve.wait_ge(a1_added, GB * (g + 1))

            def setup2():
                dve.wait_ge(s2_mm, 5)
                link(dve.tensor_copy(vo[:, :], bank[2][:, 0:D]))
                dve.sem_inc(s2_evac, 1)
                dve.wait_ge(s2_mm, 6)
                dve.tensor_copy(U[:, :, :], bank[3][:, :].rearrange("p (b d) -> p b d", b=B)).then_inc(s2_evac, 1)

            def xattn2(g):
                R = GB * K
                lo, hi = g * R, (g + 1) * R
                layer_norm([g * GT + q * BT for q in range(GB)], XN[:, 0:GB, :], x2_n)
                dve.wait_ge(x2_q, g + 1)
                for c in range(2):
                    ins = dve.tensor_tensor(kq[lo:hi, c * 512:(c + 1) * 512], kall[lo:hi, c * 512:(c + 1) * 512],
                                            bank[c][lo:hi, :], ALU.mult)
                link(ins)
                link(dve.tensor_reduce(s16[lo:hi, :], kq[lo:hi, :].rearrange("p (h d) -> p h d", h=HL), AX.X, ALU.add))
                link(dve.tensor_scalar(s16[lo:hi, :], s16[lo:hi, :], float(DL) ** -0.5, None, ALU.mult))
                link(dve.tensor_scalar(m16[lo:hi, :], s16[lo:hi, :], NEG, None, ALU.max))
                dve.tensor_tensor(e16[lo:hi, 0, :], s16[lo:hi, :], m16[lo:hi, :], ALU.subtract)
                dve.tensor_scalar(e16[lo:hi, 1, :], m16[lo:hi, :], -1.0, NEG, ALU.mult, ALU.add).then_inc(x2_m, 1)
                dve.wait_ge(x2_e, g + 1)
                link(dve.scalar_tensor_tensor(out=sum16[lo:hi, :], in0=e16[lo:hi, 1, :], scalar=float(K - 1),
                                              in1=e16[lo:hi, 0, :], op0=ALU.mult, op1=ALU.add))
                link(dve.reciprocal(sum16[lo:hi, :], sum16[lo:hi, :]))
                link(dve.tensor_tensor(e16[lo:hi, :, :], e16[lo:hi, :, :],
                                       sum16[lo:hi, :].unsqueeze(1).broadcast_to([R, 2, HL]), ALU.mult))
                link(dve.tensor_tensor(s16[lo:hi, :], e16[lo:hi, 0, :], e16[lo:hi, 1, :], ALU.subtract))

                def heads(a):
                    return a.rearrange("p (h d) -> p h d", h=HL)

                dve.tensor_tensor(heads(attn2[lo:hi, :]), heads(vall[lo:hi, :]),
                                  s16[lo:hi, :].unsqueeze(2).broadcast_to([R, HL, DL]), ALU.mult)
                link(dve.tensor_tensor(heads(kq[lo:hi, :]), heads(vsum[lo:hi, :]),
                                       e16[lo:hi, 1, :].unsqueeze(2).broadcast_to([R, HL, DL]), ALU.mult))
                dve.tensor_tensor(attn2[lo:hi, :], attn2[lo:hi, :], kq[lo:hi, :], ALU.add).then_inc(x2_o, 1)
                for q in range(GB):
                    t, b = g * GT + q * BT, g * GB + q
                    dve.tensor_tensor(X[:, t + 1:t + BT, :], X[:, t + 1:t + BT, :],
                                      U[:, b, :].unsqueeze(1).broadcast_to([P, BT - 1, D]), ALU.add)
                    link(dve.scalar_tensor_tensor(out=X[:, t, :], in0=U[:, b, :], scalar=late[:, :], in1=X[:, t, :],
                                                  op0=ALU.mult, op1=ALU.add))
                dve.wait_ge(x2_mm, g + 1)
                for q in range(GB):
                    t = g * GT + q * BT
                    ins = dve.tensor_tensor(X[0:K, t, :], X[0:K, t, :], bank[4][0:K, q * D:(q + 1) * D], ALU.add)
                link(ins)

            def setup_ffn2():
                dve.wait_ge(in_ff2, 48)
                dve.tensor_reduce(wmean[:, 0, 0:1], w1_s[:, :], AX.X, ALU.add, apply_absolute_value=True)
                dve.tensor_reduce(wmean[:, 0, 1:2], w2_s[:, :, :], AX.XY, ALU.add, apply_absolute_value=True).then_inc(fs_sum, 1)
                dve.wait_ge(fs_mm, 1)
                mean, scale = wmean[:, 1, 0:2], wmean[:, 1, 2:4]
                link(dve.tensor_scalar(mean, bank[5][:, 0:2], 1.0 / (D * F2), 1e-5, ALU.mult, ALU.max))
                link(dve.reciprocal(scale, mean))
                w2v = w2_s[:, :, :]
                link(dve.tensor_scalar(w1_s[:, :], w1_s[:, :], scale[:, 0:1], ROUND, ALU.mult, ALU.add))
                link(dve.tensor_scalar(w1_s[:, :], w1_s[:, :], ROUND, 1.0, ALU.subtract, ALU.min))
                link(dve.tensor_scalar(w1_s[:, :], w1_s[:, :], -1.0, mean[:, 0:1], ALU.max, ALU.mult))
                link(dve.tensor_scalar(w2v, w2v, scale[:, 1:2], ROUND, ALU.mult, ALU.add))
                link(dve.tensor_scalar(w2v, w2v, ROUND, 1.0, ALU.subtract, ALU.min))
                link(dve.tensor_scalar(w2q[:, :, :], w2v, -1.0, None, ALU.max))
                for j in range(TAPS):
                    link(dve.tensor_tensor(zt[:, 0, :], w1_s[:, :], bank[2 + j][:, :], ALU.mult))
                    link(dve.tensor_copy(w1c_h[:, j, :], zt[:, 0, :]))
                    link(dve.tensor_tensor(w1c_l[:, j, :], zt[:, 0, :], w1c_h[:, j, :].bitcast(F32), ALU.subtract))
                for t in (xqh, xql):
                    dve.memset(t[:, 0:1].bitcast(F32), 0.0)
                    ins = dve.memset(t[:, S + 1:S + 2].bitcast(F32), 0.0)
                ins.then_inc(fs_ready, 1)

            def ffn2(g):
                layer_norm([g * GT + j for j in range(GT)], XQ[:, :, :])
                link(dve.tensor_reduce(amax[:, :], XQ[:, :, :], AX.X, ALU.max, apply_absolute_value=True))
                link(dve.tensor_scalar(amax[:, :], amax[:, :], 1e-5, None, ALU.max))
                link(dve.reciprocal(qscale[:, :], amax[:, :]))
                dve.tensor_scalar(qinv[:, :], amax[:, :], 1.0 / 127.0, None, ALU.mult)
                link(dve.tensor_scalar(qscale[:, :], qscale[:, :], 127.0, None, ALU.mult))
                for j in range(GT):
                    ins = dve.tensor_scalar(XQ[:, j, :], XQ[:, j, :], qscale[:, j:j + 1], ROUND, ALU.mult, ALU.add)
                link(ins)
                for j in range(GT):
                    dve.tensor_scalar(XQ[:, j, :], XQ[:, j, :], ROUND, qinv[:, j:j + 1], ALU.subtract,
                                      ALU.mult).then_inc(f2_xq, 1)
                for q in range(GB):
                    n = GB * g + q
                    dve.wait_ge(f2_xh, n + 1)
                    dve.tensor_tensor(xql[:, 1:S + 1], bank[6][:, :], xqh[:, 1:S + 1].bitcast(F32), ALU.subtract).then_inc(f2_xl, 1)

                    def quantise(j):
                        i, k = n * BT + j, q * BT + j
                        dve.wait_ge(f2_tt, i + 1)
                        z = bank[4 + j % 2][:, :]
                        link(dve.tensor_reduce(zmax[:, k:k + 1], z, AX.X, ALU.max, apply_absolute_value=True))
                        link(dve.tensor_scalar(zmax[:, k:k + 1], zmax[:, k:k + 1], 1e-5, None, ALU.max))
                        link(dve.reciprocal(zscale[:, k:k + 1], zmax[:, k:k + 1]))
                        link(dve.tensor_scalar(zscale[:, k:k + 1], zscale[:, k:k + 1], 127.0, None, ALU.mult))
                        dve.tensor_scalar(zt[:, j % 2, :], z, zscale[:, k:k + 1], ROUND, ALU.mult, ALU.add).then_inc(f2_zr, 1)
                        dve.wait_ge(f2_zr, i + 1)
                        dve.tensor_scalar(zq[:, j % 2, :], zt[:, j % 2, :], ROUND, 127.0, ALU.subtract, ALU.min).then_inc(f2_zq, 1)
                        link(dve.tensor_scalar(zinv[:, k:k + 1], zmax[:, k:k + 1], 1.0 / 127.0, wmean[:, 1, 1:2],
                                               ALU.mult, ALU.mult))

                    def add(j):
                        i, k, t = n * BT + j, q * BT + j, g * GT + q * BT + j
                        dve.wait_ge(f2_dn, i + 1)
                        dve.scalar_tensor_tensor(out=X[:, t, :], in0=bank[6][:, 0:D], scalar=zinv[:, k:k + 1], in1=X[:, t, :],
                                                 op0=ALU.mult, op1=ALU.add).then_inc(f2_added, 1)

                    quantise(0)
                    quantise(1)
                    add(0)
                    quantise(2)
                    add(1)
                    quantise(3)
                    add(2)
                    add(3)
                dve.wait_ge(f2_added, BT * GB * (g + 1))

            constants()
            setup(0)
            for g in range(GROUPS):
                dve.wait_ge(in_x[g], 16)
                layer_norm(half(g), XN[:, :, :], xn_ready)
                attention(g, g)
                layer_norm(half(g), XNR[:, g, :, :], xnr_ready)
                router(g)
            setup1()
            for g in range(GROUPS):
                experts(g)
            for g in range(GROUPS):
                combine(g)
                layer_norm(half(g), XN[:, :, :], xn_ready)
                attention1(g)
                layer_norm(half(g), XNR[:, g, :, :], xnr_ready)
                router(GROUPS + g)
            setup2()
            for g in range(GROUPS):
                experts(GROUPS + g)
            dve.wait_ge(in_col, 16)
            setup(1)
            setup_ffn2()
            for g in range(GROUPS):
                combine(GROUPS + g)
                xattn2(g)
                ffn2(g)
            dve.wait_ge(in_mask3, 16)
            dve.tensor_scalar(mfill[:, :], mask3_i, 0, FILL, ALU.is_equal, ALU.mult).then_inc(mrow_ready, 1)
            for g in range(GROUPS):
                layer_norm(half(g), XN[:, :, :], xn_ready)
                attention(GROUPS + g, g)
                layer_norm(half(g), XNR[:, g, :, :], xnr_ready)
                router(2 * GROUPS + g)
            for g in range(GROUPS):
                experts(2 * GROUPS + g)
            for g in range(GROUPS):
                combine(2 * GROUPS + g)

        @block.tensor
        def _(pe):
            def setup(i, wk, wq, wv):
                mm, ev = i * (B + 2), i * (B + 1)
                pe.matmul(bank[0][:, 0:P], wk, ctxT, start=True, stop=True).then_inc(setup_mm, 1)
                for b in range(B):
                    keys = kbd[:, b, :, :].rearrange("p h k -> p (h k)")
                    pe.wait_ge(setup_evac, ev + b + 1)
                    if b >= 2:
                        pe.wait_ge(m_evac, i * B + b - 1)
                    pe.matmul(bank[1 + b % 2][:, :], wq, keys, start=True, stop=True).then_inc(setup_mm, 1)
                    if i:
                        if b >= 2:
                            pe.wait_ge(r_evac, b - 1)
                        pe.matmul(bank[4 + b % 2][0:3, :], bq3.broadcast_to([P, 3]), keys, start=True, stop=True).then_inc(r_mm, 1)
                pe.wait_ge(ctx4_ready, 1)
                for b in range(B):
                    dst = bank[3][:, b * P:(b + 1) * P]
                    ins = pe.matmul(dst, ctx4[:, b, :, :].rearrange("p h k -> p (h k)"), wv, start=True, stop=(i == 0))
                    if i:
                        ins = pe.matmul(dst, ones_row[:, :], bv3, start=False, stop=True)
                ins.then_inc(setup_mm, 1)
                pe.wait_ge(setup_evac, ev + B + 1)
                pe.wait_ge(m_evac, (i + 1) * B)

            def setup1():
                pe.wait_ge(in_w1, 16)
                pe.wait_ge(in_col, 16)
                pe.wait_ge(in_row, 16)
                pe.matmul(bank[2][:, 0:P], wk1, ctxT, start=True, stop=True).then_inc(s1_mm, 1)
                pe.wait_ge(s1_evac, 1)
                keys = kT[:, :, :].rearrange("p b k -> p (b k)")
                pe.matmul(bank[4][:, 0:P], wq1, keys, start=True, stop=True).then_inc(s1_mm, 1)
                pe.matmul(bank[5][0:1, 0:P], bq1, keys, start=True, stop=True).then_inc(s1_mm, 1)
                for b in range(B):
                    dst = bank[3][0:K, b * D:(b + 1) * D]
                    pe.matmul(dst, ctxT[:, b * K:(b + 1) * K], wv1, start=True, stop=False)
                    ins = pe.matmul(dst, ones_row[:, 0:K], bv1, start=False, stop=True)
                ins.then_inc(s1_mm, 1)

            def attention1(g, n):
                for j in range(GT):
                    b = g * GB + j // BT
                    pe.wait_ge(xt_ready, GB * n + j // BT + 1)
                    pe.matmul(bank[0][:, j * K:(j + 1) * K], XT[:, j, :], M1[:, b, :], start=True, stop=False)
                    ins = pe.matmul(bank[0][:, j * K:(j + 1) * K], ones_row[:, :], r1[:, b, :], start=False, stop=True)
                ins.then_inc(a1_s, 1)
                pe.wait_ge(a1_p, g + 1)
                for q in range(GB):
                    for j in range(BT):
                        t = q * BT + j
                        ins = pe.transpose(bank[2 + q][0:K, j * P:(j + 1) * P], PR[:, 1, t * K:(t + 1) * K], ident[:, :])
                    ins.then_inc(a1_pt, 1)
                for q in range(GB):
                    pe.wait_ge(a1_ptc, GB * g + q + 1)
                    for j in range(BT):
                        ins = pe.matmul(bank[4 + q][:, j * D:(j + 1) * D], PT[0:K, q, j, :], V1[:, g * GB + q, :],
                                        start=True, stop=True)
                    ins.then_inc(a1_o, 1)

            def setup2():
                pe.wait_ge(in_l2, 48)
                for i in range(2):
                    for c in range(2):
                        ins = pe.matmul(bank[2 + 2 * i + c][:, :], ctxT, wkv_s[:, i * INNER + c * 512:i * INNER + (c + 1) * 512],
                                        start=True, stop=True)
                    ins.then_inc(s2_mm, 1)
                for c in range(2):
                    pe.wait_ge(s2_act, 3 + c)
                    ins = pe.matmul(bank[2 + c][:, :], batch_mask[:, :], vall[:, c * 512:(c + 1) * 512], start=True, stop=True)
                ins.then_inc(s2_mm, 1)
                for c in range(IC):
                    pe.wait_ge(s2_act, 5 + c // 4)
                    ins = pe.transpose(bank[4 + c // 4][:, c % 4 * P:(c % 4 + 1) * P], vsum[:, c * P:(c + 1) * P], ident[:, :])
                ins.then_inc(s2_mm, 1)
                for c in range(IC):
                    pe.wait_ge(s2_act, 7 + c // 4)
                    ins = pe.matmul(bank[2][:, 0:D], attn2[:, c * P:(c + 1) * P], wout_s[:, c, :], start=(c == 0), stop=(c == IC - 1))
                ins.then_inc(s2_mm, 1)
                pe.wait_ge(s2_evac, 1)
                for b in range(B):
                    dst = bank[3][:, b * D:(b + 1) * D]
                    pe.matmul(dst, ident[:, b * K:b * K + 1].broadcast_to([P, P]), vo[:, :], start=True, stop=False)
                    ins = pe.matmul(dst, ones_row[:, :], bout2, start=False, stop=True)
                ins.then_inc(s2_mm, 1)
                pe.wait_ge(s2_evac, 2)

            def xattn2(g):
                R = GB * K
                n = (g + 1) * R
                for q in range(GB):
                    pe.wait_ge(x2_n, GB * g + q + 1)
                    ins = pe.transpose(bank[6][:, q * P:(q + 1) * P], XN[:, q, :], ident[:, :])
                ins.then_inc(x2_t, 1)
                pe.wait_ge(x2_xl, g + 1)
                for c in range(2):
                    ins = pe.matmul(bank[c][0:n, :], XL[:, 0:n], wq_s[:, c * 512:(c + 1) * 512], start=True, stop=True)
                ins.then_inc(x2_q, 1)
                pe.wait_ge(x2_o, g + 1)
                for c in range(IC):
                    ins = pe.transpose(bank[2 + c // 4][:, c % 4 * n:(c % 4 + 1) * n], attn2[0:n, c * P:(c + 1) * P],
                                       ident[0:n, 0:n])
                    if c % 4 == 3:
                        ins.then_inc(x2_ot, 1)
                for q in range(GB):
                    dst = bank[4][0:K, q * D:(q + 1) * D]
                    for c in range(IC):
                        pe.wait_ge(x2_otc, 2 * g + c // 4 + 1)
                        r = g * R + q * K
                        pe.matmul(dst, oT[:, c, r:r + K], wout_s[:, c, :], start=(c == 0), stop=False)
                    ins = pe.matmul(dst, ones_row[:, 0:K], bout2, start=False, stop=True)
                ins.then_inc(x2_mm, 1)

            def setup_ffn2():
                pe.wait_ge(in_ff2, 48)
                pe.wait_ge(fs_sum, 1)
                for j in range(TAPS):
                    pe.matmul(bank[2 + j][:, :], ident[0:TAPS, j:j + 1].broadcast_to([TAPS, P]), cw_s[:, :], start=True, stop=True)
                pe.matmul(bank[5][:, 0:2], ones_f[:, :], wmean[:, 0, 0:2], start=True, stop=True).then_inc(fs_mm, 1)
                pe.wait_ge(fs_ready, 1)

            def ffn2(g):
                for q in range(GB):
                    n = GB * g + q
                    if n:
                        pe.wait_ge(f2_added, BT * n)
                    for j in range(BT):
                        pe.wait_ge(f2_xq, GT * g + q * BT + j + 1)
                        ins = pe.transpose(bank[6][:, j * P:(j + 1) * P], XQ[:, q * BT + j, :], ident[:, :])
                    ins.then_inc(f2_xt, 1)
                    pe.wait_ge(f2_xl, n + 1)
                    for c in range(F2C):
                        cs = slice(c * P, (c + 1) * P)
                        if n:
                            pe.wait_ge(f2_z, F2C * (n - 1) + c + 1)
                        for j in range(TAPS):
                            for k, (w, v) in enumerate(((w1c_h, xqh), (w1c_h, xql), (w1c_l, xqh))):
                                ins = pe.matmul(bank[c][:, :], w[:, j, cs], v[:, j:j + S],
                                                start=(j == 0 and k == 0), stop=(j == TAPS - 1 and k == 2))
                        ins.then_inc(f2_h, 1)

                    def back(j):
                        i = n * BT + j
                        if i >= 2:
                            pe.wait_ge(f2_zr, i - 1)
                        for c in range(F2C):
                            pe.wait_ge(f2_z, F2C * n + c + 1)
                            ins = pe.transpose(bank[4 + j % 2][:, c * P:(c + 1) * P], Z[:, c, j * P:(j + 1) * P], ident[:, :])
                        ins.then_inc(f2_tt, 1)

                    def turn(j):
                        i = n * BT + j
                        pe.wait_ge(f2_zq, i + 1)
                        if i:
                            pe.wait_ge(f2_qtc, i)
                        zb = bank[7][:, 0:F2 // 2].bitcast(BF16)
                        for c in range(F2C):
                            ins = pe.transpose(zb[:, c * P:(c + 1) * P], zq[:, j % 2, c * P:(c + 1) * P], ident_bf[:, :])
                        ins.then_inc(f2_qt, 1)

                    def down(j):
                        i = n * BT + j
                        pe.wait_ge(f2_qtc, i + 1)
                        if i:
                            pe.wait_ge(f2_added, i)
                        for c in range(F2C):
                            ins = pe.matmul(bank[6][:, 0:D], zqT[:, j % 2, c, :], w2q[:, c, :], start=(c == 0), stop=(c == F2C - 1))
                        ins.then_inc(f2_dn, 1)

                    back(0)
                    back(1)
                    turn(0)
                    back(2)
                    down(0)
                    turn(1)
                    back(3)
                    down(1)
                    turn(2)
                    down(2)
                    turn(3)
                    down(3)

            def transposes(n, src, done, dn):
                for q in range(GB):
                    for j in range(BT):
                        pe.wait_ge(done, dn * GT + q * BT + j + 1)
                        ins = pe.transpose(bank[6 + q][:, j * P:(j + 1) * P], src[:, q * BT + j, :], ident[:, :])
                    ins.then_inc(xt_mm, 1)

            def attention(a, g, n):
                for s in range(GT + 5):
                    if s < GT:
                        b = g * GB + s // BT
                        pe.wait_ge(xt_ready, GB * n + s // BT + 1)
                        if s >= 2:
                            pe.wait_ge(s_sub, a * GT + s - 1)
                        pe.matmul(bank[s % 2][:, :], XT[:, s, :], M[:, b, :], start=True, stop=False)
                        if a < GROUPS:
                            ins = pe.matmul(bank[s % 2][:, :], ones_row_bf[:, :], mrow[:, b, :, :].rearrange("p h k -> p (h k)"),
                                            start=False, stop=True)
                        else:
                            tok = (g * GT + s) * P
                            pe.matmul(bank[s % 2][:, :], ones_bf[0:3, :], brow[:, b, :], start=False, stop=False)
                            ins = pe.matmul(bank[s % 2][:, :], mfill[:, tok:tok + P], sel[:, :, :].rearrange("p h k -> p (h k)"),
                                            start=False, stop=True)
                        ins.then_inc(s_mm, 1)
                    j = s - 1
                    if 0 <= j < GT:
                        pe.wait_ge(s_exp, a * GT + j + 1)
                        if j >= 2:
                            pe.wait_ge(pt_ready, a * GT + j - 1)
                        for c in range(HC):
                            ins = pe.transpose(bank[2 + j % 2][:, c * P:(c + 1) * P], PR[:, j % 2, c * P:(c + 1) * P], ident[:, :])
                        ins.then_inc(pt_mm, 1)
                    j = s - 2
                    if 0 <= j < GT:
                        b = g * GB + j // BT
                        pe.wait_ge(pt_ready, a * GT + j + 1)
                        if j >= 2:
                            pe.wait_ge(o_norm, a * GT + j - 1)
                        for c in range(HC):
                            ins = pe.matmul(bank[4 + j % 2][:, c * VW:(c + 1) * VW], PT[:, j % 2, c, :], VB[:, b, c, :],
                                            start=True, stop=True)
                        ins.then_inc(o_mm, 1)
                    j = s - 3
                    if 0 <= j < GT:
                        pe.wait_ge(o_norm, a * GT + j + 1)
                        if j >= 1:
                            pe.wait_ge(ot_ready, a * GT + j)
                        pe.transpose(bank[6][:, 0:P], ON[:, j % 2, :], ident[:, :]).then_inc(ot_mm, 1)
                    j = s - 4
                    if 0 <= j < GT:
                        pe.wait_ge(ot_ready, a * GT + j + 1)
                        if j >= 1:
                            pe.wait_ge(x_added, a * GT + j)
                        if a < GROUPS:
                            ins = pe.matmul(bank[7][:, 0:D], OT[:, j % 2, :], wo0, start=True, stop=True)
                        else:
                            pe.matmul(bank[7][:, 0:D], OT[:, j % 2, :], wo3, start=True, stop=False)
                            ins = pe.matmul(bank[7][:, 0:D], ones_row[:, :], bo3, start=False, stop=True)
                        ins.then_inc(wo_mm, 1)

            def router(r, n, gate_w, bias_row=None):
                for j in range(GT):
                    pe.wait_ge(xt_ready, GB * n + j // BT + 1)
                    dst = bank[0][:, j * E:(j + 1) * E]
                    ins = pe.matmul(dst, XT[:, j, :], gate_w, start=True, stop=(bias_row is None))
                    if bias_row is not None:
                        ins = pe.matmul(dst, ones_row[:, :], bias_row, start=False, stop=True)
                ins.then_inc(lg_mm, 1)
                pe.wait_ge(both_ready, r + 1)
                rank = bank[1][:, 0:GT * E]
                pe.matmul(rank, before_bf[:, :], both[:, :, :].rearrange("p t e -> p (t e)"), start=True, stop=False,
                          skip_group_check=True)
                for j in range(GT - 1):
                    rest = GT - 1 - j
                    pe.matmul(bank[1][:, (j + 1) * E:GT * E].rearrange("p (t e) -> p t e", e=E), ones_bf[:, :],
                              both[:, j, :].unsqueeze(1).broadcast_to([P, rest, E]), start=False, stop=(j == GT - 2),
                              skip_group_check=True)
                for j in range(GT):
                    ins = pe.matmul(bank[1][:, GT * E:GT * E + E], ones_bf[:, :], both[:, j, :],
                                    start=(j == 0), stop=(j == GT - 1), skip_group_check=True)
                ins.then_inc(rank_mm, 1)

            def experts(m, up, dn):
                L = MOE[m // GROUPS]
                f, fu = L["f"], L["up"]
                nc_f = f // P
                g = m % GROUPS
                base = m * NT
                per_ring = [(NT - s + RING - 1) // RING for s in range(RING)]

                def tr_x(t, s4, round_):
                    pe.wait_ge(x_loaded[s4], 16 * (m * per_ring[s4]) + 16 * (round_ + 1))
                    if m or not isinstance(t, int) or t:
                        pe.wait_ge(ex_xl, t + base)
                    pe.transpose(bank[6][:, 0:P], xrow[s4][:, :], ident[:, :]).then_inc(ex_t, 1)

                def up_mm(t, s, e):
                    pe.wait_ge(ex_xl, t + base + 1)
                    for k in range(fu // f):
                        wh, wl = (up[k][:, bass.ds(e, 1), i, 0:f].rearrange("p a f -> p (a f)") for i in range(2))
                        dst = bank[2 * k + s][:, 0:f]
                        pe.matmul(dst, xh[s][:, :], wh, start=True, stop=False)
                        pe.matmul(dst, xh[s][:, :], wl, start=False, stop=False)
                        ins = pe.matmul(dst, xl[s][:, :], wh, start=False, stop=not L["bias"])
                        if L["bias"]:
                            ins = pe.matmul(dst, ones_bf[0:3, :], bias1[:, bass.ds(e, 1), :].rearrange("p a f -> p (a f)"),
                                            start=False, stop=True)
                    ins.then_inc(ex_up, 1)

                def tr_h(t, s):
                    if fu > f:
                        pe.wait_ge(ex_mul, t + (m % GROUPS * NT + 1))
                    else:
                        pe.wait_ge(ex_act, t + base + 1)
                    for c in range(nc_f):
                        ins = pe.transpose(bank[4 + s][:, c * P:(c + 1) * P], hb[s][:, c * P:(c + 1) * P], ident[:, :])
                    ins.then_inc(ex_ht, 1)

                def dn_mm(t, s, e):
                    pe.wait_ge(ex_hl, t + base + 1)
                    if m or not isinstance(t, int) or t:
                        pe.wait_ge(ex_y, t + base)
                    y = bank[7][:, 0:2 * D]
                    for c in range(nc_f):
                        w = dn[:, bass.ds(e, 1), :, c * P:(c + 1) * P].rearrange("p a k d -> p (a k) d")
                        pe.matmul(y, hh[s][:, c, :], w, start=(c == 0), stop=False, skip_group_check=True)
                        ins = pe.matmul(y, hl[s][:, c, :], w, start=False, stop=(c == nc_f - 1), skip_group_check=True)
                    if L["bias"]:
                        ins = pe.matmul(bank[7][:, 0:D], ones_bf[0:3, :], bias2[:, bass.ds(e, 1), :].rearrange("p a f -> p (a f)"),
                                        start=False, stop=True, skip_group_check=True)
                    ins.then_inc(ex_dn, 1)

                def experts_of(t, count):
                    _, values = nc.values_load_multi_w_load_instructions(
                        eid_i[0:1, g, bass.ds(t, count)], engines=[mybir.EngineType.PE], min_val=0, max_val=E - 1,
                        skip_runtime_bounds_check_because="the numbers are clamped where they are made", bass_reorder=False)
                    return values

                pe.wait_ge(routed, m + 1)
                e0, e1 = experts_of(0, 2)
                tr_x(0, 0, 0)
                tr_x(1, 1, 0)
                up_mm(0, 0, e0)
                tr_x(2, 2, 0)
                up_mm(1, 1, e1)
                tr_h(0, 0)
                with pe.Fori(0, STEPS // RING) as i:
                    ids = experts_of(RING * i, RING + 2)
                    for u in range(RING):
                        tr_x(RING * i + (u + 3), (u + 3) % RING, i + (u + 3) // RING)
                        up_mm(RING * i + (u + 2), u % 2, ids[u + 2])
                        tr_h(RING * i + (u + 1), (u + 1) % 2)
                        dn_mm(RING * i + u, u % 2, ids[u])
                ea, eb, ec = experts_of(NT - 3, 3)
                up_mm(NT - 1, (NT - 1) % 2, ec)
                tr_h(NT - 2, (NT - 2) % 2)
                dn_mm(NT - 3, (NT - 3) % 2, ea)
                tr_h(NT - 1, (NT - 1) % 2)
                dn_mm(NT - 2, (NT - 2) % 2, eb)
                dn_mm(NT - 1, (NT - 1) % 2, ec)

            pe.wait_ge(const_ready, 1)
            pe.wait_ge(in_w0, 16)
            setup(0, wk0, wq0, wv0)
            pe.wait_ge(mrow_ready, 1)
            for g in range(GROUPS):
                transposes(LN_ORDER["a0", g], XN[:, :, :], xn_ready, g)
                attention(g, g, LN_ORDER["a0", g])
                transposes(LN_ORDER["r0", g], XNR[:, g, :, :], xnr_ready, g)
                router(g, LN_ORDER["r0", g], gate0)
            setup1()
            pe.wait_ge(w_split, 2 * E)
            for g in range(GROUPS):
                experts(g, [WA], WB)
            pe.wait_ge(s1_evac, 2)
            for g in range(GROUPS):
                transposes(LN_ORDER["a1", g], XN[:, :, :], xn_ready, GROUPS + g)
                attention1(g, LN_ORDER["a1", g])
                transposes(LN_ORDER["r1", g], XNR[:, g, :, :], xnr_ready, GROUPS + g)
                router(GROUPS + g, LN_ORDER["r1", g], gate1, br1)
            setup2()
            pe.wait_ge(w_split, 4 * E)
            for g in range(GROUPS):
                experts(GROUPS + g, [WC[:, :, :, 0:256]], WC[:, :, :, 256:512])
            pe.wait_ge(in_w3, 16)
            setup(1, wk3, wq3, wv3)
            setup_ffn2()
            for g in range(GROUPS):
                xattn2(g)
                ffn2(g)
            pe.wait_ge(mrow_ready, 2)
            for g in range(GROUPS):
                transposes(LN_ORDER["a3", g], XN[:, :, :], xn_ready, 2 * GROUPS + g)
                attention(GROUPS + g, g, LN_ORDER["a3", g])
                transposes(LN_ORDER["r3", g], XNR[:, g, :, :], xnr_ready, 2 * GROUPS + g)
                router(2 * GROUPS + g, LN_ORDER["r3", g], gate3)
            pe.wait_ge(w_split, 4 * E + 3 * E)
            for g in range(GROUPS):
                experts(2 * GROUPS + g, [WC, WA], WB)


def kernel(**inputs):
    import numpy as _np
    import concourse.bacc as _bacc
    from concourse import mybir as _mybir
    from concourse.bass_utils import run_bass_kernel_spmd as _run

    a = {k: _np.asarray(v) for k, v in inputs.items()}
    ctxT = a["ctx_1024"].reshape(-1, 128).T
    columns = [a[k][:, None] for k in ("L1_xattn_bq", "L1_xattn_bk", "L3_xattn_bq", "L3_xattn_bk")]
    arrays = {
        "p0": _np.concatenate([ctxT, a["L0_xattn_Wk"].T, a["L0_xattn_Wq"], a["L0_xattn_Wv"].T, a["L0_xattn_Wo"].T,
                               a["L0_ffn_gate_w"]], axis=1),
        "p1": _np.concatenate([a["L1_xattn_Wk"].T, a["L1_xattn_Wq"], a["L1_xattn_Wv"].T, a["L1_ffn_Wr"]], axis=1),
        "p3": _np.concatenate([a["L3_xattn_Wk"], a["L3_xattn_Wq"].T, a["L3_xattn_Wv"], a["L3_xattn_Wo"],
                               a["L3_ffn_w_gate"]], axis=1),
        "cols": _np.concatenate(columns + [a["L2_ffn_conv_b"].reshape(4, 128).T], axis=1),
        "rows": _np.concatenate([a["L1_xattn_bv"], a["L3_xattn_bv"], a["L3_xattn_bo"], a["L2_xattn_bout"],
                                 a["L1_ffn_br"]])[None],
        "bias": _np.concatenate([a["L1_ffn_b1"].reshape(-1), a["L1_ffn_b2"].reshape(-1)])[None],
        "x": a["x"].reshape(-1, 128),
        "mask0": a["mask_Bx1xS2_if1"].reshape(1, 4, 32),
        "mask3": a["mask_BxSxS2_if1"].reshape(-1, 32).T,
        "fc0": a["L0_ffn_fc_w"],
        "pj0": a["L0_ffn_proj_w"],
        "fc1": a["L1_ffn_W1"],
        "pj1": a["L1_ffn_W2"],
        "fc3": a["L3_ffn_w_gate_up"],
        "pj3": a["L3_ffn_w_down"],
        "wkv": a["L2_xattn_Wkv"],
        "wq2": a["L2_xattn_Wq"],
        "wout2": a["L2_xattn_Wout"],
        "w1t": a["L2_ffn_w1"].T,
        "w2t": a["L2_ffn_w2"].T,
        "cw": a["L2_ffn_conv_w"][:, 0, :].T,
    }
    nc = _bacc.Bacc("TRN2", target_bir_lowering=False, num_devices=1)
    args, maps = [], {}
    for name, v in arrays.items():
        v = _np.ascontiguousarray(v)
        maps[f"in_{name}_dram"] = v
        args.append(nc.dram_tensor(f"in_{name}_dram", v.shape, _mybir.dt.from_np(v.dtype), kind="ExternalInput").ap())
    out = nc.dram_tensor("out_dram", (2048, 128), _mybir.dt.float32, kind="ExternalOutput").ap()
    build(nc, *args, out)
    r = _run(nc, [maps], core_ids=[0])
    return r.results[0]["out_dram"].reshape(4, 512, 128)
```

```python
from contextlib import ExitStack

import concourse.bass as bass
from concourse import mybir

F32 = mybir.dt.float32
F32R = mybir.dt.float32r
BF16 = mybir.dt.bfloat16
I32 = mybir.dt.int32
ACT = mybir.ActivationFunctionType
ALU = mybir.AluOpType
AX = mybir.AxisListType

P = 128
B, S, D = 4, 512, 128
K = 32
H = 16
DK = D // H
HK = H * K
TILES = B * S // P
BT = S // P
GROUPS = 2
GT = TILES // GROUPS
GB = B // GROUPS
E, TOPK = 8, 2
HPC = P // K
HC = H // HPC
VW = HPC * DK + HPC
NT = (GT * P * TOPK + E * (P - 1)) // P
PAD = 4
RAW = 6
RING = 4
STEPS = NT - 3
EPS = 1e-5
FILL = -float(2 ** 100)
ROUND = 1.5 * 2.0 ** 23
NEG = -3.4028234663852886e38
HL, DL = 16, 64
INNER = HL * DL
IC = INNER // P
ZBUFS = 4
F2, F2C, TAPS = 512, 4, 3
RSQRT_SEED = float(0x5F3759DF)
assert STEPS % RING == 0 and GT == E == 2 * PAD

MOE = [
    dict(up=512, f=512, act=ACT.Gelu, bias=False),
    dict(up=256, f=256, act=ACT.Relu, bias=True),
    dict(up=1024, f=512, act=ACT.Silu, bias=False),
]


def build(nc, p0, p1, p3, cols, rows, bias, x, mask0, mask3, fc0, pj0, fc1, pj1, fc3, pj3, wkv, wq2, wout2, w1t, w2t, cw,
          out):
    ctx = ExitStack()
    with ctx:
        def sb(name, shape, dt):
            return ctx.enter_context(nc.sbuf_tensor(name, shape, dt))

        def sem(name):
            return ctx.enter_context(nc.semaphore(name))

        xs_dram = [nc.dram_tensor(f"xs{g}", (NT * P, D), F32, kind="Internal").ap() for g in range(GROUPS)]
        ys_dram = [nc.dram_tensor(f"ys{g}", (NT * P, D), F32, kind="Internal").ap() for g in range(GROUPS)]
        xs_tiles = [a.rearrange("(t p) d -> t p d", p=P) for a in xs_dram]
        ys_tiles = [a.rearrange("(t p) d -> t p d", p=P) for a in ys_dram]

        bank = [ctx.enter_context(nc.psum_tensor(f"bank{i}", [P, 512], F32)) for i in range(8)]

        ident = sb("ident", [P, P], F32)
        ones_row = sb("ones_row", [1, P], F32)
        ones_row_bf = sb("ones_row_bf", [1, P], BF16)
        ones_bf = sb("ones_bf", [P, P], BF16)
        before_bf = sb("before_bf", [P, P], BF16)
        head_mask = sb("head_mask", [P, H], F32)
        chunk_mask = sb("chunk_mask", [P, HPC], F32)
        expert_i = sb("expert_i", [P, E], I32)
        prefer = sb("prefer", [P, E], F32)
        tile_i = sb("tile_i", [1, NT, E], I32)
        tile_no = sb("tile_no", [1, NT, E], F32)
        zeros = sb("zeros", [P, P], F32)
        ones_f = sb("ones_f", [P, P], F32)
        ident_bf = sb("ident_bf", [P, P], BF16)

        X = sb("X", [P, TILES, D], F32)
        w0 = sb("w0", [P, 5 * P + E], F32)
        ctxT, wk0, wq0, wv0, wo0 = (w0[:, i * P:(i + 1) * P] for i in range(5))
        gate0 = w0[:, 5 * P:5 * P + E]
        mask0_i = sb("mask0_i", [1, B, K], I32)
        w1 = sb("w1", [P, 3 * P + E], F32)
        wk1, wq1, wv1 = (w1[:, i * P:(i + 1) * P] for i in range(3))
        gate1 = w1[:, 3 * P:3 * P + E]
        w3 = sb("w3", [P, 4 * P + E], F32)
        wk3, wq3, wv3, wo3 = (w3[:, i * P:(i + 1) * P] for i in range(4))
        gate3 = w3[:, 4 * P:4 * P + E]
        col = sb("col", [P, 4], F32)
        bq1, bk1, bq3, bk3 = (col[:, i:i + 1] for i in range(4))
        row = sb("row", [1, 4 * P + E], F32)
        bv1, bv3, bo3, bout2 = (row[:, i * P:(i + 1) * P] for i in range(4))
        br1 = row[:, 4 * P:4 * P + E]
        part_no = sb("part_no", [3, 1], I32)
        part_f = sb("part_f", [3, 1], F32)
        minus_12 = sb("minus_12", [3, 1], F32)
        minus_2 = sb("minus_2", [3, 1], F32)
        brow = sb("brow", [3, B, HK], BF16)
        sel = sb("sel", [K, H, K], BF16)
        sel_f = sb("sel_f", [K, K], F32)
        vo = sb("vo", [P, D], F32)
        M1 = sb("M1", [P, B, K], F32)
        r1 = sb("r1", [P, B, K], F32)
        br_all = sb("br_all", [P, E], F32)
        V1 = sb("V1", [K, B, D], F32)
        batch_mask = sb("batch_mask", [P, P], F32)
        late = sb("late", [P, 1], F32)

        ctx4 = sb("ctx4", [P, B, HPC, K], F32)
        kT = sb("kT", [P, B, K], F32)
        with nc.sbuf_tensor("bias1", [3, E, 256], BF16) as bias1, nc.sbuf_tensor("bias2", [3, E, D], BF16) as bias2:
            pass
        M = sb("M", [P, B, HK], F32)
        VB = sb("VB", [P, B, HC, VW], F32)
        mfill = sb("mfill", [K, B * S], BF16)
        mrow = mfill[0:1, :].rearrange("p (b h k) -> p b h k", b=B, h=H)
        stats = sb("stats", [P, TILES, 6], F32)
        mv = sb("mv", [P, TILES, 2], F32)
        ve, ya, yb, rstd = (sb(n, [P, TILES], F32) for n in ("ve", "ya", "yb", "rstd"))
        ti, yi = (sb(n, [P, TILES], I32) for n in ("ti", "yi"))
        XNR = sb("XNR", [P, TILES, D], F32)
        smax = sb("smax", [P, 2, H], F32)
        rsum = sb("rsum", [P, 2, H], F32)
        ON = sb("ON", [P, 2, D], F32)
        OT = sb("OT", [P, 2, P], F32)

        both = sb("both", [P, GROUPS, GT, E], BF16)
        ahead_a = sb("ahead_a", [P, GROUPS, PAD + GT, E], BF16)
        ahead_b = sb("ahead_b", [P, GROUPS, PAD + GT, E], BF16)
        m1, m2, c1, de, e2, es, pr1, pr2, den = (
            sb(n, [P, TILES], F32) for n in ("m1", "m2", "c1", "de", "e2", "es", "pr1", "pr2", "den"))
        ex = sb("ex", [P, TILES, E], F32)
        gates = sb("gates", [P, TOPK, TILES], F32)
        cnt = sb("cnt", [P, GROUPS, E], F32)
        inc_a = sb("inc_a", [P, GROUPS, PAD + E], F32)
        inc_b = sb("inc_b", [P, GROUPS, PAD + E], F32)
        start_f = sb("start_f", [P, GROUPS, E], F32)
        slot_f = sb("slot_f", [P, TOPK, TILES], F32)
        slot_i = sb("slot_i", [P, TOPK, TILES], I32)
        eid_f = sb("eid_f", [1, GROUPS, NT], F32)
        eid_c = sb("eid_c", [1, GROUPS, NT], F32)
        eid_i = sb("eid_i", [1, GROUPS, NT + 1], I32)

        with ExitStack() as l2f_tiles:
            def l2f(name, shape, dt=F32):
                return l2f_tiles.enter_context(nc.sbuf_tensor(name, shape, dt))

            w1c_h = l2f("w1c_h", [P, TAPS, F2], F32R)
            w1c_l = l2f("w1c_l", [P, TAPS, F2], F32R)
            w1_s = l2f("w1_s", [P, F2])
            w2_s = l2f("w2_s", [P, F2C, D])
            w2q = l2f("w2q", [P, F2C, D], BF16)
            cw_s = l2f("cw_s", [TAPS, F2])
            U = l2f("U", [P, B, D])
            cb_raw = l2f("cb_raw", [3, F2])
            cb = l2f("cb", [3, F2], BF16)
            Z = l2f("Z", [P, ZBUFS, F2])
        WA = sb("WA", [P, E, 2, 512], F32R)
        with ExitStack() as l2_tiles:
            def l2x(name, shape, dt=F32):
                return l2_tiles.enter_context(nc.sbuf_tensor(name, shape, dt))

            wkv_s = l2x("wkv_s", [P, 2 * INNER])
            wq_s = l2x("wq_s", [P, INNER])
            wout_s = l2x("wout_s", [P, IC, D])
            kall = l2x("kall", [P, INNER])
            vall = l2x("vall", [P, INNER])
            vsum = l2x("vsum", [P, INNER])
            attn2 = l2x("attn2", [P, INNER])
        WB = sb("WB", [P, E, 2, 512], F32R)
        WC = sb("WC", [P, E, 2, 512], F32R)
        wmean = sb("wmean", [P, 2, 4], F32)
        raw = sb("raw", [P, RAW, 512], F32)
        xrow = [sb(f"xrow{i}", [P, D], F32) for i in range(RING)]
        with ExitStack() as attention_tiles:
            def at(name, shape, dt):
                return attention_tiles.enter_context(nc.sbuf_tensor(name, shape, dt))

            rrow = at("rrow", [3, HK], F32)
            XT = at("XT", [P, TILES, P], F32)
            with ExitStack() as routing_tiles:
                lg, second, cand, oh1, oh2, dl, place, pick = (
                    routing_tiles.enter_context(nc.sbuf_tensor(n, [P, TILES, E], F32))
                    for n in ("lg", "second", "cand", "oh1", "oh2", "dl", "place", "pick"))
                le = routing_tiles.enter_context(nc.sbuf_tensor("le", [1, GROUPS, NT, E], F32))
            PR = at("PR", [P, 2, HK], F32)
            with nc.sbuf_tensor("PT1", [K, TILES, P], F32) as PT1:
                pass
            PT = at("PT", [P, 2, HC, P], F32)
        with ExitStack() as ffn_tiles:
            def ff(name, shape, dt):
                return ffn_tiles.enter_context(nc.sbuf_tensor(name, shape, dt))

            XQ = ff("XQ", [P, TILES, D], F32)
            xqh = ff("xqh", [P, 2, S + 2], F32R)
            xql = ff("xql", [P, 2, S + 2], F32R)
            zqT = ff("zqT", [P, 2, F2C, P], BF16)
        xh = [sb(f"xh{i}", [P, P], F32R) for i in range(2)]
        xl = [sb(f"xl{i}", [P, P], F32R) for i in range(2)]
        hb = [sb(f"hb{i}", [P, 512], F32) for i in range(2)]
        hh = [sb(f"hh{i}", [P, 4, P], F32R) for i in range(2)]
        gb = [sb(f"gb{i}", [P, 512], F32) for i in range(2)]
        hl = [sb(f"hl{i}", [P, 4, P], F32R) for i in range(2)]
        with nc.sbuf_tensor("kbd", [P, B, H, K], F32) as kbd:
            pass
        with nc.sbuf_tensor("bias1_raw", [3, E, 256], F32) as bias1_raw:
            pass
        Y = sb("Y", [P, NT, D], F32)
        YG = sb("YG", [P, GT, D], F32)
        XL = sb("XL", [P, P], F32)
        s16 = sb("s16", [P, HL], F32)
        m16 = sb("m16", [P, HL], F32)
        e16 = sb("e16", [P, 2, HL], F32)
        sum16 = sb("sum16", [P, HL], F32)
        amax = sb("amax", [P, GT], F32)
        qscale = sb("qscale", [P, GT], F32)
        qinv = sb("qinv", [P, GT], F32)
        zmax = sb("zmax", [P, 2], F32)
        zscale = sb("zscale", [P, 2], F32)
        zinv = sb("zinv", [P, TILES], F32)

        in_w0, in_mask0 = sem("in_w0"), sem("in_mask0")
        in_x = [sem(f"in_x{g}") for g in range(GROUPS)]
        in_raw = [sem(f"in_raw{i}") for i in range(RAW)]
        zeroed, const_ready, pool_chain, dve_chain = sem("zeroed"), sem("const_ready"), sem("pool_chain"), sem("dve_chain")
        zeros_ready, xn_ready, xnr_ready = sem("zeros_ready"), sem("xn_ready"), sem("xnr_ready")
        setup_mm, setup_evac, m_evac, ctx4_ready, mrow_ready = sem("setup_mm"), sem("setup_evac"), sem("m_evac"), sem("ctx4_ready"), sem("mrow_ready")
        xt_mm, xt_ready = sem("xt_mm"), sem("xt_ready")
        s_mm, s_sub, s_exp, pt_mm, pt_ready = sem("s_mm"), sem("s_sub"), sem("s_exp"), sem("pt_mm"), sem("pt_ready")
        o_mm, o_norm, ot_mm, ot_ready, wo_mm, x_added = sem("o_mm"), sem("o_norm"), sem("ot_mm"), sem("ot_ready"), sem("wo_mm"), sem("x_added")
        lg_mm, both_ready, rank_mm, routed, dl_ready, ex_ready = sem("lg_mm"), sem("both_ready"), sem("rank_mm"), sem("routed"), sem("dl_ready"), sem("ex_ready")
        scattered, y_stored = ([sem(f"{n}{g}") for g in range(GROUPS)] for n in ("scattered", "y_stored"))
        gathered = [[sem(f"gathered{g}{k}") for k in range(TOPK)] for g in range(GROUPS)]
        x_loaded = [sem(f"x_loaded{i}") for i in range(RING)]
        w_split = sem("w_split")
        ex_t, ex_xh, ex_xl, ex_up, ex_act = sem("ex_t"), sem("ex_xh"), sem("ex_xl"), sem("ex_up"), sem("ex_act")
        ex_ht, ex_hh, ex_hl, ex_dn, ex_y = sem("ex_ht"), sem("ex_hh"), sem("ex_hl"), sem("ex_dn"), sem("ex_y")
        stored = sem("stored")
        in_w1, in_w3, in_col, in_row, in_b1, in_b2, in_mask3, in_l2, in_ff2 = (
            sem(n) for n in ("in_w1", "in_w3", "in_col", "in_row", "in_b1", "in_b2", "in_mask3", "in_l2", "in_ff2"))
        s1_mm, s1_evac, s2_mm, s2_evac, s2_act, r_mm, r_evac = (
            sem(n) for n in ("s1_mm", "s1_evac", "s2_mm", "s2_evac", "s2_act", "r_mm", "r_evac"))
        a1_s, a1_sub, a1_exp, a1_p, a1_pt, a1_ptc, a1_o, a1_added = (
            sem(n) for n in ("a1_s", "a1_sub", "a1_exp", "a1_p", "a1_pt", "a1_ptc", "a1_o", "a1_added"))
        x2_n, x2_t, x2_xl, x2_q, x2_m, x2_e, x2_o, x2_ot, x2_otc, x2_y, x2_yc, x2_mm, x2_added = (
            sem(n) for n in ("x2_n", "x2_t", "x2_xl", "x2_q", "x2_m", "x2_e", "x2_o", "x2_ot", "x2_otc", "x2_y", "x2_yc",
                             "x2_mm", "x2_added"))
        fs_sum, fs_mm, fs_ready = (sem(n) for n in ("fs_sum", "fs_mm", "fs_ready"))
        f2_xq, f2_xt, f2_xh, f2_xl, f2_h, f2_z, f2_zq, f2_qt, f2_qtc, f2_dn, f2_added = (
            sem(n) for n in ("f2_xq", "f2_xt", "f2_xh", "f2_xl", "f2_h", "f2_z", "f2_zq", "f2_qt", "f2_qtc",
                             "f2_dn", "f2_added"))
        ex_mul = sem("ex_mul")
        combined = sem("combined")

        N_W1, N_W3 = 2 * E, 4 * E
        N_D3, N_U3 = N_W3 + E, N_W3 + 2 * E
        mask3_i = XNR[0:K, :, :].rearrange("p t d -> p (t d)").bitcast(I32)
        oT = wkv_s[:, INNER:2 * INNER].rearrange("p (c r) -> p c r", c=IC)
        kq = wkv_s[:, 0:INNER]
        zq = w1_s[:, :].bitcast(BF16).rearrange("p (i f) -> p i f", i=2)

        block = ctx.enter_context(nc.Block())

        @block.sync
        def _(sp):
            sp.dma_start(w0[:, :], p0).then_inc(in_w0, 16)
            sp.dma_start(mask0_i[:, :, :], mask0).then_inc(in_mask0, 16)
            x_v = x.rearrange("(g t p) d -> g p t d", g=GROUPS, p=P)
            for g in range(GROUPS):
                sp.dma_start(X[:, g * GT:(g + 1) * GT, :], x_v[g]).then_inc(in_x[g], 16)
            sp.dma_start(col[:, :], cols).then_inc(in_col, 16)
            sp.dma_start(row[:, :], rows).then_inc(in_row, 16)
            sp.dma_start(w1[:, :], p1).then_inc(in_w1, 16)
            sp.dma_start(w3[:, :], p3).then_inc(in_w3, 16)
            def load_weights(n0, matrices):
                for i, (src, width) in enumerate(matrices):
                    n = n0 + i
                    if n >= RAW:
                        sp.wait_ge(w_split, n - RAW + 1)
                    dst = raw[:, n % RAW, 0:width]
                    if src.shape[0] != P:
                        src = src.rearrange("(c p) d -> p c d", p=P)
                        dst = dst.rearrange("p (c d) -> p c d", d=D)
                    sp.dma_start(dst, src).then_inc(in_raw[n % RAW], 16)

            sp.wait_ge(zeros_ready, 1)
            for g in range(GROUPS):
                sp.dma_start(xs_tiles[g].rearrange("t p d -> p t d"),
                             zeros[:, :].unsqueeze(1).broadcast_to([P, NT, D])).then_inc(zeroed, 16)
            load_weights(0, [(w[e], 512) for e in range(E) for w in (fc0, pj0)])

            def experts(m):
                g = m % GROUPS
                xs_t, ys_t = xs_tiles[g], ys_tiles[g]
                base = m * NT

                def load(t, s):
                    sp.dma_start(xrow[s][:, :], xs_t[bass.ds(t, 1)].rearrange("a p d -> p (a d)")).then_inc(x_loaded[s], 16)

                def store(t):
                    sp.wait_ge(ex_y, t + base + 1)
                    sp.dma_start(ys_t[bass.ds(t, 1)].rearrange("a p d -> p (a d)"),
                                 Y[:, bass.ds(t, 1), :].rearrange("p a d -> p (a d)")).then_inc(y_stored[g], 16)

                sp.wait_ge(scattered[g], 16 * TOPK * GT * (m // GROUPS + 1))
                if m:
                    sp.wait_ge(ex_t, base)
                for s in range(RING):
                    load(s, s)
                for s in range(RING):
                    sp.wait_ge(ex_t, base + s + 1)
                    load(RING + s, s)
                with sp.Fori(2, NT // RING) as i:
                    for s in range(RING):
                        sp.wait_ge(ex_t, i * RING + (base - RING + s + 1))
                        load(i * RING + s, s)
                        store((i - 2) * RING + s)
                for t in range(NT // RING * RING, NT):
                    sp.wait_ge(ex_t, base + t - RING + 1)
                    load(t, t % RING)
                    store(t - 2 * RING)
                for t in range(NT - 2 * RING, NT):
                    store(t)

            sp.wait_ge(m_evac, B)
            for i in range(3):
                sp.dma_start(bias1_raw[i:i + 1, :, :].rearrange("p e f -> p (e f)"), bias[:, 0:E * 256]).then_inc(in_b1, 16)
                sp.dma_start(YG[i:i + 1, :, :].rearrange("p e f -> p (e f)"), bias[:, E * 256:E * (256 + D)]).then_inc(in_b2, 16)
            sp.wait_ge(w_split, N_W1 - RAW + 2)
            load_weights(N_W1, [(w[e], 256) for e in range(E) for w in (fc1, pj1)])
            for g in range(GROUPS):
                experts(g)
            sp.wait_ge(ex_dn, 2 * NT)
            sp.dma_start(wkv_s[:, :], wkv).then_inc(in_l2, 16)
            sp.dma_start(wq_s[:, :], wq2).then_inc(in_l2, 16)
            sp.dma_start(wout_s[:, :, :], wout2.rearrange("(c p) d -> p c d", p=P)).then_inc(in_l2, 16)
            sp.dma_start(w1_s[:, :], w1t).then_inc(in_ff2, 16)
            sp.dma_start(w2_s[:, :, :], w2t.rearrange("(c p) d -> p c d", p=P)).then_inc(in_ff2, 16)
            sp.dma_start(cw_s[:, :], cw).then_inc(in_ff2, 16)
            for i in range(3):
                sp.dma_start(cb_raw[i:i + 1, :], bias[:, E * (256 + D):]).then_inc(in_ff2, 16)
            for g in range(GROUPS):
                experts(GROUPS + g)
            load_weights(N_W3, [(fc3[e, :, 0:512], 512) for e in range(E)])
            sp.wait_ge(x2_added, 1)
            sp.dma_start(mask3_i, mask3).then_inc(in_mask3, 16)
            load_weights(N_D3, [(pj3[e], 512) for e in range(E)])
            load_weights(N_U3, [(fc3[e, :, 512:1024], 512) for e in range(E)])
            for g in range(GROUPS):
                experts(2 * GROUPS + g)
            out_v = out.rearrange("(g t p) d -> g p t d", g=GROUPS, p=P)
            for g in range(GROUPS):
                sp.wait_ge(combined, 2 * GROUPS + g + 1)
                sp.dma_start(out_v[g], X[:, g * GT:(g + 1) * GT, :]).then_inc(stored, 16)
            sp.wait_ge(stored, 16 * GROUPS)

        @block.gpsimd
        def _(pool):
            n = [0]

            def link(ins):
                n[0] += 1
                ins.then_inc(pool_chain, 1)
                pool.wait_ge(pool_chain, n[0])

            link(pool.memset(zeros[:, :], 0.0))
            pool.sem_inc(zeros_ready, 1)
            link(pool.affine_select(out=ident[:, :], in_=zeros[:, :], compare_op=ALU.not_equal, fill=1.0,
                                    base=0, pattern=[[-1, P]], channel_multiplier=1))
            pool.memset(ones_row[:, :], 1.0)
            pool.memset(ones_row_bf[:, :], 1.0)
            pool.memset(ones_bf[:, :], 1.0)
            pool.memset(ones_f[:, :], 1.0)
            pool.memset(batch_mask[:, :], 1.0)
            pool.memset(late[:, :], 1.0)
            pool.memset(head_mask[:, :], 1.0)
            link(pool.memset(chunk_mask[:, :], 1.0))
            link(pool.affine_select(out=head_mask[:, :], in_=head_mask[:, :], compare_op=ALU.is_ge, fill=0.0,
                                    base=0, pattern=[[-DK, H]], channel_multiplier=1))
            link(pool.affine_select(out=head_mask[:, :], in_=head_mask[:, :], compare_op=ALU.is_ge, fill=0.0,
                                    base=DK - 1, pattern=[[DK, H]], channel_multiplier=-1))
            link(pool.affine_select(out=chunk_mask[:, :], in_=chunk_mask[:, :], compare_op=ALU.is_ge, fill=0.0,
                                    base=0, pattern=[[-K, HPC]], channel_multiplier=1))
            link(pool.affine_select(out=chunk_mask[:, :], in_=chunk_mask[:, :], compare_op=ALU.is_ge, fill=0.0,
                                    base=K - 1, pattern=[[K, HPC]], channel_multiplier=-1))
            link(pool.affine_select(out=before_bf[:, :], in_=ones_bf[:, :], compare_op=ALU.is_ge, fill=0.0,
                                    base=-1, pattern=[[1, P]], channel_multiplier=-1))
            bm = batch_mask[:, :].rearrange("p (b k) -> p b k", b=B)
            link(pool.affine_select(out=bm, in_=bm, compare_op=ALU.is_ge, fill=0.0,
                                    base=0, pattern=[[-K, B], [0, K]], channel_multiplier=1))
            link(pool.affine_select(out=bm, in_=bm, compare_op=ALU.is_ge, fill=0.0,
                                    base=K - 1, pattern=[[K, B], [0, K]], channel_multiplier=-1))
            link(pool.affine_select(out=late[:, :], in_=late[:, :], compare_op=ALU.is_ge, fill=0.0,
                                    base=-K, pattern=[[0, 1]], channel_multiplier=1))
            pool.iota(part_no[:, :], [[0, 1]], base=0, channel_multiplier=1)
            pool.iota(expert_i[:, :], [[-1, E]], base=E, channel_multiplier=0)
            pool.iota(tile_i[:, :, :], [[1, NT], [0, E]], base=0, channel_multiplier=0).then_inc(const_ready, 1)

            def split(n0, matrices):
                for i, dst in enumerate(matrices):
                    n = n0 + i
                    src = raw[:, n % RAW, 0:dst.shape[2]]
                    pool.wait_ge(in_raw[n % RAW], 16 * (n // RAW + 1))
                    link(pool.tensor_copy(dst[:, 0, :], src))
                    pool.tensor_tensor(dst[:, 1, :], src, dst[:, 0, :].bitcast(F32),
                                       ALU.subtract).then_inc(w_split, 1)

            def scatter(r):
                g = r % GROUPS
                if r == 0:
                    pool.wait_ge(zeroed, 16 * GROUPS)
                pool.wait_ge(routed, r // GROUPS + 1)
                for k in range(TOPK):
                    for j in range(GT):
                        pool.indirect_dma_start(
                            out=xs_dram[g], out_offset=bass.IndirectOffsetOnAxis(ap=slot_i[:, k, g * GT + j:g * GT + j + 1], axis=0),
                            in_=XNR[:, g * GT + j, :], in_offset=None).then_inc(scattered[g], 16)

            def gather(m):
                g = m % GROUPS
                pool.wait_ge(y_stored[g], 16 * NT * (m // GROUPS + 1))
                for k, dst in enumerate((XNR[:, g * GT:(g + 1) * GT, :], YG[:, :, :])):
                    if k and m:
                        pool.wait_ge(combined, m)
                    for j in range(GT):
                        t = g * GT + j
                        pool.indirect_dma_start(
                            out=dst[:, j, :], out_offset=None, in_=ys_dram[g],
                            in_offset=bass.IndirectOffsetOnAxis(ap=slot_i[:, k, t:t + 1], axis=0)).then_inc(gathered[g][k], 16)

            split(0, [w[:, e, :, :] for e in range(E) for w in (WA, WB)])
            split(N_W1, [WC[:, e, :, c:c + 256] for e in range(E) for c in (0, 256)])
            scatter(0)
            scatter(1)
            gather(0)
            gather(1)
            scatter(2)
            scatter(3)
            gather(2)
            gather(3)
            pool.wait_ge(ex_dn, 4 * NT)
            split(N_W3, [WC[:, e, :, :] for e in range(E)])
            pool.wait_ge(x2_added, 1)
            split(N_D3, [WB[:, e, :, :] for e in range(E)])
            pool.wait_ge(f2_added, TILES)
            split(N_U3, [WA[:, e, :, :] for e in range(E)])
            scatter(4)
            scatter(5)
            gather(4)
            gather(5)

        @block.scalar
        def _(act):
            def evac_xt(n):
                for q in range(B):
                    act.wait_ge(xt_mm, B * n + q + 1)
                    act.activation(XT[:, q * BT:(q + 1) * BT, :], bank[4 + q][:, :].rearrange("p (t c) -> p t c", c=P),
                                   ACT.Copy).then_inc(xt_ready, 1)

            def setup(i):
                for b in range(B):
                    act.wait_ge(setup_mm, i * (B + 2) + 2 + b)
                    act.activation(M[:, b, :], bank[1 + b % 2][:, :], ACT.Copy).then_inc(m_evac, 1)

            def attention(a):
                for s in range(TILES + 4):
                    if s < TILES:
                        act.wait_ge(s_sub, a * TILES + s + 1)
                        act.activation(PR[:, s % 2, :], PR[:, s % 2, :], ACT.Exp, scale=float(DK) ** -0.5).then_inc(s_exp, 1)
                    j = s - 1
                    if 0 <= j < TILES:
                        act.wait_ge(pt_mm, a * TILES + j + 1)
                        act.activation(PT[:, j % 2, :, :], bank[2 + j % 2][:, :].rearrange("p (c t) -> p c t", c=HC),
                                       ACT.Copy).then_inc(pt_ready, 1)
                    j = s - 3
                    if 0 <= j < TILES:
                        act.wait_ge(ot_mm, a * TILES + j + 1)
                        act.activation(OT[:, j % 2, :], bank[6][:, 0:P], ACT.Copy).then_inc(ot_ready, 1)

            def router(r):
                act.wait_ge(dl_ready, r + 1)
                act.activation(ex[:, :, :], dl[:, :, :], ACT.Exp)
                act.activation(e2[:, :], de[:, :], ACT.Exp).then_inc(ex_ready, 1)

            def experts(m):
                L = MOE[m // GROUPS]
                f = L["f"]
                nc_f = f // P
                base = m * NT

                def x_high(t, s):
                    act.wait_ge(ex_t, t + base + 1)
                    act.activation(xh[s][:, :], bank[6][:, 0:P], ACT.Copy).then_inc(ex_xh, 1)

                def activate(t, s):
                    act.wait_ge(ex_up, t + base + 1)
                    dst = gb if L["up"] > L["f"] else hb
                    act.activation(dst[s][:, 0:f], bank[s][:, 0:f], L["act"]).then_inc(ex_act, 1)

                def h_high(t, s):
                    act.wait_ge(ex_ht, t + base + 1)
                    act.activation(hh[s][:, 0:nc_f, :], bank[4 + s][:, 0:f].rearrange("p (c t) -> p c t", c=nc_f),
                                   ACT.Copy).then_inc(ex_hh, 1)

                x_high(0, 0)
                x_high(1, 1)
                activate(0, 0)
                x_high(2, 0)
                activate(1, 1)
                h_high(0, 0)
                with act.Fori(0, STEPS // 2) as i:
                    for u in range(2):
                        x_high(2 * i + (u + 3), (u + 1) % 2)
                        activate(2 * i + (u + 2), u % 2)
                        h_high(2 * i + (u + 1), (u + 1) % 2)
                activate(NT - 1, (NT - 1) % 2)
                h_high(NT - 2, (NT - 2) % 2)
                h_high(NT - 1, (NT - 1) % 2)

            def attention1():
                act.wait_ge(a1_sub, 1)
                act.activation(PR[:, 0, :], PR[:, 0, :], ACT.Exp, scale=float(D) ** -0.5).then_inc(a1_exp, 1)
                for b in range(B):
                    act.wait_ge(a1_pt, b + 1)
                    act.activation(PT1[:, b * BT:(b + 1) * BT, :], bank[b % 4][0:K, :].rearrange("p (t c) -> p t c", t=BT),
                                   ACT.Copy).then_inc(a1_ptc, 1)

            def setup2():
                for i, dst in enumerate((kall, vall)):
                    act.wait_ge(s2_mm, i + 1)
                    for c in range(2):
                        act.activation(dst[:, c * 512:(c + 1) * 512], bank[2 + 2 * i + c][:, :], ACT.Copy).then_inc(s2_act, 1)
                act.wait_ge(s2_mm, 3)
                for c in range(2):
                    act.activation(vsum[:, c * 512:(c + 1) * 512], bank[2 + c][:, :], ACT.Copy).then_inc(s2_act, 1)
                act.wait_ge(s2_mm, 4)
                for c in range(2):
                    act.activation(attn2[:, c * 512:(c + 1) * 512], bank[4 + c][:, :], ACT.Copy, scale=1.0 / K).then_inc(s2_act, 1)

            def xattn2():
                act.wait_ge(x2_t, 1)
                act.activation(XL[:, :], bank[6][:, 0:B * K], ACT.Copy).then_inc(x2_xl, 1)
                act.wait_ge(x2_m, 1)
                act.activation(e16[:, :, :], e16[:, :, :], ACT.Exp).then_inc(x2_e, 1)
                for c in range(2):
                    act.wait_ge(x2_ot, c + 1)
                    act.activation(oT[:, c * 4:(c + 1) * 4, :],
                                   bank[2 + c][:, :].rearrange("p (c r) -> p c r", c=4), ACT.Copy).then_inc(x2_otc, 1)
                act.wait_ge(x2_y, 1)
                act.activation(XL[:, :], bank[4][:, 0:B * K], ACT.Copy).then_inc(x2_yc, 1)

            def ffn2():
                def x_high(b):
                    act.wait_ge(f2_xt, b + 1)
                    act.activation(xqh[:, b % 2, 1:S + 1], bank[6][:, :], ACT.Copy).then_inc(f2_xh, 1)

                def hidden(i):
                    act.wait_ge(f2_h, i + 1)
                    if i >= ZBUFS:
                        act.wait_ge(f2_zq, i - ZBUFS + 1)
                    act.activation(Z[:, i % ZBUFS, :], bank[i % 4][:, :], ACT.Silu).then_inc(f2_z, 1)

                def turned(i):
                    act.wait_ge(f2_qt, i + 1)
                    act.activation(zqT[:, i % 2, :, :], bank[4 + i % 2][:, 0:F2 // 2].bitcast(BF16)
                                   .rearrange("p (c t) -> p c t", c=F2C), ACT.Copy).then_inc(f2_qtc, 1)

                x_high(0)
                for p in range(TILES // 2 + 1):
                    if p % 2 == 0 and p // 2 + 1 < B:
                        x_high(p // 2 + 1)
                    if p < TILES // 2:
                        hidden(2 * p)
                        hidden(2 * p + 1)
                    if p:
                        turned(2 * p - 2)
                        turned(2 * p - 1)

            setup(0)
            evac_xt(0)
            attention(0)
            evac_xt(1)
            router(0)
            for g in range(GROUPS):
                experts(g)
            evac_xt(2)
            attention1()
            evac_xt(3)
            router(1)
            setup2()
            for g in range(GROUPS):
                experts(GROUPS + g)
            setup(1)
            xattn2()
            ffn2()
            evac_xt(4)
            attention(1)
            evac_xt(5)
            router(2)
            for g in range(GROUPS):
                experts(2 * GROUPS + g)

        @block.vector
        def _(dve):
            n = [0]

            def link(ins):
                n[0] += 1
                ins.then_inc(dve_chain, 1)
                dve.wait_ge(dve_chain, n[0])

            def layer_norm(tiles, dst, done=None):
                nt = len(tiles)
                for j, t in enumerate(tiles):
                    ins = dve.bn_stats(stats[:, j, :], X[:, t, :])
                link(ins)
                for j in range(nt):
                    ins = dve.bn_aggr(mv[:, j, :], stats[:, j, :])
                link(ins)
                link(dve.tensor_scalar(ve[:, 0:nt], mv[:, 0:nt, 1], EPS, None, ALU.add))
                link(dve.tensor_scalar(ti[:, 0:nt], ve[:, 0:nt].bitcast(I32), 1, None, ALU.logical_shift_right))
                link(dve.tensor_scalar(yi[:, 0:nt], ti[:, 0:nt], -1.0, RSQRT_SEED, ALU.mult, ALU.add))
                y = yi[:, 0:nt].bitcast(F32)
                for k in range(3):
                    link(dve.tensor_tensor(ya[:, 0:nt], y, y, ALU.mult))
                    link(dve.scalar_tensor_tensor(out=yb[:, 0:nt], in0=ve[:, 0:nt], scalar=-0.5, in1=ya[:, 0:nt],
                                                  op0=ALU.mult, op1=ALU.mult))
                    link(dve.scalar_tensor_tensor(out=rstd[:, 0:nt], in0=yb[:, 0:nt], scalar=1.5, in1=y,
                                                  op0=ALU.add, op1=ALU.mult))
                    y = rstd[:, 0:nt]
                for j, t in enumerate(tiles):
                    ins = dve.tensor_scalar(dst[:, j, :], X[:, t, :], mv[:, j, 0:1], rstd[:, j:j + 1],
                                            ALU.subtract, ALU.mult)
                    if done is not None:
                        ins.then_inc(done, 1)
                if done is None:
                    link(ins)

            def half(g):
                return [g * GT + j for j in range(GT)]

            def constants():
                dve.wait_ge(const_ready, 1)
                dve.tensor_copy(prefer[:, :], expert_i[:, :])
                dve.tensor_copy(ident_bf[:, :], ident[:, :])
                link(dve.tensor_copy(tile_no[:, :, :], tile_i[:, :, :]))
                link(dve.memset(inc_a[:, :, :], 0.0))
                link(dve.memset(inc_b[:, :, :], 0.0))
                link(dve.memset(ahead_a[:, :, :, :], 0.0))
                link(dve.memset(ahead_b[:, :, :, :], 0.0))
                link(dve.memset(eid_i[:, :, :], 0))
                dve.wait_ge(in_w0, 16)
                dve.tensor_copy(ctx4[:, :, :, :], ctxT.rearrange("p (b k) -> p b k", b=B).unsqueeze(2)
                                .broadcast_to([P, B, HPC, K])).then_inc(ctx4_ready, 1)
                dve.wait_ge(in_mask0, 16)
                dve.tensor_scalar(mrow, mask0_i[:, :, :].unsqueeze(2).broadcast_to([1, B, H, K]),
                                  0, FILL, ALU.is_equal, ALU.mult).then_inc(mrow_ready, 1)
                dve.tensor_scalar(part_f[:, :], part_no[:, :], 0.0, None, ALU.is_equal)
                link(dve.tensor_copy(sel_f[:, :], ident[0:K, 0:K]))
                link(dve.tensor_scalar(minus_12[:, :], part_f[:, :], 1.0, None, ALU.subtract))
                dve.tensor_scalar(minus_2[:, :], part_no[:, :], 2.0, -1.0, ALU.is_equal, ALU.mult)
                link(dve.tensor_copy(sel[:, :, :], sel_f[:, :].unsqueeze(1).broadcast_to([K, H, K])))

            def split3(dst, src):
                link(dve.tensor_copy(dst, src))
                link(dve.scalar_tensor_tensor(out=src, in0=dst, scalar=minus_12[:, :], in1=src, op0=ALU.mult, op1=ALU.add))
                link(dve.tensor_copy(dst, src))
                link(dve.scalar_tensor_tensor(out=src, in0=dst, scalar=minus_2[:, :], in1=src, op0=ALU.mult, op1=ALU.add))
                return dve.tensor_copy(dst, src)

            def setup(i):
                dve.wait_ge(setup_mm, i * (B + 2) + 1)
                kps = bank[0][:, 0:P].rearrange("p (b k) -> p b k", b=B)
                if i == 0:
                    link(dve.tensor_copy(kT[:, :, :], kps))
                else:
                    dve.wait_ge(y_stored[1], 16 * NT * 2)
                    link(dve.tensor_scalar(kT[:, :, :], kps, bk3, None, ALU.add))
                for b in range(B):
                    dve.tensor_tensor(kbd[:, b, :, :], kT[:, b, :].unsqueeze(1).broadcast_to([P, H, K]),
                                      head_mask[:, :].unsqueeze(2).broadcast_to([P, H, K]), ALU.mult).then_inc(setup_evac, 1)
                if i == 1:
                    for b in range(B):
                        dve.wait_ge(r_mm, b + 1)
                        if b:
                            dve.wait_ge(r_evac, b)
                        link(dve.tensor_copy(rrow[:, :], bank[4 + b % 2][0:3, :]))
                        split3(brow[:, b, :], rrow[:, :]).then_inc(r_evac, 1)
                dve.wait_ge(setup_mm, (i + 1) * (B + 2))
                for b in range(B):
                    v = bank[3][:, b * P:(b + 1) * P].rearrange("p (c h d) -> p c h d", c=HC, h=HPC)
                    dve.tensor_tensor(VB[:, b, :, 0:HPC * DK].rearrange("p c (h d) -> p c h d", h=HPC), v,
                                      chunk_mask[:, :].unsqueeze(1).unsqueeze(3).broadcast_to([P, HC, HPC, DK]), ALU.mult)
                    ins = dve.tensor_copy(VB[:, b, :, HPC * DK:VW], chunk_mask[:, :].unsqueeze(1).broadcast_to([P, HC, HPC]))
                ins.then_inc(setup_evac, 1)

            def attention(a):
                for s in range(TILES + 4):
                    if s < TILES:
                        dve.wait_ge(s_mm, a * TILES + s + 1)
                        sc = bank[s % 2][:, :].rearrange("p (h k) -> p h k", h=H)
                        link(dve.tensor_reduce(smax[:, s % 2, :], sc, AX.X, ALU.max))
                        dve.tensor_tensor(PR[:, s % 2, :].rearrange("p (h k) -> p h k", h=H), sc,
                                          smax[:, s % 2, :].unsqueeze(2).broadcast_to([P, H, K]),
                                          ALU.subtract).then_inc(s_sub, 1)
                    j = s - 2
                    if 0 <= j < TILES:
                        dve.wait_ge(o_mm, a * TILES + j + 1)
                        o = bank[4 + j % 2][:, 0:HC * VW].rearrange("p (c w) -> p c w", c=HC)
                        link(dve.reciprocal(rsum[:, j % 2, :].rearrange("p (c h) -> p c h", c=HC), o[:, :, HPC * DK:VW]))
                        dve.tensor_tensor(ON[:, j % 2, :].rearrange("p (c h d) -> p c h d", c=HC, h=HPC),
                                          o[:, :, 0:HPC * DK].rearrange("p c (h d) -> p c h d", h=HPC),
                                          rsum[:, j % 2, :].rearrange("p (c h) -> p c h", c=HC).unsqueeze(3)
                                          .broadcast_to([P, HC, HPC, DK]), ALU.mult).then_inc(o_norm, 1)
                    j = s - 4
                    if 0 <= j < TILES:
                        dve.wait_ge(wo_mm, a * TILES + j + 1)
                        dve.tensor_tensor(X[:, j, :], X[:, j, :], bank[7][:, 0:D], ALU.add).then_inc(x_added, 1)
                dve.wait_ge(x_added, (a + 1) * TILES)

            def router(r):
                flat, halves = [P, TILES, E], [P, GROUPS, GT, E]

                def by_half(a):
                    return a.rearrange("p (g t) e -> p g t e", g=GROUPS)

                dve.wait_ge(lg_mm, r + 1)
                logits = bank[0][:, 0:TILES * E].rearrange("p (t e) -> p t e", e=E)
                if r == 1:
                    link(dve.tensor_tensor(lg[:, :, :], logits, br_all[:, :].unsqueeze(1).broadcast_to(flat), ALU.add))
                else:
                    link(dve.tensor_copy(lg[:, :, :], logits))
                pref = prefer[:, :].unsqueeze(1).broadcast_to(flat)

                def first_of_max(src, mx, onehot):
                    link(dve.tensor_reduce(mx[:, :], src, AX.X, ALU.max))
                    link(dve.tensor_tensor(cand[:, :, :], src, mx[:, :].unsqueeze(2).broadcast_to(flat), ALU.is_equal))
                    link(dve.tensor_tensor(cand[:, :, :], cand[:, :, :], pref, ALU.mult))
                    link(dve.tensor_reduce(c1[:, :], cand[:, :, :], AX.X, ALU.max))
                    link(dve.tensor_tensor(onehot[:, :, :], cand[:, :, :], c1[:, :].unsqueeze(2).broadcast_to(flat),
                                           ALU.is_equal))

                first_of_max(lg[:, :, :], m1, oh1)
                link(dve.scalar_tensor_tensor(out=second[:, :, :], in0=oh1[:, :, :], scalar=-3.0e38, in1=lg[:, :, :],
                                              op0=ALU.mult, op1=ALU.add))
                first_of_max(second[:, :, :], m2, oh2)
                link(dve.tensor_tensor(both[:, :, :, :], by_half(oh1[:, :, :]), by_half(oh2[:, :, :]), ALU.add))
                link(dve.tensor_tensor(ahead_a[:, :, PAD + 1:, :], both[:, :, 1:, :], both[:, :, 0:GT - 1, :], ALU.add))
                link(dve.tensor_copy(ahead_a[:, :, PAD, :], both[:, :, 0, :]))
                link(dve.tensor_tensor(ahead_b[:, :, PAD:, :], ahead_a[:, :, PAD:, :], ahead_a[:, :, PAD - 2:-2, :], ALU.add))
                dve.tensor_tensor(ahead_a[:, :, PAD:, :], ahead_b[:, :, PAD:, :], ahead_b[:, :, 0:GT, :],
                                  ALU.add).then_inc(both_ready, 1)
                dve.tensor_tensor(dl[:, :, :], lg[:, :, :], m1[:, :].unsqueeze(2).broadcast_to(flat), ALU.subtract)
                dve.tensor_tensor(de[:, :], m2[:, :], m1[:, :], ALU.subtract).then_inc(dl_ready, 1)
                dve.wait_ge(ex_ready, r + 1)
                link(dve.tensor_reduce(es[:, :], ex[:, :, :], AX.X, ALU.add))
                link(dve.reciprocal(pr1[:, :], es[:, :]))
                link(dve.tensor_tensor(pr2[:, :], e2[:, :], pr1[:, :], ALU.mult))
                link(dve.tensor_tensor(den[:, :], pr1[:, :], pr2[:, :], ALU.add))
                link(dve.tensor_scalar(den[:, :], den[:, :], 1e-9, None, ALU.max))
                link(dve.reciprocal(den[:, :], den[:, :]))
                dve.tensor_tensor(gates[:, 0, :], pr1[:, :], den[:, :], ALU.mult)
                link(dve.tensor_tensor(gates[:, 1, :], pr2[:, :], den[:, :], ALU.mult))
                dve.wait_ge(rank_mm, r + 1)
                ranks = TILES * E
                link(dve.tensor_scalar(cnt[:, :, :], bank[1][:, ranks:ranks + GROUPS * E].rearrange("p (g e) -> p g e", g=GROUPS),
                                       1.0 / P, (P - 1) / P - 0.5 + 0.5 / P, ALU.mult, ALU.add))
                link(dve.tensor_scalar(cnt[:, :, :], cnt[:, :, :], ROUND, -ROUND, ALU.add, ALU.add))
                link(dve.tensor_tensor(inc_a[:, :, PAD + 1:], cnt[:, :, 1:E], cnt[:, :, 0:E - 1], ALU.add))
                link(dve.tensor_copy(inc_a[:, :, PAD:PAD + 1], cnt[:, :, 0:1]))
                link(dve.tensor_tensor(inc_b[:, :, PAD:], inc_a[:, :, PAD:], inc_a[:, :, PAD - 2:-2], ALU.add))
                link(dve.tensor_tensor(inc_a[:, :, PAD:], inc_b[:, :, PAD:], inc_b[:, :, 0:E], ALU.add))
                link(dve.tensor_tensor(start_f[:, :, :], inc_a[:, :, PAD:], cnt[:, :, :], ALU.subtract))
                link(dve.tensor_scalar(start_f[:, :, :], start_f[:, :, :], float(P), None, ALU.mult))
                link(dve.tensor_tensor(by_half(place[:, :, :]), by_half(bank[1][:, 0:ranks].rearrange("p (t e) -> p t e", e=E)),
                                       start_f[:, :, :].unsqueeze(2).broadcast_to(halves), ALU.add))
                for k, oh in enumerate((oh1, oh2)):
                    link(dve.tensor_tensor(pick[:, :, :], place[:, :, :], oh[:, :, :], ALU.mult))
                    link(dve.tensor_reduce(slot_f[:, k, :], pick[:, :, :], AX.X, ALU.add))
                link(dve.tensor_copy(slot_i[:, :, :], slot_f[:, :, :]))
                tiles = [1, GROUPS, NT, E]
                link(dve.tensor_tensor(le[:, :, :, :], tile_no[:, :, :].unsqueeze(1).broadcast_to(tiles),
                                       inc_a[0:1, :, PAD:].unsqueeze(2).broadcast_to(tiles), ALU.is_ge))
                link(dve.tensor_reduce(eid_f[:, :, :], le[:, :, :, :], AX.X, ALU.add))
                link(dve.tensor_scalar(eid_c[:, :, :], eid_f[:, :, :], float(E - 1), None, ALU.min))
                dve.tensor_copy(eid_i[:, :, 0:NT], eid_c[:, :, :]).then_inc(routed, 1)
                dve.wait_ge(routed, r + 1)

            def experts(m):
                L = MOE[m // GROUPS]
                f = L["f"]
                nc_f = f // P
                base = m * NT

                def x_low(t, s):
                    dve.wait_ge(ex_xh, t + base + 1)
                    dve.tensor_tensor(xl[s][:, :], bank[6][:, 0:P], xh[s][:, :].bitcast(F32), ALU.subtract).then_inc(ex_xl, 1)

                def multiply(t, s):
                    if L["up"] > f:
                        dve.wait_ge(ex_act, t + base + 1)
                        dve.tensor_tensor(hb[s][:, :], gb[s][:, :], bank[2 + s][:, :], ALU.mult).then_inc(ex_mul, 1)

                def h_low(t, s):
                    dve.wait_ge(ex_hh, t + base + 1)
                    dve.tensor_tensor(hl[s][:, 0:nc_f, :], bank[4 + s][:, 0:f].rearrange("p (c t) -> p c t", c=nc_f),
                                      hh[s][:, 0:nc_f, :].bitcast(F32), ALU.subtract).then_inc(ex_hl, 1)

                def y_copy(t):
                    dve.wait_ge(ex_dn, t + base + 1)
                    dve.tensor_reduce(Y[:, bass.ds(t, 1), :].rearrange("p a d -> p (a d)"),
                                      bank[7][:, 0:2 * D].rearrange("p (k d) -> p d k", k=2), AX.X, ALU.add).then_inc(ex_y, 1)

                if m:
                    dve.wait_ge(y_stored[(m - 1) % GROUPS], 16 * NT * ((m - 1) // GROUPS + 1))
                x_low(0, 0)
                x_low(1, 1)
                multiply(0, 0)
                x_low(2, 0)
                multiply(1, 1)
                h_low(0, 0)
                with dve.Fori(0, STEPS // 2) as i:
                    for u in range(2):
                        x_low(2 * i + (u + 3), (u + 1) % 2)
                        multiply(2 * i + (u + 2), u % 2)
                        h_low(2 * i + (u + 1), (u + 1) % 2)
                        y_copy(2 * i + u)
                multiply(NT - 1, (NT - 1) % 2)
                h_low(NT - 2, (NT - 2) % 2)
                y_copy(NT - 3)
                h_low(NT - 1, (NT - 1) % 2)
                y_copy(NT - 2)
                y_copy(NT - 1)

            def combine(m):
                g = m % GROUPS
                for k, src in enumerate((XNR[:, g * GT:(g + 1) * GT, :], YG[:, :, :])):
                    dve.wait_ge(gathered[g][k], 16 * GT * (m // GROUPS + 1))
                    for j in range(GT):
                        t = g * GT + j
                        ins = dve.scalar_tensor_tensor(out=X[:, t, :], in0=src[:, j, :], scalar=gates[:, k, t:t + 1],
                                                       in1=X[:, t, :], op0=ALU.mult, op1=ALU.add)
                    if k < TOPK - 1:
                        link(ins)
                ins.then_inc(combined, 1)
                dve.wait_ge(combined, m + 1)

            def setup1():
                dve.wait_ge(in_col, 16)
                dve.wait_ge(s1_mm, 1)
                dve.tensor_scalar(kT[:, :, :], bank[2][:, 0:P].rearrange("p (b k) -> p b k", b=B), bk1, None,
                                  ALU.add).then_inc(s1_evac, 1)
                dve.wait_ge(s1_mm, 4)
                dve.tensor_copy(M1[:, :, :], bank[4][:, 0:P].rearrange("p (b k) -> p b k", b=B))
                dve.tensor_copy(br_all[:, :], bank[5][:, P:P + E])
                dve.tensor_copy(r1[:, :, :], bank[5][:, 0:P].rearrange("p (b k) -> p b k", b=B))
                link(dve.tensor_copy(V1[:, :, :], bank[3][0:K, :].rearrange("p (b d) -> p b d", b=B)))
                dve.wait_ge(in_b1, 48)
                link(split3(bias1[:, :, :], bias1_raw[:, :, :]))
                dve.wait_ge(in_b2, 48)
                split3(bias2[:, :, :], YG[0:3, :, :]).then_inc(s1_evac, 1)

            def attention1():
                sc = PR[:, 0, :].rearrange("p (t k) -> p t k", k=K)
                pr = PR[:, 1, :].rearrange("p (t k) -> p t k", k=K)
                dve.wait_ge(a1_s, 1)
                link(dve.tensor_tensor(PR[:, 1, :].rearrange("p (b t k) -> p b t k", b=B, t=BT),
                                       bank[0][:, :].rearrange("p (b t k) -> p b t k", b=B, t=BT),
                                       r1[:, :, :].unsqueeze(2).broadcast_to([P, B, BT, K]), ALU.add))
                link(dve.tensor_reduce(m1[:, :], pr, AX.X, ALU.max))
                dve.tensor_tensor(sc, pr, m1[:, :].unsqueeze(2).broadcast_to([P, TILES, K]), ALU.subtract).then_inc(a1_sub, 1)
                dve.wait_ge(a1_exp, 1)
                link(dve.tensor_reduce(es[:, :], sc, AX.X, ALU.add))
                link(dve.reciprocal(es[:, :], es[:, :]))
                dve.tensor_tensor(pr, sc, es[:, :].unsqueeze(2).broadcast_to([P, TILES, K]), ALU.mult).then_inc(a1_p, 1)
                for b in range(B):
                    dve.wait_ge(a1_o, b + 1)
                    xv = X[:, b * BT:(b + 1) * BT, :]
                    dve.tensor_tensor(xv, xv, bank[4 + b][:, :].rearrange("p (t d) -> p t d", d=D), ALU.add).then_inc(a1_added, 1)
                dve.wait_ge(a1_added, B)

            def setup2():
                dve.wait_ge(s2_mm, 5)
                link(dve.tensor_copy(vo[:, :], bank[2][:, 0:D]))
                dve.sem_inc(s2_evac, 1)
                dve.wait_ge(s2_mm, 6)
                dve.tensor_copy(U[:, :, :], bank[3][:, :].rearrange("p (b d) -> p b d", b=B)).then_inc(s2_evac, 1)

            def xattn2():
                layer_norm([b * BT for b in range(B)], XNR[:, 0:B, :], x2_n)
                dve.wait_ge(x2_q, 1)
                for c in range(2):
                    ins = dve.tensor_tensor(kq[:, c * 512:(c + 1) * 512], kall[:, c * 512:(c + 1) * 512], bank[c][:, :], ALU.mult)
                link(ins)
                link(dve.tensor_reduce(s16[:, :], kq.rearrange("p (h d) -> p h d", h=HL), AX.X, ALU.add))
                link(dve.tensor_scalar(s16[:, :], s16[:, :], float(DL) ** -0.5, None, ALU.mult))
                link(dve.tensor_scalar(m16[:, :], s16[:, :], NEG, None, ALU.max))
                dve.tensor_tensor(e16[:, 0, :], s16[:, :], m16[:, :], ALU.subtract)
                dve.tensor_scalar(e16[:, 1, :], m16[:, :], -1.0, NEG, ALU.mult, ALU.add).then_inc(x2_m, 1)
                dve.wait_ge(x2_e, 1)
                link(dve.scalar_tensor_tensor(out=sum16[:, :], in0=e16[:, 1, :], scalar=float(K - 1),
                                              in1=e16[:, 0, :], op0=ALU.mult, op1=ALU.add))
                link(dve.reciprocal(sum16[:, :], sum16[:, :]))
                link(dve.tensor_tensor(e16[:, :, :], e16[:, :, :],
                                       sum16[:, :].unsqueeze(1).broadcast_to([P, 2, HL]), ALU.mult))
                link(dve.tensor_tensor(s16[:, :], e16[:, 0, :], e16[:, 1, :], ALU.subtract))

                def heads(a):
                    return a.rearrange("p (h d) -> p h d", h=HL)

                dve.tensor_tensor(heads(attn2[:, :]), heads(vall[:, :]),
                                  s16[:, :].unsqueeze(2).broadcast_to([P, HL, DL]), ALU.mult)
                link(dve.tensor_tensor(heads(kq), heads(vsum[:, :]),
                                       e16[:, 1, :].unsqueeze(2).broadcast_to([P, HL, DL]), ALU.mult))
                dve.tensor_tensor(attn2[:, :], attn2[:, :], kq, ALU.add).then_inc(x2_o, 1)
                for b in range(B):
                    t = b * BT
                    dve.tensor_tensor(X[:, t + 1:t + BT, :], X[:, t + 1:t + BT, :],
                                      U[:, b, :].unsqueeze(1).broadcast_to([P, BT - 1, D]), ALU.add)
                    ins = dve.scalar_tensor_tensor(out=X[:, t, :], in0=U[:, b, :], scalar=late[:, :], in1=X[:, t, :],
                                                   op0=ALU.mult, op1=ALU.add)
                link(ins)
                dve.wait_ge(x2_mm, 1)
                xv = X[0:K, :, :].rearrange("p (b t) d -> p b t d", b=B)[:, :, 0, :]
                dve.tensor_tensor(xv, xv, bank[5][0:K, :].rearrange("p (b d) -> p b d", b=B), ALU.add).then_inc(x2_added, 1)
                dve.wait_ge(x2_added, 1)

            def setup_ffn2():
                dve.wait_ge(in_ff2, 96)
                dve.tensor_reduce(wmean[:, 0, 0:1], w1_s[:, :], AX.X, ALU.add, apply_absolute_value=True)
                dve.tensor_reduce(wmean[:, 0, 1:2], w2_s[:, :, :], AX.XY, ALU.add, apply_absolute_value=True).then_inc(fs_sum, 1)
                dve.wait_ge(fs_mm, 1)
                mean, scale = wmean[:, 1, 0:2], wmean[:, 1, 2:4]
                link(dve.tensor_scalar(mean, bank[5][:, 0:2], 1.0 / (D * F2), 1e-5, ALU.mult, ALU.max))
                link(dve.reciprocal(scale, mean))
                w2v = w2_s[:, :, :]
                link(dve.tensor_scalar(w1_s[:, :], w1_s[:, :], scale[:, 0:1], ROUND, ALU.mult, ALU.add))
                link(dve.tensor_scalar(w1_s[:, :], w1_s[:, :], ROUND, 1.0, ALU.subtract, ALU.min))
                link(dve.tensor_scalar(w1_s[:, :], w1_s[:, :], -1.0, mean[:, 0:1], ALU.max, ALU.mult))
                link(dve.tensor_scalar(w2v, w2v, scale[:, 1:2], ROUND, ALU.mult, ALU.add))
                link(dve.tensor_scalar(w2v, w2v, ROUND, 1.0, ALU.subtract, ALU.min))
                link(dve.tensor_scalar(w2q[:, :, :], w2v, -1.0, None, ALU.max))
                for j in range(TAPS):
                    link(dve.tensor_tensor(Z[:, j, :], w1_s[:, :], bank[2 + j][:, :], ALU.mult))
                link(dve.tensor_copy(w1c_h[:, :, :], Z[:, 0:TAPS, :]))
                dve.tensor_tensor(w1c_l[:, :, :], Z[:, 0:TAPS, :], w1c_h[:, :, :].bitcast(F32), ALU.subtract)
                split3(cb[:, :], cb_raw[:, :]).then_inc(fs_ready, 1)

            def ffn2():
                for t in (xqh, xql):
                    dve.memset(t[:, :, 0:1].bitcast(F32), 0.0)
                    dve.memset(t[:, :, S + 1:S + 2].bitcast(F32), 0.0)

                def quantise_x(g):
                    tiles = half(g)
                    xq = XQ[:, g * GT:(g + 1) * GT, :]
                    layer_norm(tiles, xq)
                    link(dve.tensor_reduce(amax[:, :], xq, AX.X, ALU.max, apply_absolute_value=True))
                    link(dve.tensor_scalar(amax[:, :], amax[:, :], 1e-5, None, ALU.max))
                    link(dve.reciprocal(qscale[:, :], amax[:, :]))
                    dve.tensor_scalar(qinv[:, :], amax[:, :], 1.0 / 127.0, None, ALU.mult)
                    link(dve.tensor_scalar(qscale[:, :], qscale[:, :], 127.0, None, ALU.mult))
                    for j in range(GT):
                        ins = dve.tensor_scalar(xq[:, j, :], xq[:, j, :], qscale[:, j:j + 1], ROUND, ALU.mult, ALU.add)
                    link(ins)
                    for j in range(GT):
                        dve.tensor_scalar(xq[:, j, :], xq[:, j, :], ROUND, qinv[:, j:j + 1], ALU.subtract,
                                          ALU.mult).then_inc(f2_xq, 1)

                def x_low(b):
                    dve.wait_ge(f2_xh, b + 1)
                    dve.tensor_tensor(xql[:, b % 2, 1:S + 1], bank[6][:, :], xqh[:, b % 2, 1:S + 1].bitcast(F32),
                                      ALU.subtract).then_inc(f2_xl, 1)

                def quantise(p):
                    dve.wait_ge(f2_z, 2 * p + 2)
                    z = Z[:, 2 * p % ZBUFS:2 * p % ZBUFS + 2, :]
                    link(dve.tensor_reduce(zmax[:, :], z, AX.X, ALU.max, apply_absolute_value=True))
                    link(dve.tensor_scalar(zmax[:, :], zmax[:, :], 1e-5, None, ALU.max))
                    link(dve.reciprocal(zscale[:, :], zmax[:, :]))
                    dve.tensor_scalar(zinv[:, 2 * p:2 * p + 2], zmax[:, :], 1.0 / 127.0, wmean[:, 1, 1:2], ALU.mult, ALU.mult)
                    link(dve.tensor_scalar(zscale[:, :], zscale[:, :], 127.0, None, ALU.mult))
                    for i in range(2):
                        ins = dve.tensor_scalar(z[:, i, :], z[:, i, :], zscale[:, i:i + 1], ROUND, ALU.mult, ALU.add)
                    link(ins)
                    if p:
                        dve.wait_ge(f2_qt, 2 * p)
                    for i in range(2):
                        dve.tensor_scalar(zq[:, i, :], z[:, i, :], ROUND, 127.0, ALU.subtract, ALU.min).then_inc(f2_zq, 1)

                def add(p):
                    dve.wait_ge(f2_dn, p + 1)
                    for i in (2 * p, 2 * p + 1):
                        dve.scalar_tensor_tensor(out=X[:, i, :], in0=bank[7][:, i % 2 * D:(i % 2 + 1) * D], scalar=zinv[:, i:i + 1],
                                                 in1=X[:, i, :], op0=ALU.mult, op1=ALU.add).then_inc(f2_added, 1)

                quantise_x(0)
                x_low(0)
                quantise_x(1)
                for p in range(TILES // 2 + 2):
                    if p % 2 == 0 and p // 2 + 1 < B:
                        x_low(p // 2 + 1)
                    if p >= 2:
                        add(p - 2)
                    if p < TILES // 2:
                        quantise(p)
                dve.wait_ge(f2_added, TILES)

            everything = list(range(TILES))
            constants()
            setup(0)
            for g in range(GROUPS):
                dve.wait_ge(in_x[g], 16)
                layer_norm(half(g), XNR[:, g * GT:(g + 1) * GT, :], xn_ready)
            attention(0)
            layer_norm(everything, XNR[:, :, :], xn_ready)
            router(0)
            setup1()
            for g in range(GROUPS):
                experts(g)
            for g in range(GROUPS):
                combine(g)
                layer_norm(half(g), XNR[:, g * GT:(g + 1) * GT, :], xn_ready)
            attention1()
            layer_norm(everything, XNR[:, :, :], xn_ready)
            router(1)
            setup2()
            setup_ffn2()
            for g in range(GROUPS):
                experts(GROUPS + g)
            combine(GROUPS)
            setup(1)
            combine(GROUPS + 1)
            xattn2()
            ffn2()
            dve.wait_ge(in_mask3, 16)
            link(dve.tensor_scalar(mfill[:, :], mask3_i, 0, FILL, ALU.is_equal, ALU.mult))
            dve.sem_inc(mrow_ready, 1)
            layer_norm(everything, XNR[:, :, :], xn_ready)
            attention(1)
            layer_norm(everything, XNR[:, :, :], xn_ready)
            router(2)
            for g in range(GROUPS):
                experts(2 * GROUPS + g)
            for g in range(GROUPS):
                combine(2 * GROUPS + g)

        @block.tensor
        def _(pe):
            def setup(i, wk, wq, wv):
                mm, ev = i * (B + 2), i * (B + 1)
                pe.matmul(bank[0][:, 0:P], wk, ctxT, start=True, stop=True).then_inc(setup_mm, 1)
                for b in range(B):
                    keys = kbd[:, b, :, :].rearrange("p h k -> p (h k)")
                    pe.wait_ge(setup_evac, ev + b + 1)
                    if b >= 2:
                        pe.wait_ge(m_evac, i * B + b - 1)
                    pe.matmul(bank[1 + b % 2][:, :], wq, keys, start=True, stop=True).then_inc(setup_mm, 1)
                    if i:
                        if b >= 2:
                            pe.wait_ge(r_evac, b - 1)
                        pe.matmul(bank[4 + b % 2][0:3, :], bq3.broadcast_to([P, 3]), keys, start=True, stop=True).then_inc(r_mm, 1)
                pe.wait_ge(ctx4_ready, 1)
                for b in range(B):
                    dst = bank[3][:, b * P:(b + 1) * P]
                    ins = pe.matmul(dst, ctx4[:, b, :, :].rearrange("p h k -> p (h k)"), wv, start=True, stop=(i == 0))
                    if i:
                        ins = pe.matmul(dst, ones_row[:, :], bv3, start=False, stop=True)
                ins.then_inc(setup_mm, 1)
                pe.wait_ge(setup_evac, ev + B + 1)
                pe.wait_ge(m_evac, (i + 1) * B)

            def setup1():
                pe.wait_ge(in_w1, 16)
                pe.wait_ge(in_col, 16)
                pe.wait_ge(in_row, 16)
                pe.matmul(bank[2][:, 0:P], wk1, ctxT, start=True, stop=True).then_inc(s1_mm, 1)
                pe.wait_ge(s1_evac, 1)
                keys = kT[:, :, :].rearrange("p b k -> p (b k)")
                pe.matmul(bank[4][:, 0:P], wq1, keys, start=True, stop=True).then_inc(s1_mm, 1)
                pe.matmul(bank[5][:, 0:P], bq1.broadcast_to([P, P]), keys, start=True, stop=True)
                pe.matmul(bank[5][:, P:P + E], ones_row[:, :], br1, start=True, stop=True).then_inc(s1_mm, 1)
                for b in range(B):
                    dst = bank[3][0:K, b * D:(b + 1) * D]
                    pe.matmul(dst, ctxT[:, b * K:(b + 1) * K], wv1, start=True, stop=False)
                    ins = pe.matmul(dst, ones_row[:, 0:K], bv1, start=False, stop=True)
                ins.then_inc(s1_mm, 1)

            def attention1(n):
                for j in range(TILES):
                    b = j // BT
                    pe.wait_ge(xt_ready, B * n + b + 1)
                    ins = pe.matmul(bank[0][:, j * K:(j + 1) * K], XT[:, j, :], M1[:, b, :], start=True, stop=True)
                ins.then_inc(a1_s, 1)
                pe.wait_ge(a1_p, 1)
                for b in range(B):
                    for j in range(BT):
                        t = b * BT + j
                        ins = pe.transpose(bank[b % 4][0:K, j * P:(j + 1) * P], PR[:, 1, t * K:(t + 1) * K], ident[:, :])
                    ins.then_inc(a1_pt, 1)
                for b in range(B):
                    pe.wait_ge(a1_ptc, b + 1)
                    for j in range(BT):
                        ins = pe.matmul(bank[4 + b][:, j * D:(j + 1) * D], PT1[:, b * BT + j, :], V1[:, b, :],
                                        start=True, stop=True)
                    ins.then_inc(a1_o, 1)

            def setup2():
                pe.wait_ge(in_l2, 48)
                for i in range(2):
                    for c in range(2):
                        ins = pe.matmul(bank[2 + 2 * i + c][:, :], ctxT, wkv_s[:, i * INNER + c * 512:i * INNER + (c + 1) * 512],
                                        start=True, stop=True)
                    ins.then_inc(s2_mm, 1)
                for c in range(2):
                    pe.wait_ge(s2_act, 3 + c)
                    ins = pe.matmul(bank[2 + c][:, :], batch_mask[:, :], vall[:, c * 512:(c + 1) * 512], start=True, stop=True)
                ins.then_inc(s2_mm, 1)
                for c in range(IC):
                    pe.wait_ge(s2_act, 5 + c // 4)
                    ins = pe.transpose(bank[4 + c // 4][:, c % 4 * P:(c % 4 + 1) * P], vsum[:, c * P:(c + 1) * P], ident[:, :])
                ins.then_inc(s2_mm, 1)
                for c in range(IC):
                    pe.wait_ge(s2_act, 7 + c // 4)
                    ins = pe.matmul(bank[2][:, 0:D], attn2[:, c * P:(c + 1) * P], wout_s[:, c, :], start=(c == 0), stop=(c == IC - 1))
                ins.then_inc(s2_mm, 1)
                pe.wait_ge(s2_evac, 1)
                for b in range(B):
                    dst = bank[3][:, b * D:(b + 1) * D]
                    pe.matmul(dst, ident[:, b * K:b * K + 1].broadcast_to([P, P]), vo[:, :], start=True, stop=False)
                    ins = pe.matmul(dst, ones_row[:, :], bout2, start=False, stop=True)
                ins.then_inc(s2_mm, 1)
                pe.wait_ge(s2_evac, 2)

            def xattn2():
                for b in range(B):
                    pe.wait_ge(x2_n, b + 1)
                    ins = pe.transpose(bank[6][:, b * K:(b + 1) * K], XNR[0:K, b, :], ident[0:K, 0:K])
                ins.then_inc(x2_t, 1)
                pe.wait_ge(x2_xl, 1)
                for c in range(2):
                    ins = pe.matmul(bank[c][:, :], XL[:, :], wq_s[:, c * 512:(c + 1) * 512], start=True, stop=True)
                ins.then_inc(x2_q, 1)
                pe.wait_ge(x2_o, 1)
                for c in range(IC):
                    ins = pe.transpose(bank[2 + c // 4][:, c % 4 * P:(c % 4 + 1) * P], attn2[:, c * P:(c + 1) * P], ident[:, :])
                    if c % 4 == 3:
                        ins.then_inc(x2_ot, 1)
                dst = bank[4][:, 0:B * K]
                for c in range(IC):
                    pe.wait_ge(x2_otc, c // 4 + 1)
                    pe.matmul(dst, wout_s[:, c, :], oT[:, c, :], start=(c == 0), stop=False)
                pe.matmul(dst, bout2, ones_row[:, :], start=False, stop=True).then_inc(x2_y, 1)
                pe.wait_ge(x2_yc, 1)
                for b in range(B):
                    ins = pe.transpose(bank[5][0:K, b * D:(b + 1) * D], XL[:, b * K:(b + 1) * K], ident[:, :])
                ins.then_inc(x2_mm, 1)

            def setup_ffn2():
                pe.wait_ge(in_ff2, 96)
                pe.wait_ge(fs_sum, 1)
                for j in range(TAPS):
                    pe.matmul(bank[2 + j][:, :], ident[0:TAPS, j:j + 1].broadcast_to([TAPS, P]), cw_s[:, :], start=True, stop=True)
                pe.matmul(bank[5][:, 0:2], ones_f[:, :], wmean[:, 0, 0:2], start=True, stop=True).then_inc(fs_mm, 1)
                pe.wait_ge(fs_ready, 1)

            def ffn2():
                def turn_x(b):
                    if b:
                        pe.wait_ge(f2_xl, b)
                    for j in range(BT):
                        pe.wait_ge(f2_xq, b * BT + j + 1)
                        ins = pe.transpose(bank[6][:, j * P:(j + 1) * P], XQ[:, b * BT + j, :], ident[:, :])
                    ins.then_inc(f2_xt, 1)

                def up(i):
                    b, at = i // BT, i % BT * P
                    pe.wait_ge(f2_xl, b + 1)
                    if i >= 4:
                        pe.wait_ge(f2_z, i - 3)
                    dst = bank[i % 4][:, :]
                    for j in range(TAPS):
                        for k, (v, w) in enumerate(((xqh, w1c_h), (xqh, w1c_l), (xql, w1c_h))):
                            pe.matmul(dst, v[:, b % 2, at + j:at + j + P], w[:, j, :], start=(j == 0 and k == 0), stop=False)
                    pe.matmul(dst, ones_bf[0:3, :], cb[:, :], start=False, stop=True).then_inc(f2_h, 1)

                def turn(i):
                    pe.wait_ge(f2_zq, i + 1)
                    if i >= 2:
                        pe.wait_ge(f2_qtc, i - 1)
                    zb = bank[4 + i % 2][:, 0:F2 // 2].bitcast(BF16)
                    for c in range(F2C):
                        ins = pe.transpose(zb[:, c * P:(c + 1) * P], zq[:, i % 2, c * P:(c + 1) * P], ident_bf[:, :])
                    ins.then_inc(f2_qt, 1)

                def down(p):
                    if p:
                        pe.wait_ge(f2_added, 2 * p)
                    for i in (2 * p, 2 * p + 1):
                        pe.wait_ge(f2_qtc, i + 1)
                        for c in range(F2C):
                            ins = pe.matmul(bank[7][:, i % 2 * D:(i % 2 + 1) * D], zqT[:, i % 2, c, :], w2q[:, c, :],
                                            start=(c == 0), stop=(c == F2C - 1))
                    ins.then_inc(f2_dn, 1)

                turn_x(0)
                for p in range(TILES // 2 + 2):
                    if p % 2 == 0 and p // 2 + 1 < B:
                        turn_x(p // 2 + 1)
                    if p < TILES // 2:
                        up(2 * p)
                    if p >= 2:
                        down(p - 2)
                    if p < TILES // 2:
                        up(2 * p + 1)
                    if 1 <= p <= TILES // 2:
                        turn(2 * p - 2)
                        turn(2 * p - 1)

            def transposes(n):
                for q in range(B):
                    for j in range(BT):
                        pe.wait_ge(xn_ready, n * TILES + q * BT + j + 1)
                        ins = pe.transpose(bank[4 + q][:, j * P:(j + 1) * P], XNR[:, q * BT + j, :], ident[:, :])
                    ins.then_inc(xt_mm, 1)

            def attention(a, n):
                def tokens_out(q):
                    pe.wait_ge(xt_ready, B * n + q + 1)

                def scores(s):
                    b = s // BT
                    tokens_out(b)
                    if s >= 2:
                        pe.wait_ge(s_sub, a * TILES + s - 1)
                    pe.matmul(bank[s % 2][:, :], XT[:, s, :], M[:, b, :], start=True, stop=False)
                    if a == 0:
                        ins = pe.matmul(bank[s % 2][:, :], ones_row_bf[:, :], mrow[:, b, :, :].rearrange("p h k -> p (h k)"),
                                        start=False, stop=True)
                    else:
                        pe.matmul(bank[s % 2][:, :], ones_bf[0:3, :], brow[:, b, :], start=False, stop=False)
                        ins = pe.matmul(bank[s % 2][:, :], mfill[:, s * P:(s + 1) * P], sel[:, :, :].rearrange("p h k -> p (h k)"),
                                        start=False, stop=True)
                    ins.then_inc(s_mm, 1)

                scores(0)
                for s in range(TILES + 5):
                    j = s - 1
                    if 0 <= j < TILES:
                        pe.wait_ge(s_exp, a * TILES + j + 1)
                        if j >= 2:
                            pe.wait_ge(pt_ready, a * TILES + j - 1)
                        for c in range(HC):
                            ins = pe.transpose(bank[2 + j % 2][:, c * P:(c + 1) * P], PR[:, j % 2, c * P:(c + 1) * P], ident[:, :])
                        ins.then_inc(pt_mm, 1)
                    j = s - 2
                    if 0 <= j < TILES:
                        b = j // BT
                        pe.wait_ge(pt_ready, a * TILES + j + 1)
                        if j < 2:
                            tokens_out(j)
                        else:
                            pe.wait_ge(o_norm, a * TILES + j - 1)
                        for c in range(HC):
                            ins = pe.matmul(bank[4 + j % 2][:, c * VW:(c + 1) * VW], PT[:, j % 2, c, :], VB[:, b, c, :],
                                            start=True, stop=True)
                        ins.then_inc(o_mm, 1)
                    if s + 1 < TILES:
                        scores(s + 1)
                    j = s - 3
                    if 0 <= j < TILES:
                        pe.wait_ge(o_norm, a * TILES + j + 1)
                        if j:
                            pe.wait_ge(ot_ready, a * TILES + j)
                        else:
                            tokens_out(2)
                        pe.transpose(bank[6][:, 0:P], ON[:, j % 2, :], ident[:, :]).then_inc(ot_mm, 1)
                    j = s - 4
                    if 0 <= j < TILES:
                        pe.wait_ge(ot_ready, a * TILES + j + 1)
                        if j:
                            pe.wait_ge(x_added, a * TILES + j)
                        else:
                            tokens_out(3)
                        if a == 0:
                            ins = pe.matmul(bank[7][:, 0:D], OT[:, j % 2, :], wo0, start=True, stop=True)
                        else:
                            pe.matmul(bank[7][:, 0:D], OT[:, j % 2, :], wo3, start=True, stop=False)
                            ins = pe.matmul(bank[7][:, 0:D], ones_row[:, :], bo3, start=False, stop=True)
                        ins.then_inc(wo_mm, 1)

            def router(r, n, gate_w):
                for j in range(TILES):
                    pe.wait_ge(xt_ready, B * n + j // BT + 1)
                    ins = pe.matmul(bank[0][:, j * E:(j + 1) * E], XT[:, j, :], gate_w, start=True, stop=True)
                ins.then_inc(lg_mm, 1)
                pe.wait_ge(both_ready, r + 1)
                rank = bank[1][:, 0:TILES * E]
                pe.matmul(rank, before_bf[:, :], both[:, :, :, :].rearrange("p g t e -> p (g t e)"), start=True, stop=False)
                pe.matmul(rank.rearrange("p (g t e) -> p g t e", g=GROUPS, t=GT), ones_bf[:, :],
                          ahead_a[:, :, PAD - 1:-1, :], start=False, stop=True)
                pe.matmul(bank[1][:, TILES * E:(TILES + GROUPS) * E].rearrange("p (g e) -> p g e", g=GROUPS), ones_bf[:, :],
                          ahead_a[:, :, PAD + GT - 1, :], start=True, stop=True).then_inc(rank_mm, 1)

            def experts(m, up, dn):
                L = MOE[m // GROUPS]
                f, fu = L["f"], L["up"]
                nc_f = f // P
                g = m % GROUPS
                base = m * NT
                per_ring = [(NT - s + RING - 1) // RING for s in range(RING)]

                def tr_x(t, s4, round_):
                    pe.wait_ge(x_loaded[s4], 16 * (m * per_ring[s4]) + 16 * (round_ + 1))
                    if m or not isinstance(t, int) or t:
                        pe.wait_ge(ex_xl, t + base)
                    pe.transpose(bank[6][:, 0:P], xrow[s4][:, :], ident[:, :]).then_inc(ex_t, 1)

                def up_mm(t, s, e):
                    pe.wait_ge(ex_xl, t + base + 1)
                    for k in range(fu // f):
                        wh, wl = (up[k][:, bass.ds(e, 1), i, 0:f].rearrange("p a f -> p (a f)") for i in range(2))
                        dst = bank[2 * k + s][:, 0:f]
                        pe.matmul(dst, xh[s][:, :], wh, start=True, stop=False)
                        pe.matmul(dst, xh[s][:, :], wl, start=False, stop=False)
                        ins = pe.matmul(dst, xl[s][:, :], wh, start=False, stop=not L["bias"])
                        if L["bias"]:
                            ins = pe.matmul(dst, ones_bf[0:3, :], bias1[:, bass.ds(e, 1), :].rearrange("p a f -> p (a f)"),
                                            start=False, stop=True)
                    ins.then_inc(ex_up, 1)

                def tr_h(t, s):
                    if fu > f:
                        pe.wait_ge(ex_mul, t + (m % GROUPS * NT + 1))
                    else:
                        pe.wait_ge(ex_act, t + base + 1)
                    for c in range(nc_f):
                        ins = pe.transpose(bank[4 + s][:, c * P:(c + 1) * P], hb[s][:, c * P:(c + 1) * P], ident[:, :])
                    ins.then_inc(ex_ht, 1)

                def dn_mm(t, s, e):
                    pe.wait_ge(ex_hl, t + base + 1)
                    if m or not isinstance(t, int) or t:
                        pe.wait_ge(ex_y, t + base)
                    y = bank[7][:, 0:2 * D]
                    for c in range(nc_f):
                        w = dn[:, bass.ds(e, 1), :, c * P:(c + 1) * P].rearrange("p a k d -> p (a k) d")
                        pe.matmul(y, hh[s][:, c, :], w, start=(c == 0), stop=False, skip_group_check=True)
                        ins = pe.matmul(y, hl[s][:, c, :], w, start=False, stop=(c == nc_f - 1), skip_group_check=True)
                    if L["bias"]:
                        ins = pe.matmul(bank[7][:, 0:D], ones_bf[0:3, :], bias2[:, bass.ds(e, 1), :].rearrange("p a f -> p (a f)"),
                                        start=False, stop=True, skip_group_check=True)
                    ins.then_inc(ex_dn, 1)

                def experts_of(t, count):
                    _, values = nc.values_load_multi_w_load_instructions(
                        eid_i[0:1, g, bass.ds(t, count)], engines=[mybir.EngineType.PE], min_val=0, max_val=E - 1,
                        skip_runtime_bounds_check_because="the numbers are clamped where they are made", bass_reorder=False)
                    return values

                pe.wait_ge(routed, m // GROUPS + 1)
                e0, e1 = experts_of(0, 2)
                tr_x(0, 0, 0)
                tr_x(1, 1, 0)
                up_mm(0, 0, e0)
                tr_x(2, 2, 0)
                up_mm(1, 1, e1)
                tr_h(0, 0)
                with pe.Fori(0, STEPS // RING) as i:
                    ids = experts_of(RING * i, RING + 2)
                    for u in range(RING):
                        tr_x(RING * i + (u + 3), (u + 3) % RING, i + (u + 3) // RING)
                        up_mm(RING * i + (u + 2), u % 2, ids[u + 2])
                        tr_h(RING * i + (u + 1), (u + 1) % 2)
                        dn_mm(RING * i + u, u % 2, ids[u])
                ea, eb, ec = experts_of(NT - 3, 3)
                up_mm(NT - 1, (NT - 1) % 2, ec)
                tr_h(NT - 2, (NT - 2) % 2)
                dn_mm(NT - 3, (NT - 3) % 2, ea)
                tr_h(NT - 1, (NT - 1) % 2)
                dn_mm(NT - 2, (NT - 2) % 2, eb)
                dn_mm(NT - 1, (NT - 1) % 2, ec)

            pe.wait_ge(const_ready, 1)
            pe.wait_ge(in_w0, 16)
            setup(0, wk0, wq0, wv0)
            transposes(0)
            pe.wait_ge(mrow_ready, 1)
            attention(0, 0)
            transposes(1)
            router(0, 1, gate0)
            setup1()
            pe.wait_ge(w_split, 2 * E)
            for g in range(GROUPS):
                experts(g, [WA], WB)
            pe.wait_ge(s1_evac, 2)
            transposes(2)
            attention1(2)
            transposes(3)
            router(1, 3, gate1)
            setup2()
            setup_ffn2()
            pe.wait_ge(w_split, 4 * E)
            for g in range(GROUPS):
                experts(GROUPS + g, [WC[:, :, :, 0:256]], WC[:, :, :, 256:512])
            pe.wait_ge(in_w3, 16)
            setup(1, wk3, wq3, wv3)
            xattn2()
            ffn2()
            transposes(4)
            pe.wait_ge(mrow_ready, 2)
            attention(1, 4)
            transposes(5)
            router(2, 5, gate3)
            pe.wait_ge(w_split, 7 * E)
            for g in range(GROUPS):
                experts(2 * GROUPS + g, [WC, WA], WB)


def kernel(**inputs):
    import numpy as _np
    import concourse.bacc as _bacc
    from concourse import mybir as _mybir
    from concourse.bass_utils import run_bass_kernel_spmd as _run

    a = {k: _np.asarray(v) for k, v in inputs.items()}
    ctxT = a["ctx_1024"].reshape(-1, 128).T
    columns = [a[k][:, None] for k in ("L1_xattn_bq", "L1_xattn_bk", "L3_xattn_bq", "L3_xattn_bk")]
    arrays = {
        "p0": _np.concatenate([ctxT, a["L0_xattn_Wk"].T, a["L0_xattn_Wq"], a["L0_xattn_Wv"].T, a["L0_xattn_Wo"].T,
                               a["L0_ffn_gate_w"]], axis=1),
        "p1": _np.concatenate([a["L1_xattn_Wk"].T, a["L1_xattn_Wq"], a["L1_xattn_Wv"].T, a["L1_ffn_Wr"]], axis=1),
        "p3": _np.concatenate([a["L3_xattn_Wk"], a["L3_xattn_Wq"].T, a["L3_xattn_Wv"], a["L3_xattn_Wo"],
                               a["L3_ffn_w_gate"]], axis=1),
        "cols": _np.concatenate(columns, axis=1),
        "rows": _np.concatenate([a["L1_xattn_bv"], a["L3_xattn_bv"], a["L3_xattn_bo"], a["L2_xattn_bout"],
                                 a["L1_ffn_br"]])[None],
        "bias": _np.concatenate([a["L1_ffn_b1"].reshape(-1), a["L1_ffn_b2"].reshape(-1),
                                 a["L2_ffn_conv_b"]])[None],
        "x": a["x"].reshape(-1, 128),
        "mask0": a["mask_Bx1xS2_if1"].reshape(1, 4, 32),
        "mask3": a["mask_BxSxS2_if1"].reshape(-1, 32).T,
        "fc0": a["L0_ffn_fc_w"],
        "pj0": a["L0_ffn_proj_w"],
        "fc1": a["L1_ffn_W1"],
        "pj1": a["L1_ffn_W2"],
        "fc3": a["L3_ffn_w_gate_up"],
        "pj3": a["L3_ffn_w_down"],
        "wkv": a["L2_xattn_Wkv"],
        "wq2": a["L2_xattn_Wq"],
        "wout2": a["L2_xattn_Wout"],
        "w1t": a["L2_ffn_w1"].T,
        "w2t": a["L2_ffn_w2"].T,
        "cw": a["L2_ffn_conv_w"][:, 0, :].T,
    }
    nc = _bacc.Bacc("TRN2", target_bir_lowering=False, num_devices=1)
    args, maps = [], {}
    for name, v in arrays.items():
        v = _np.ascontiguousarray(v)
        maps[f"in_{name}_dram"] = v
        args.append(nc.dram_tensor(f"in_{name}_dram", v.shape, _mybir.dt.from_np(v.dtype), kind="ExternalInput").ap())
    out = nc.dram_tensor("out_dram", (2048, 128), _mybir.dt.float32, kind="ExternalOutput").ap()
    build(nc, *args, out)
    r = _run(nc, [maps], core_ids=[0])
    return r.results[0]["out_dram"].reshape(4, 512, 128)
```

```python
from contextlib import ExitStack

import concourse.bass as bass
from concourse import mybir

F32 = mybir.dt.float32
F32R = mybir.dt.float32r
BF16 = mybir.dt.bfloat16
I32 = mybir.dt.int32
ACT = mybir.ActivationFunctionType
ALU = mybir.AluOpType
AX = mybir.AxisListType

P = 128
B, S, D = 4, 512, 128
K = 32
H = 16
DK = D // H
HK = H * K
TILES = B * S // P
BT = S // P
GROUPS = 2
GT = TILES // GROUPS
GB = B // GROUPS
E, TOPK = 8, 2
HPC = P // K
HC = H // HPC
VW = HPC * DK + HPC
NT = (GT * P * TOPK + E * (P - 1)) // P
PAD = 4
RAW = 6
SLOTS = GROUPS * NT
RING = 4
STEPS = SLOTS - 3
LAG = 2 * RING
ROUNDS = STEPS // RING
EPS = 1e-5
FILL = -float(2 ** 100)
ROUND = 1.5 * 2.0 ** 23
NEG = -3.4028234663852886e38
HL, DL = 16, 64
INNER = HL * DL
IC = INNER // P
ZBUFS = 4
F2, F2C, TAPS = 512, 4, 3
PARTS = 3
NB = (E * (256 + D) + F2 + D) // P
RSQRT_SEED = float(0x5F3759DF)
assert GT == E == 2 * PAD


def uses(tiles, slot):
    return (tiles - slot + RING - 1) // RING


def turn_of(n, q):
    return B * n + q if n not in (2, 3) else 2 * B + q // GB * 2 * GB + (n - 2) * GB + q % GB


MOE = [
    dict(up=512, f=512, act=ACT.Gelu, bias=False),
    dict(up=256, f=256, act=ACT.Relu, bias=True),
    dict(up=1024, f=512, act=ACT.Silu, bias=False),
]


def build(nc, p0, p1, p3, cols, rows, bias, x, mask0, mask3, fc0, pj0, fc1, pj1, fc3, pj3,
          wkv, wq2, wout2, w1t, w2t, cw, out):
    ctx = ExitStack()
    with ctx:
        def sb(name, shape, dt):
            return ctx.enter_context(nc.sbuf_tensor(name, shape, dt))

        def sem(name):
            return ctx.enter_context(nc.semaphore(name))

        xs_dram = [nc.dram_tensor(f"xs{g}", (NT * P, D), F32, kind="Internal").ap() for g in range(GROUPS)]
        ys_dram = [nc.dram_tensor(f"ys{g}", (NT * P, D), F32, kind="Internal").ap() for g in range(GROUPS)]
        xs_tiles = [a.rearrange("(t p) d -> t p d", p=P) for a in xs_dram]
        ys_tiles = [a.rearrange("(t p) d -> t p d", p=P) for a in ys_dram]

        bias_dram = nc.dram_tensor("bias_split", (PARTS, P, NB), BF16, kind="Internal").ap()
        rows_dram = nc.dram_tensor("key_rows", (PARTS, B, HK), BF16, kind="Internal").ap()

        bank = [ctx.enter_context(nc.psum_tensor(f"bank{i}", [P, 512], F32)) for i in range(8)]

        ident = sb("ident", [P, P], F32)
        ones_row = sb("ones_row", [1, P], F32)
        ones_row_bf = sb("ones_row_bf", [1, P], BF16)
        ones_bf = sb("ones_bf", [P, P], BF16)
        before_bf = sb("before_bf", [P, P], BF16)
        head_mask = sb("head_mask", [P, H], F32)
        chunk_mask = sb("chunk_mask", [P, HPC], F32)
        expert_i = sb("expert_i", [P, E], I32)
        prefer = sb("prefer", [P, E], F32)
        tile_i = sb("tile_i", [1, NT, E], I32)
        tile_no = sb("tile_no", [1, NT, E], F32)
        zeros = sb("zeros", [P, P], F32)
        ones_f = sb("ones_f", [P, P], F32)
        ident_bf = sb("ident_bf", [P, P], BF16)

        X = sb("X", [P, TILES, D], F32)
        w0 = sb("w0", [P, 5 * P + E], F32)
        ctxT, wk0, wq0, wv0, wo0 = (w0[:, i * P:(i + 1) * P] for i in range(5))
        gate0 = w0[:, 5 * P:5 * P + E]
        mask0_i = sb("mask0_i", [1, B, K], I32)
        w1 = sb("w1", [P, 3 * P + E], F32)
        wk1, wq1, wv1 = (w1[:, i * P:(i + 1) * P] for i in range(3))
        gate1 = w1[:, 3 * P:3 * P + E]
        w3 = sb("w3", [P, 4 * P + E], F32)
        wk3, wq3, wv3, wo3 = (w3[:, i * P:(i + 1) * P] for i in range(4))
        gate3 = w3[:, 4 * P:4 * P + E]
        col = sb("col", [P, 4], F32)
        bq1, bk1, bq3, bk3 = (col[:, i:i + 1] for i in range(4))
        row = sb("row", [1, 3 * P + E], F32)
        bv1, bv3, bout2 = (row[:, i * P:(i + 1) * P] for i in range(3))
        br1 = row[:, 3 * P:3 * P + E]
        bias_s = sb("bias_s", [P, NB], F32)
        bias_parts = sb("bias_parts", [P, PARTS, NB], BF16)
        bo_rows = sb("bo_rows", [PARTS, D], BF16)
        bq_cols = sb("bq_cols", [P, B, B], F32)
        score_rows = sb("score_rows", [PARTS + K, B, HK], BF16)
        vo = sb("vo", [P, D], F32)
        M1 = sb("M1", [P, B, K], F32)
        r1 = sb("r1", [P, B, K], F32)
        br_all = sb("br_all", [P, E], F32)
        V1 = sb("V1", [K, B, D], F32)
        batch_mask = sb("batch_mask", [P, P], F32)
        late = sb("late", [P, 1], F32)

        ctx4 = sb("ctx4", [P, B, HPC, K], F32)
        kT = sb("kT", [P, B, K], F32)
        with nc.sbuf_tensor("bias_rows", [PARTS, E * (256 + D)], BF16) as bias_rows:
            pass
        M = sb("M", [P, B, HK], F32)
        VB = sb("VB", [P, B, HC, VW], F32)
        mfill = sb("mfill", [PARTS + K, B * S], BF16)
        mrow = mfill[0:1, :].rearrange("p (b h k) -> p b h k", b=B, h=H)
        stats = sb("stats", [P, TILES, 6], F32)
        mv = sb("mv", [P, TILES, 2], F32)
        var_eps, y_squared, minus_half_vyy, rstd = (
            sb(n, [P, TILES], F32) for n in ("var_eps", "y_squared", "minus_half_vyy", "rstd"))
        half_bits, seed_bits = (sb(n, [P, TILES], I32) for n in ("half_bits", "seed_bits"))
        XNR = sb("XNR", [P, TILES, D], F32)
        smax = sb("smax", [P, 2, H], F32)
        rsum = sb("rsum", [P, 2, H], F32)
        ON = sb("ON", [P, 2, D], F32)
        OT = sb("OT", [P, 2, P], F32)

        both = sb("both", [P, GROUPS, GT, E], BF16)
        ahead_a = sb("ahead_a", [P, GROUPS, PAD + GT, E], BF16)
        ahead_b = sb("ahead_b", [P, GROUPS, PAD + GT, E], BF16)
        l1_max = sb("l1_max", [P, TILES], F32)
        l1_sum = sb("l1_sum", [P, TILES], F32)
        m1, m2, c1, de, e2, es, pr1, pr2, den = (
            sb(n, [P, GT], F32) for n in ("m1", "m2", "c1", "de", "e2", "es", "pr1", "pr2", "den"))
        ex = sb("ex", [P, GT, E], F32)
        gates = sb("gates", [P, TOPK, TILES], F32)
        cnt = sb("cnt", [P, E], F32)
        inc_a = sb("inc_a", [P, PAD + E], F32)
        inc_b = sb("inc_b", [P, PAD + E], F32)
        start_f = sb("start_f", [P, E], F32)
        slot_f = sb("slot_f", [P, TOPK, GT], F32)
        slot_i = sb("slot_i", [P, TOPK, TILES], I32)
        eid_f = sb("eid_f", [1, NT], F32)
        eid_c = sb("eid_c", [1, NT], F32)
        eid_i = sb("eid_i", [1, SLOTS], I32)

        with ExitStack() as l2f_tiles:
            def l2f(name, shape, dt=F32):
                return l2f_tiles.enter_context(nc.sbuf_tensor(name, shape, dt))

            w1c_h = l2f("w1c_h", [P, TAPS, F2], F32R)
            w1c_l = l2f("w1c_l", [P, TAPS, F2], F32R)
            w1_s = l2f("w1_s", [P, F2])
            w2_s = l2f("w2_s", [P, F2C, D])
            w2q = l2f("w2q", [P, F2C, D], BF16)
            cw_s = l2f("cw_s", [TAPS, F2])
            U = l2f("U", [P, B, D])
            cb = l2f("cb", [PARTS, F2], BF16)
            Z = l2f("Z", [P, ZBUFS, F2])
        WA = sb("WA", [P, E, 2, 512], F32R)
        with ExitStack() as l2_tiles:
            def l2x(name, shape, dt=F32):
                return l2_tiles.enter_context(nc.sbuf_tensor(name, shape, dt))

            wkv_s = l2x("wkv_s", [P, 2 * INNER])
            wq_s = l2x("wq_s", [P, INNER])
            wout_s = l2x("wout_s", [P, IC, D])
            kall = l2x("kall", [P, INNER])
            vall = l2x("vall", [P, INNER])
            vsum = l2x("vsum", [P, INNER])
            attn2 = l2x("attn2", [P, INNER])
        WB = sb("WB", [P, E, 2, 512], F32R)
        WC = sb("WC", [P, E, 2, 512], F32R)
        wmean = sb("wmean", [P, 2, 4], F32)
        raw = sb("raw", [P, RAW, 512], F32)
        xrow = [sb(f"xrow{i}", [P, D], F32) for i in range(RING)]
        with ExitStack() as attention_tiles:
            def at(name, shape, dt):
                return attention_tiles.enter_context(nc.sbuf_tensor(name, shape, dt))

            rrow = at("rrow", [B, HK], F32)
            with nc.sbuf_tensor("rparts", [B, PARTS, HK], BF16) as rparts:
                pass
            XT = at("XT", [P, TILES, P], F32)
            with ExitStack() as routing_tiles:
                lg, second, cand, oh1, oh2, dl, place, pick = (
                    routing_tiles.enter_context(nc.sbuf_tensor(n, [P, GT, E], F32))
                    for n in ("lg", "second", "cand", "oh1", "oh2", "dl", "place", "pick"))
                le = routing_tiles.enter_context(nc.sbuf_tensor("le", [1, NT, E], F32))
            PR = at("PR", [P, 2, HK], F32)
            with nc.sbuf_tensor("PT1", [K, TILES, P], F32) as PT1:
                pass
            PT = at("PT", [P, 2, HC, P], F32)
        with ExitStack() as ffn_tiles:
            def ff(name, shape, dt):
                return ffn_tiles.enter_context(nc.sbuf_tensor(name, shape, dt))

            XQ = ff("XQ", [P, TILES, D], F32)
            xqh = ff("xqh", [P, 2, S + 2], F32R)
            xql = ff("xql", [P, 2, S + 2], F32R)
            zqT = ff("zqT", [P, 2, F2C, P], BF16)
        xh = [sb(f"xh{i}", [P, P], F32R) for i in range(2)]
        xl = [sb(f"xl{i}", [P, P], F32R) for i in range(2)]
        hb = [sb(f"hb{i}", [P, 512], F32) for i in range(2)]
        hh = [sb(f"hh{i}", [P, 4, P], F32R) for i in range(2)]
        gb = [sb(f"gb{i}", [P, 512], F32) for i in range(2)]
        hl = [sb(f"hl{i}", [P, 4, P], F32R) for i in range(2)]
        with nc.sbuf_tensor("kbd", [P, B, H, K], F32) as kbd:
            pass
        YG = [sb("YG0", [P, GT, D], F32)]
        Y = sb("Y", [P, RING, D], F32)
        kbd_rest = sb("kbd_rest", [P, B * H * K - (GT + RING) * D], F32)
        YG.append(sb("YG1", [P, GT, D], F32))
        XL = sb("XL", [P, P], F32)
        s16 = sb("s16", [P, HL], F32)
        m16 = sb("m16", [P, HL], F32)
        e16 = sb("e16", [P, 2, HL], F32)
        sum16 = sb("sum16", [P, HL], F32)
        amax = sb("amax", [P, TILES], F32)
        qscale = sb("qscale", [P, TILES], F32)
        qinv = sb("qinv", [P, TILES], F32)
        zmax = sb("zmax", [P, 2], F32)
        zscale = sb("zscale", [P, 2], F32)
        zinv = sb("zinv", [P, TILES], F32)

        in_w0, in_mask0 = (
            sem(n) for n in ("in_w0", "in_mask0"))
        in_x = [sem(f"in_x{g}") for g in range(GROUPS)]
        in_raw = [sem(f"in_raw{i}") for i in range(RAW)]
        zeroed, const_ready, pool_chain, dve_chain = (
            sem(n) for n in ("zeroed", "const_ready", "pool_chain", "dve_chain"))
        zeros_ready, xn_ready = (
            sem(n) for n in ("zeros_ready", "xn_ready"))
        setup_mm, setup_evac, m_evac, ctx4_ready, mrow_ready = (
            sem(n) for n in ("setup_mm", "setup_evac", "m_evac", "ctx4_ready", "mrow_ready"))
        xt_mm, xt_ready = (
            sem(n) for n in ("xt_mm", "xt_ready"))
        s_mm, s_sub, s_exp, pt_mm, pt_ready = (
            sem(n) for n in ("s_mm", "s_sub", "s_exp", "pt_mm", "pt_ready"))
        o_mm, o_norm, ot_mm, ot_ready, wo_mm, x_added = (
            sem(n) for n in ("o_mm", "o_norm", "ot_mm", "ot_ready", "wo_mm", "x_added"))
        lg_mm, both_ready, rank_mm, routed, dl_ready, ex_ready = (
            sem(n) for n in ("lg_mm", "both_ready", "rank_mm", "routed", "dl_ready", "ex_ready"))
        scattered = [sem(f"scattered{g}") for g in range(GROUPS)]
        y_stored = [sem(f"y_stored{i}") for i in range(RING)]
        gathered = [[sem(f"gathered{g}{k}") for k in range(TOPK)] for g in range(GROUPS)]
        x_loaded = [sem(f"x_loaded{i}") for i in range(RING)]
        w_split = sem("w_split")
        ex_t, ex_xh, ex_xl, ex_up, ex_act = (
            sem(n) for n in ("ex_t", "ex_xh", "ex_xl", "ex_up", "ex_act"))
        ex_ht, ex_hh, ex_hl, ex_dn, ex_y = (
            sem(n) for n in ("ex_ht", "ex_hh", "ex_hl", "ex_dn", "ex_y"))
        stored = sem("stored")
        in_w1, in_w3, in_col, in_row, in_bias, in_rows, in_mask3, in_l2, in_ff2 = (
            sem(n) for n in ("in_w1", "in_w3", "in_col", "in_row", "in_bias", "in_rows", "in_mask3", "in_l2", "in_ff2"))
        s1_mm, s1_evac, s2_mm, s2_evac, s2_act, r_mm, r_evac = (
            sem(n) for n in ("s1_mm", "s1_evac", "s2_mm", "s2_evac", "s2_act", "r_mm", "r_evac"))
        a1_s, a1_sub, a1_exp, a1_p, a1_pt, a1_ptc, a1_o, a1_added = (
            sem(n) for n in ("a1_s", "a1_sub", "a1_exp", "a1_p", "a1_pt", "a1_ptc", "a1_o", "a1_added"))
        x2_n, x2_t, x2_xl, x2_q, x2_m, x2_e, x2_o, x2_ot, x2_otc, x2_y, x2_yc, x2_mm, x2_added = (
            sem(n) for n in ("x2_n", "x2_t", "x2_xl", "x2_q", "x2_m", "x2_e", "x2_o", "x2_ot", "x2_otc", "x2_y", "x2_yc",
                             "x2_mm", "x2_added"))
        fs_sum, fs_mm, fs_ready = (sem(n) for n in ("fs_sum", "fs_mm", "fs_ready"))
        f2_xq, f2_xt, f2_xh, f2_xl, f2_h, f2_z, f2_zq, f2_qt, f2_qtc, f2_dn, f2_added = (
            sem(n) for n in ("f2_xq", "f2_xt", "f2_xh", "f2_xl", "f2_h", "f2_z", "f2_zq", "f2_qt", "f2_qtc",
                             "f2_dn", "f2_added"))
        ex_mul = sem("ex_mul")
        experts_known = sem("experts_known")
        bias_split, bias_out, rows_out, in_key_rows, sel_ready, fs_read, fs_taps = (
            sem(n) for n in ("bias_split", "bias_out", "rows_out", "in_key_rows", "sel_ready", "fs_read", "fs_taps"))
        combined = sem("combined")

        N_W1, N_W3 = 2 * E, 4 * E
        N_D3, N_U3 = N_W3 + E, N_W3 + 2 * E
        mask3_i = XNR[0:PARTS + K, :, :].rearrange("p t d -> p (t d)").bitcast(I32)
        bias1 = bias_rows[:, 0:E * 256].rearrange("i (e f) -> i e f", e=E)
        bias2 = bias_rows[:, E * 256:].rearrange("i (e f) -> i e f", e=E)
        bias_flat = bias_dram.rearrange("i p c -> i (p c)")
        oT = wkv_s[:, INNER:2 * INNER].rearrange("p (c r) -> p c r", c=IC)
        kq = wkv_s[:, 0:INNER]
        zq = w1_s[:, :].bitcast(BF16).rearrange("p (i f) -> p i f", i=2)

        def y_banks_of(layer):
            return [bank[7]] if layer["up"] > layer["f"] else [bank[7], bank[3]]

        block = ctx.enter_context(nc.Block())

        @block.sync
        def _(sp):
            x_v = x.rearrange("(g t p) d -> g p t d", g=GROUPS, p=P)
            sp.dma_start(X[:, 0:GT, :], x_v[0]).then_inc(in_x[0], 16)
            sp.dma_start(w0[:, :], p0).then_inc(in_w0, 16)
            sp.dma_start(mask0_i[:, :, :], mask0).then_inc(in_mask0, 16)
            sp.dma_start(X[:, GT:TILES, :], x_v[1]).then_inc(in_x[1], 16)
            sp.dma_start(bias_s[:, :], bias).then_inc(in_bias, 16)
            sp.dma_start(col[:, :], cols).then_inc(in_col, 16)
            sp.dma_start(row[:, :], rows).then_inc(in_row, 16)
            sp.dma_start(w1[:, :], p1).then_inc(in_w1, 16)
            sp.dma_start(w3[:, :], p3).then_inc(in_w3, 16)

            def load_weights(n0, matrices):
                for i, (src, width) in enumerate(matrices):
                    n = n0 + i
                    if n >= RAW:
                        sp.wait_ge(w_split, n - RAW + 1)
                    dst = raw[:, n % RAW, 0:width]
                    if src.shape[0] != P:
                        src = src.rearrange("(c p) d -> p c d", p=P)
                        dst = dst.rearrange("p (c d) -> p c d", d=D)
                    sp.dma_start(dst, src).then_inc(in_raw[n % RAW], 16)

            sp.wait_ge(zeros_ready, 1)
            for g in range(GROUPS):
                sp.dma_start(xs_tiles[g].rearrange("t p d -> p t d"),
                             zeros[:, :].unsqueeze(1).broadcast_to([P, NT, D])).then_inc(zeroed, 16)
            load_weights(0, [(w[e], 512) for e in range(E) for w in (fc0, pj0)])

            def experts(layer):
                base = layer * SLOTS

                def load(g, t, s):
                    sp.dma_start(xrow[s][:, :],
                                 xs_tiles[g][bass.ds(t - g * NT, 1)].rearrange("a p d -> p (a d)")).then_inc(x_loaded[s], 16)

                def store(g, t, s):
                    sp.wait_ge(ex_y, t + base + 1)
                    sp.dma_start(ys_tiles[g][bass.ds(t - g * NT, 1)].rearrange("a p d -> p (a d)"),
                                 Y[:, s, :]).then_inc(y_stored[s], 16)

                def step(load_half, store_half, t, s):
                    sp.wait_ge(ex_t, t + (base - RING + 1))
                    load(load_half, t, s)
                    store(store_half, t - LAG, (s - LAG) % RING)

                def half_of(t):
                    return t // NT

                sp.wait_ge(scattered[0], 16 * TOPK * GT * (layer + 1))
                if layer:
                    sp.wait_ge(ex_t, base)
                for t in range(LAG):
                    if t >= RING:
                        sp.wait_ge(ex_t, base + t - RING + 1)
                    load(0, t, t % RING)
                t = LAG
                while t < SLOTS:
                    ends = [e for e in (NT, NT + LAG, SLOTS) if e > t]
                    rounds = (ends[0] - t) // RING if t % RING == 0 else 0
                    if t == NT:
                        sp.wait_ge(scattered[1], 16 * TOPK * GT * (layer + 1))
                    if rounds > 1:
                        with sp.Fori(0, rounds) as i:
                            for u in range(RING):
                                step(half_of(t), half_of(t - LAG), i * RING + (t + u), u)
                        t += rounds * RING
                    else:
                        step(half_of(t), half_of(t - LAG), t, t % RING)
                        t += 1
                for t in range(SLOTS - LAG, SLOTS):
                    store(1, t, t % RING)

            sp.wait_ge(bias_split, 1)
            sp.dma_start(bias_dram.rearrange("i p c -> p i c"), bias_parts[:, :, :]).then_inc(bias_out, 16)
            load_weights(N_W1, [(w[e], 256) for e in range(E) for w in (fc1, pj1)])
            sp.wait_ge(bias_out, 16)
            sp.wait_ge(s_mm, TILES)
            sp.dma_start(bias_rows[:, :], bias_flat[:, 0:E * (256 + D)]).then_inc(in_rows, 16)
            sp.dma_start(bo_rows[:, :], bias_flat[:, E * (256 + D) + F2:]).then_inc(in_rows, 16)
            experts(0)
            sp.wait_ge(ex_dn, SLOTS)
            sp.dma_start(w1_s[:, :], w1t).then_inc(in_ff2, 16)
            sp.dma_start(w2_s[:, :, :], w2t.rearrange("(c p) d -> p c d", p=P)).then_inc(in_ff2, 16)
            sp.dma_start(cw_s[:, :], cw).then_inc(in_ff2, 16)
            sp.dma_start(cb[:, :], bias_flat[:, E * (256 + D):E * (256 + D) + F2]).then_inc(in_ff2, 16)
            sp.dma_start(wkv_s[:, :], wkv).then_inc(in_l2, 16)
            sp.dma_start(wq_s[:, :], wq2).then_inc(in_l2, 16)
            sp.dma_start(wout_s[:, :, :], wout2.rearrange("(c p) d -> p c d", p=P)).then_inc(in_l2, 16)
            experts(1)
            load_weights(N_W3, [(fc3[e, :, 0:512], 512) for e in range(RAW)])
            sp.wait_ge(r_evac, 1)
            sp.dma_start(rows_dram.rearrange("i b f -> b i f"), rparts[:, :, :]).then_inc(rows_out, 16)
            sp.wait_ge(rows_out, 16)
            sp.wait_ge(sel_ready, 1)
            sp.dma_start(score_rows[0:PARTS, :, :], rows_dram).then_inc(in_key_rows, 16)
            load_weights(N_W3 + RAW, [(fc3[e, :, 0:512], 512) for e in range(RAW, E)])
            sp.wait_ge(x2_added, 1)
            sp.dma_start(mask3_i[PARTS:PARTS + K, :], mask3).then_inc(in_mask3, 16)
            load_weights(N_D3, [(pj3[e], 512) for e in range(E)])
            load_weights(N_U3, [(fc3[e, :, 512:1024], 512) for e in range(E)])
            experts(2)
            out_v = out.rearrange("(g t p) d -> g p t d", g=GROUPS, p=P)
            for g in range(GROUPS):
                sp.wait_ge(combined, 2 * GROUPS + g + 1)
                sp.dma_start(out_v[g], X[:, g * GT:(g + 1) * GT, :]).then_inc(stored, 16)
            sp.wait_ge(stored, 16 * GROUPS)

        @block.gpsimd
        def _(pool):
            n = [0]

            def link(ins):
                n[0] += 1
                ins.then_inc(pool_chain, 1)
                pool.wait_ge(pool_chain, n[0])

            link(pool.memset(zeros[:, :], 0.0))
            pool.sem_inc(zeros_ready, 1)
            link(pool.affine_select(out=ident[:, :], in_=zeros[:, :], compare_op=ALU.not_equal, fill=1.0,
                                    base=0, pattern=[[-1, P]], channel_multiplier=1))
            pool.memset(ones_row[:, :], 1.0)
            pool.memset(ones_row_bf[:, :], 1.0)
            pool.memset(ones_bf[:, :], 1.0)
            pool.memset(ones_f[:, :], 1.0)
            pool.memset(batch_mask[:, :], 1.0)
            pool.memset(late[:, :], 1.0)
            pool.memset(head_mask[:, :], 1.0)
            link(pool.memset(chunk_mask[:, :], 1.0))
            link(pool.affine_select(out=head_mask[:, :], in_=head_mask[:, :], compare_op=ALU.is_ge, fill=0.0,
                                    base=0, pattern=[[-DK, H]], channel_multiplier=1))
            link(pool.affine_select(out=head_mask[:, :], in_=head_mask[:, :], compare_op=ALU.is_ge, fill=0.0,
                                    base=DK - 1, pattern=[[DK, H]], channel_multiplier=-1))
            link(pool.affine_select(out=chunk_mask[:, :], in_=chunk_mask[:, :], compare_op=ALU.is_ge, fill=0.0,
                                    base=0, pattern=[[-K, HPC]], channel_multiplier=1))
            link(pool.affine_select(out=chunk_mask[:, :], in_=chunk_mask[:, :], compare_op=ALU.is_ge, fill=0.0,
                                    base=K - 1, pattern=[[K, HPC]], channel_multiplier=-1))
            link(pool.affine_select(out=before_bf[:, :], in_=ones_bf[:, :], compare_op=ALU.is_ge, fill=0.0,
                                    base=-1, pattern=[[1, P]], channel_multiplier=-1))
            bm = batch_mask[:, :].rearrange("p (b k) -> p b k", b=B)
            link(pool.affine_select(out=bm, in_=bm, compare_op=ALU.is_ge, fill=0.0,
                                    base=0, pattern=[[-K, B], [0, K]], channel_multiplier=1))
            link(pool.affine_select(out=bm, in_=bm, compare_op=ALU.is_ge, fill=0.0,
                                    base=K - 1, pattern=[[K, B], [0, K]], channel_multiplier=-1))
            link(pool.affine_select(out=late[:, :], in_=late[:, :], compare_op=ALU.is_ge, fill=0.0,
                                    base=-K, pattern=[[0, 1]], channel_multiplier=1))
            pool.iota(expert_i[:, :], [[-1, E]], base=E, channel_multiplier=0)
            pool.iota(tile_i[:, :, :], [[1, NT], [0, E]], base=0, channel_multiplier=0).then_inc(const_ready, 1)
            pool.wait_ge(const_ready, 1)
            pool.tensor_copy(prefer[:, :], expert_i[:, :])
            pool.tensor_copy(tile_no[:, :, :], tile_i[:, :, :])
            pool.tensor_copy(ident_bf[:, :], ident[:, :])
            for scan in (inc_a[:, :], inc_b[:, :], ahead_a[:, :, :, :], ahead_b[:, :, :, :]):
                ins = pool.memset(scan, 0.0)
            link(ins)
            pool.sem_inc(const_ready, 1)

            def split(n0, matrices):
                for i, dst in enumerate(matrices):
                    n = n0 + i
                    src = raw[:, n % RAW, 0:dst.shape[2]]
                    pool.wait_ge(in_raw[n % RAW], 16 * (n // RAW + 1))
                    link(pool.tensor_copy(dst[:, 0, :], src))
                    pool.tensor_tensor(dst[:, 1, :], src, dst[:, 0, :].bitcast(F32),
                                       ALU.subtract).then_inc(w_split, 1)

            def scatter(r):
                g = r % GROUPS
                if r == 0:
                    pool.wait_ge(zeroed, 16 * GROUPS)
                pool.wait_ge(routed, r + 1)
                for k in range(TOPK):
                    for j in range(GT):
                        t = g * GT + j
                        pool.indirect_dma_start(
                            out=xs_dram[g], out_offset=bass.IndirectOffsetOnAxis(ap=slot_i[:, k, t:t + 1], axis=0),
                            in_=XNR[:, t, :], in_offset=None).then_inc(scattered[g], 16)

            def gather(m):
                g = m % GROUPS
                for i in range(RING):
                    pool.wait_ge(y_stored[i], 16 * (m // GROUPS * uses(SLOTS, i) + uses((g + 1) * NT, i)))
                for k, dst in enumerate((XNR[:, g * GT:(g + 1) * GT, :], YG[g][:, :, :])):
                    for j in range(GT):
                        t = g * GT + j
                        pool.indirect_dma_start(
                            out=dst[:, j, :], out_offset=None, in_=ys_dram[g],
                            in_offset=bass.IndirectOffsetOnAxis(ap=slot_i[:, k, t:t + 1], axis=0)).then_inc(gathered[g][k], 16)

            split(0, [w[:, e, :, :] for e in range(E) for w in (WA, WB)])
            w1_halves = [WC[:, e, :, c:c + 256] for e in range(E) for c in (0, 256)]
            split(N_W1, w1_halves[:-RAW])
            scatter(0)
            scatter(1)
            split(N_W3 - RAW, w1_halves[-RAW:])
            link(pool.memset(score_rows[:, :, :], 0.0))
            pool.affine_select(out=score_rows[:, :, :].rearrange("p b (h k) -> p (b h) k", h=H),
                               in_=score_rows[:, :, :].rearrange("p b (h k) -> p (b h) k", h=H),
                               compare_op=ALU.not_equal, fill=1.0, base=-PARTS, pattern=[[0, B * H], [-1, K]],
                               channel_multiplier=1).then_inc(sel_ready, 1)
            gather(0)
            gather(1)
            scatter(2)
            scatter(3)
            gather(2)
            gather(3)
            pool.wait_ge(ex_dn, 2 * SLOTS)
            split(N_W3, [WC[:, e, :, :] for e in range(E)])
            pool.wait_ge(x2_added, 1)
            split(N_D3, [WB[:, e, :, :] for e in range(E)])
            pool.wait_ge(f2_added, TILES)
            split(N_U3, [WA[:, e, :, :] for e in range(E)])
            scatter(4)
            scatter(5)
            gather(4)
            gather(5)

        @block.scalar
        def _(act):
            def evac_xt(n, batches=range(B)):
                for q in batches:
                    act.wait_ge(xt_mm, turn_of(n, q) + 1)
                    act.activation(XT[:, q * BT:(q + 1) * BT, :], bank[4 + q][:, :].rearrange("p (t c) -> p t c", c=P),
                                   ACT.Copy).then_inc(xt_ready, 1)

            def setup(i):
                for b in range(B):
                    act.wait_ge(setup_mm, i * (B + 2) + 2 + b)
                    act.activation(M[:, b, :], bank[1 + b % 2][:, :], ACT.Copy).then_inc(m_evac, 1)

            def attention(a):
                for s in range(TILES + 4):
                    if s < TILES:
                        act.wait_ge(s_sub, a * TILES + s + 1)
                        act.activation(PR[:, s % 2, :], PR[:, s % 2, :], ACT.Exp, scale=float(DK) ** -0.5).then_inc(s_exp, 1)
                    j = s - 1
                    if 0 <= j < TILES:
                        act.wait_ge(pt_mm, a * TILES + j + 1)
                        act.activation(PT[:, j % 2, :, :], bank[2 + j % 2][:, :].rearrange("p (c t) -> p c t", c=HC),
                                       ACT.Copy).then_inc(pt_ready, 1)
                    j = s - 3
                    if 0 <= j < TILES:
                        act.wait_ge(ot_mm, a * TILES + j + 1)
                        act.activation(OT[:, j % 2, :], bank[6][:, 0:P], ACT.Copy).then_inc(ot_ready, 1)

            def router(r):
                act.wait_ge(dl_ready, r + 1)
                act.activation(ex[:, :, :], dl[:, :, :], ACT.Exp)
                act.activation(e2[:, :], de[:, :], ACT.Exp).then_inc(ex_ready, 1)

            def experts(layer):
                L = MOE[layer]
                f = L["f"]
                nc_f = f // P
                base = layer * SLOTS

                def x_high(t, s):
                    act.wait_ge(ex_t, t + base + 1)
                    act.activation(xh[s][:, :], bank[6][:, 0:P], ACT.Copy).then_inc(ex_xh, 1)

                def activate(t, s):
                    act.wait_ge(ex_up, t + base + 1)
                    dst = gb if L["up"] > L["f"] else hb
                    act.activation(dst[s][:, 0:f], bank[s][:, 0:f], L["act"]).then_inc(ex_act, 1)

                def h_high(t, s):
                    act.wait_ge(ex_ht, t + base + 1)
                    act.activation(hh[s][:, 0:nc_f, :], bank[4 + s][:, 0:f].rearrange("p (c t) -> p c t", c=nc_f),
                                   ACT.Copy).then_inc(ex_hh, 1)

                x_high(0, 0)
                x_high(1, 1)
                activate(0, 0)
                x_high(2, 0)
                activate(1, 1)
                h_high(0, 0)

                def step(t, u):
                    x_high(t + 3, (u + 1) % 2)
                    activate(t + 2, u % 2)
                    h_high(t + 1, (u + 1) % 2)

                with act.Fori(0, ROUNDS * RING // 2) as i:
                    for u in range(2):
                        step(2 * i + u, u)
                for t in range(ROUNDS * RING, STEPS):
                    step(t, t)
                activate(SLOTS - 1, (SLOTS - 1) % 2)
                h_high(SLOTS - 2, (SLOTS - 2) % 2)
                h_high(SLOTS - 1, (SLOTS - 1) % 2)

            def attention1(g):
                sc = PR[:, 0, g * GT * K:(g + 1) * GT * K]
                act.wait_ge(a1_sub, g + 1)
                act.activation(sc, sc, ACT.Exp, scale=float(D) ** -0.5).then_inc(a1_exp, 1)
                for b in range(g * GB, (g + 1) * GB):
                    act.wait_ge(a1_pt, b + 1)
                    act.activation(PT1[:, b * BT:(b + 1) * BT, :], bank[b % 4][0:K, :].rearrange("p (t c) -> p t c", t=BT),
                                   ACT.Copy).then_inc(a1_ptc, 1)

            def setup2():
                for i, dst in enumerate((kall, vall)):
                    act.wait_ge(s2_mm, i + 1)
                    for c in range(2):
                        act.activation(dst[:, c * 512:(c + 1) * 512], bank[4 + 2 * i + c][:, :], ACT.Copy).then_inc(s2_act, 1)
                act.wait_ge(s2_mm, 3)
                for c in range(2):
                    act.activation(vsum[:, c * 512:(c + 1) * 512], bank[4 + c][:, :], ACT.Copy).then_inc(s2_act, 1)
                act.wait_ge(s2_mm, 4)
                for c in range(2):
                    act.activation(attn2[:, c * 512:(c + 1) * 512], bank[6 + c][:, :], ACT.Copy, scale=1.0 / K).then_inc(s2_act, 1)

            def xattn2():
                act.wait_ge(x2_t, 1)
                act.activation(XL[:, :], bank[6][:, 0:B * K], ACT.Copy).then_inc(x2_xl, 1)
                act.wait_ge(x2_m, 1)
                act.activation(e16[:, :, :], e16[:, :, :], ACT.Exp).then_inc(x2_e, 1)
                for c in range(2):
                    act.wait_ge(x2_ot, c + 1)
                    act.activation(oT[:, c * 4:(c + 1) * 4, :],
                                   bank[2 + c][:, :].rearrange("p (c r) -> p c r", c=4), ACT.Copy).then_inc(x2_otc, 1)
                act.wait_ge(x2_y, 1)
                act.activation(XL[:, :], bank[4][:, 0:B * K], ACT.Copy).then_inc(x2_yc, 1)

            def ffn2():
                def x_high(b):
                    act.wait_ge(f2_xt, b + 1)
                    act.activation(xqh[:, b % 2, 1:S + 1], bank[6][:, :], ACT.Copy).then_inc(f2_xh, 1)

                def hidden(i):
                    act.wait_ge(f2_h, i + 1)
                    if i >= ZBUFS:
                        act.wait_ge(f2_zq, i - ZBUFS + 1)
                    act.activation(Z[:, i % ZBUFS, :], bank[i % 4][:, :], ACT.Silu).then_inc(f2_z, 1)

                def turned(i):
                    act.wait_ge(f2_qt, i + 1)
                    act.activation(zqT[:, i % 2, :, :], bank[4 + i % 2][:, 0:F2 // 2].bitcast(BF16)
                                   .rearrange("p (c t) -> p c t", c=F2C), ACT.Copy).then_inc(f2_qtc, 1)

                x_high(0)
                for p in range(TILES // 2 + 1):
                    if p % 2 == 0 and p // 2 + 1 < B:
                        x_high(p // 2 + 1)
                    if p < TILES // 2:
                        hidden(2 * p)
                        hidden(2 * p + 1)
                    if p:
                        turned(2 * p - 2)
                        turned(2 * p - 1)

            setup(0)
            evac_xt(0)
            attention(0)
            evac_xt(1)
            for g in range(GROUPS):
                router(g)
            experts(0)
            for g in range(GROUPS):
                batches = range(g * GB, (g + 1) * GB)
                if g == 0:
                    evac_xt(2, batches)
                attention1(g)
                evac_xt(3, batches)
                if g == 0:
                    evac_xt(2, range(GB, B))
                router(1 * GROUPS + g)
            experts(1)
            setup2()
            setup(1)
            xattn2()
            ffn2()
            evac_xt(4)
            attention(1)
            evac_xt(5)
            for g in range(GROUPS):
                router(2 * GROUPS + g)
            experts(2)

        @block.vector
        def _(dve):
            n = [0]

            def link(ins):
                n[0] += 1
                ins.then_inc(dve_chain, 1)
                dve.wait_ge(dve_chain, n[0])

            def ln_stats(tiles):
                for j, t in enumerate(tiles):
                    ins = dve.bn_stats(stats[:, j, :], X[:, t, :])
                link(ins)

            def ln_aggregate(tiles, first=0):
                for j in range(len(tiles)):
                    ins = dve.bn_aggr(mv[:, j, :], stats[:, first + j, :])
                link(ins)

            def ln_rstd(nt):
                v, a, b = var_eps[:, 0:nt], y_squared[:, 0:nt], minus_half_vyy[:, 0:nt]
                link(dve.tensor_scalar(v, mv[:, 0:nt, 1], EPS, None, ALU.add))
                link(dve.tensor_scalar(half_bits[:, 0:nt], v.bitcast(I32), 1, None, ALU.logical_shift_right))
                link(dve.tensor_scalar(seed_bits[:, 0:nt], half_bits[:, 0:nt], -1.0, RSQRT_SEED, ALU.mult, ALU.add))
                y = seed_bits[:, 0:nt].bitcast(F32)
                for k in range(3):
                    link(dve.tensor_tensor(a, y, y, ALU.mult))
                    link(dve.scalar_tensor_tensor(out=b, in0=v, scalar=-0.5, in1=a, op0=ALU.mult, op1=ALU.mult))
                    link(dve.scalar_tensor_tensor(out=rstd[:, 0:nt], in0=b, scalar=1.5, in1=y, op0=ALU.add, op1=ALU.mult))
                    y = rstd[:, 0:nt]

            def ln_scale(tiles, dst, done=None):
                for j, t in enumerate(tiles):
                    ins = dve.tensor_scalar(dst[:, j, :], X[:, t, :], mv[:, j, 0:1], rstd[:, j:j + 1],
                                            ALU.subtract, ALU.mult)
                    if done is not None:
                        ins.then_inc(done, 1)
                if done is None:
                    link(ins)

            def layer_norm(tiles, dst, done=None):
                ln_stats(tiles)
                ln_aggregate(tiles)
                ln_rstd(len(tiles))
                ln_scale(tiles, dst, done)

            everything = list(range(TILES))

            def half(g):
                return everything[g * GT:(g + 1) * GT]

            def mask_row():
                dve.wait_ge(in_mask0, 16)
                dve.tensor_scalar(mrow, mask0_i[:, :, :].unsqueeze(2).broadcast_to([1, B, H, K]),
                                  0, FILL, ALU.is_equal, ALU.mult).then_inc(mrow_ready, 1)

            def split_biases():
                dve.wait_ge(in_bias, 16)
                split3([bias_parts[:, i, :] for i in range(PARTS)], bias_s[:, :]).then_inc(bias_split, 1)

            def split3(parts, src):
                for part in parts[:-1]:
                    link(dve.tensor_copy(part, src))
                    link(dve.tensor_tensor(src, src, part, ALU.subtract))
                return dve.tensor_copy(parts[-1], src)

            def keys(i):
                dve.wait_ge(setup_mm, i * (B + 2) + 1)
                kps = bank[0][:, 0:P].rearrange("p (b k) -> p b k", b=B)
                if i == 0:
                    link(dve.tensor_copy(kT[:, :, :], kps))
                else:
                    for s in range(RING):
                        dve.wait_ge(y_stored[s], 16 * 2 * uses(SLOTS, s))
                    link(dve.memset(bq_cols[:, :, :], 0.0))
                    dve.tensor_copy(bq_cols[:, :, :].rearrange("p a b -> p (a b)")[:, 0::B + 1], bq3.broadcast_to([P, B]))
                    link(dve.tensor_scalar(kT[:, :, :], kps, bk3, None, ALU.add))
                for b in range(B):
                    dve.tensor_tensor(kbd[:, b, :, :], kT[:, b, :].unsqueeze(1).broadcast_to([P, H, K]),
                                      head_mask[:, :].unsqueeze(2).broadcast_to([P, H, K]), ALU.mult).then_inc(setup_evac, 1)

            def query_bias_rows():
                dve.wait_ge(r_mm, 1)
                link(dve.tensor_copy(rrow[:, :], bank[4][0:B, :]))
                split3([rparts[:, i, :] for i in range(PARTS)], rrow[:, :]).then_inc(r_evac, 1)

            def values(i):
                dve.wait_ge(setup_mm, (i + 1) * (B + 2))
                for b in range(B):
                    v = bank[3][:, b * P:(b + 1) * P].rearrange("p (c h d) -> p c h d", c=HC, h=HPC)
                    dve.tensor_tensor(VB[:, b, :, 0:HPC * DK].rearrange("p c (h d) -> p c h d", h=HPC), v,
                                      chunk_mask[:, :].unsqueeze(1).unsqueeze(3).broadcast_to([P, HC, HPC, DK]), ALU.mult)
                    ins = dve.tensor_copy(VB[:, b, :, HPC * DK:VW], chunk_mask[:, :].unsqueeze(1).broadcast_to([P, HC, HPC]))
                ins.then_inc(setup_evac, 1)

            def attention(a):
                for s in range(TILES + 6):
                    if s < TILES:
                        dve.wait_ge(s_mm, a * TILES + s + 1)
                        sc = bank[s % 2][:, :].rearrange("p (h k) -> p h k", h=H)
                        link(dve.tensor_reduce(smax[:, s % 2, :], sc, AX.X, ALU.max))
                        dve.tensor_tensor(PR[:, s % 2, :].rearrange("p (h k) -> p h k", h=H), sc,
                                          smax[:, s % 2, :].unsqueeze(2).broadcast_to([P, H, K]),
                                          ALU.subtract).then_inc(s_sub, 1)
                    j = s - 5
                    if 0 <= j < TILES:
                        dve.wait_ge(wo_mm, a * TILES + j + 1)
                        dve.tensor_tensor(X[:, j, :], X[:, j, :], bank[7][:, 0:D], ALU.add).then_inc(x_added, 1)
                    if j >= 1:
                        dve.wait_ge(x_added, a * TILES + j)
                        ins = dve.bn_stats(stats[:, j - 1, :], X[:, j - 1, :])
                        if s == TILES + 2:
                            link(ins)
                    j = s - 2
                    if 0 <= j < TILES:
                        dve.wait_ge(o_mm, a * TILES + j + 1)
                        o = bank[4 + j % 2][:, 0:HC * VW].rearrange("p (c w) -> p c w", c=HC)
                        link(dve.reciprocal(rsum[:, j % 2, :].rearrange("p (c h) -> p c h", c=HC), o[:, :, HPC * DK:VW]))
                        dve.tensor_tensor(ON[:, j % 2, :].rearrange("p (c h d) -> p c h d", c=HC, h=HPC),
                                          o[:, :, 0:HPC * DK].rearrange("p c (h d) -> p c h d", h=HPC),
                                          rsum[:, j % 2, :].rearrange("p (c h) -> p c h", c=HC).unsqueeze(3)
                                          .broadcast_to([P, HC, HPC, DK]), ALU.mult).then_inc(o_norm, 1)
                    if s == TILES + 2:
                        ln_aggregate(half(0))
                        ln_rstd(GT)
                    if s == TILES + 3:
                        ln_scale(half(0), XNR[:, 0:GT, :], xn_ready)
                link(ins)
                ln_aggregate(half(1), GT)
                ln_rstd(GT)
                ln_scale(half(1), XNR[:, GT:TILES, :], xn_ready)

            def router(layer, g):
                r = layer * GROUPS + g
                flat = [P, GT, E]
                half_tiles = slice(g * GT, (g + 1) * GT)

                dve.wait_ge(lg_mm, r + 1)
                logits = bank[2 * g][:, 0:GT * E].rearrange("p (t e) -> p t e", e=E)
                if layer == 1:
                    link(dve.tensor_tensor(lg[:, :, :], logits, br_all[:, :].unsqueeze(1).broadcast_to(flat), ALU.add))
                else:
                    link(dve.tensor_copy(lg[:, :, :], logits))
                pref = prefer[:, :].unsqueeze(1).broadcast_to(flat)

                def first_of_max(src, mx, onehot):
                    link(dve.tensor_reduce(mx[:, :], src, AX.X, ALU.max))
                    link(dve.tensor_tensor(cand[:, :, :], src, mx[:, :].unsqueeze(2).broadcast_to(flat), ALU.is_equal))
                    link(dve.tensor_tensor(cand[:, :, :], cand[:, :, :], pref, ALU.mult))
                    link(dve.tensor_reduce(c1[:, :], cand[:, :, :], AX.X, ALU.max))
                    link(dve.tensor_tensor(onehot[:, :, :], cand[:, :, :], c1[:, :].unsqueeze(2).broadcast_to(flat),
                                           ALU.is_equal))

                first_of_max(lg[:, :, :], m1, oh1)
                link(dve.scalar_tensor_tensor(out=second[:, :, :], in0=oh1[:, :, :], scalar=-3.0e38, in1=lg[:, :, :],
                                              op0=ALU.mult, op1=ALU.add))
                first_of_max(second[:, :, :], m2, oh2)
                link(dve.tensor_tensor(both[:, g, :, :], oh1[:, :, :], oh2[:, :, :], ALU.add))
                link(dve.tensor_tensor(ahead_a[:, g, PAD + 1:, :], both[:, g, 1:, :], both[:, g, 0:GT - 1, :], ALU.add))
                link(dve.tensor_copy(ahead_a[:, g, PAD, :], both[:, g, 0, :]))
                link(dve.tensor_tensor(ahead_b[:, g, PAD:, :], ahead_a[:, g, PAD:, :], ahead_a[:, g, PAD - 2:-2, :], ALU.add))
                dve.tensor_tensor(ahead_a[:, g, PAD:, :], ahead_b[:, g, PAD:, :], ahead_b[:, g, 0:GT, :],
                                  ALU.add).then_inc(both_ready, 1)
                dve.tensor_tensor(dl[:, :, :], lg[:, :, :], m1[:, :].unsqueeze(2).broadcast_to(flat), ALU.subtract)
                dve.tensor_tensor(de[:, :], m2[:, :], m1[:, :], ALU.subtract).then_inc(dl_ready, 1)
                dve.wait_ge(rank_mm, r + 1)
                rank, count = bank[2 * g + 1][:, 0:GT * E], bank[2 * g + 1][:, GT * E:(GT + 1) * E]
                link(dve.tensor_scalar(cnt[:, :], count, 1.0 / P, (P - 1) / P - 0.5 + 0.5 / P, ALU.mult, ALU.add))
                link(dve.tensor_scalar(cnt[:, :], cnt[:, :], ROUND, -ROUND, ALU.add, ALU.add))
                link(dve.tensor_tensor(inc_a[:, PAD + 1:], cnt[:, 1:E], cnt[:, 0:E - 1], ALU.add))
                link(dve.tensor_copy(inc_a[:, PAD:PAD + 1], cnt[:, 0:1]))
                link(dve.tensor_tensor(inc_b[:, PAD:], inc_a[:, PAD:], inc_a[:, PAD - 2:-2], ALU.add))
                link(dve.tensor_tensor(inc_a[:, PAD:], inc_b[:, PAD:], inc_b[:, 0:E], ALU.add))
                link(dve.tensor_tensor(start_f[:, :], inc_a[:, PAD:], cnt[:, :], ALU.subtract))
                link(dve.tensor_scalar(start_f[:, :], start_f[:, :], float(P), None, ALU.mult))
                link(dve.tensor_tensor(place[:, :, :], rank.rearrange("p (t e) -> p t e", e=E),
                                       start_f[:, :].unsqueeze(1).broadcast_to(flat), ALU.add))
                for k, oh in enumerate((oh1, oh2)):
                    link(dve.tensor_tensor(pick[:, :, :], place[:, :, :], oh[:, :, :], ALU.mult))
                    link(dve.tensor_reduce(slot_f[:, k, :], pick[:, :, :], AX.X, ALU.add))
                dve.tensor_copy(slot_i[:, :, half_tiles], slot_f[:, :, :]).then_inc(routed, 1)
                tiles = [1, NT, E]
                link(dve.tensor_tensor(le[:, :, :], tile_no[:, :, :],
                                       inc_a[0:1, PAD:].unsqueeze(1).broadcast_to(tiles), ALU.is_ge))
                link(dve.tensor_reduce(eid_f[:, :], le[:, :, :], AX.X, ALU.add))
                link(dve.tensor_scalar(eid_c[:, :], eid_f[:, :], float(E - 1), None, ALU.min))
                dve.tensor_copy(eid_i[:, g * NT:(g + 1) * NT], eid_c[:, :]).then_inc(experts_known, 1)
                dve.wait_ge(experts_known, r + 1)
                dve.wait_ge(ex_ready, r + 1)
                link(dve.tensor_reduce(es[:, :], ex[:, :, :], AX.X, ALU.add))
                link(dve.reciprocal(pr1[:, :], es[:, :]))
                link(dve.tensor_tensor(pr2[:, :], e2[:, :], pr1[:, :], ALU.mult))
                link(dve.tensor_tensor(den[:, :], pr1[:, :], pr2[:, :], ALU.add))
                link(dve.tensor_scalar(den[:, :], den[:, :], 1e-9, None, ALU.max))
                link(dve.reciprocal(den[:, :], den[:, :]))
                dve.tensor_tensor(gates[:, 0, half_tiles], pr1[:, :], den[:, :], ALU.mult)
                link(dve.tensor_tensor(gates[:, 1, half_tiles], pr2[:, :], den[:, :], ALU.mult))

            def experts(layer):
                L = MOE[layer]
                f = L["f"]
                nc_f = f // P
                base = layer * SLOTS
                y_banks = y_banks_of(L)

                def x_low(t, s):
                    dve.wait_ge(ex_xh, t + base + 1)
                    dve.tensor_tensor(xl[s][:, :], bank[6][:, 0:P], xh[s][:, :].bitcast(F32), ALU.subtract).then_inc(ex_xl, 1)

                def multiply(t, s):
                    if L["up"] > f:
                        dve.wait_ge(ex_act, t + base + 1)
                        dve.tensor_tensor(hb[s][:, :], gb[s][:, :], bank[2 + s][:, :], ALU.mult).then_inc(ex_mul, 1)

                def h_low(t, s):
                    dve.wait_ge(ex_hh, t + base + 1)
                    dve.tensor_tensor(hl[s][:, 0:nc_f, :], bank[4 + s][:, 0:f].rearrange("p (c t) -> p c t", c=nc_f),
                                      hh[s][:, 0:nc_f, :].bitcast(F32), ALU.subtract).then_inc(ex_hl, 1)

                def y_copy(t, s, turn):
                    if layer or not isinstance(turn, int) or turn:
                        dve.wait_ge(y_stored[s], 16 * (layer * uses(SLOTS, s)) + 16 * turn)
                    dve.wait_ge(ex_dn, t + base + 1)
                    y = y_banks[s % len(y_banks)]
                    dve.tensor_reduce(Y[:, s, :], y[:, 0:2 * D].rearrange("p (k d) -> p d k", k=2), AX.X,
                                      ALU.add).then_inc(ex_y, 1)

                def step(i, u):
                    t = RING * i + u
                    x_low(t + 3, (u + 1) % 2)
                    multiply(t + 2, u % 2)
                    h_low(t + 1, (u + 1) % 2)
                    y_copy(t, u, i)

                x_low(0, 0)
                x_low(1, 1)
                multiply(0, 0)
                x_low(2, 0)
                multiply(1, 1)
                h_low(0, 0)
                for u in range(RING):
                    step(0, u)
                with dve.Fori(1, ROUNDS) as i:
                    for u in range(RING):
                        step(i, u)
                for u in range(STEPS % RING):
                    step(ROUNDS, u)
                multiply(SLOTS - 1, (SLOTS - 1) % 2)
                h_low(SLOTS - 2, (SLOTS - 2) % 2)
                y_copy(SLOTS - 3, (SLOTS - 3) % RING, (SLOTS - 3) // RING)
                h_low(SLOTS - 1, (SLOTS - 1) % 2)
                y_copy(SLOTS - 2, (SLOTS - 2) % RING, (SLOTS - 2) // RING)
                y_copy(SLOTS - 1, (SLOTS - 1) % RING, (SLOTS - 1) // RING)

            def combine(m):
                g = m % GROUPS
                for k, src in enumerate((XNR[:, g * GT:(g + 1) * GT, :], YG[g][:, :, :])):
                    dve.wait_ge(gathered[g][k], 16 * GT * (m // GROUPS + 1))
                    for j in range(GT):
                        t = g * GT + j
                        ins = dve.scalar_tensor_tensor(out=X[:, t, :], in0=src[:, j, :], scalar=gates[:, k, t:t + 1],
                                                       in1=X[:, t, :], op0=ALU.mult, op1=ALU.add)
                    if k < TOPK - 1:
                        link(ins)
                ins.then_inc(combined, 1)
                dve.wait_ge(combined, m + 1)

            def setup1():
                dve.wait_ge(in_col, 16)
                dve.wait_ge(s1_mm, 1)
                dve.tensor_scalar(kT[:, :, :], bank[6][:, 0:P].rearrange("p (b k) -> p b k", b=B), bk1, None,
                                  ALU.add).then_inc(s1_evac, 1)
                dve.wait_ge(s1_mm, 4)
                dve.tensor_copy(M1[:, :, :], bank[4][:, 0:P].rearrange("p (b k) -> p b k", b=B))
                dve.tensor_copy(br_all[:, :], bank[5][:, P:P + E])
                dve.tensor_copy(r1[:, :, :], bank[5][:, 0:P].rearrange("p (b k) -> p b k", b=B))
                link(dve.tensor_copy(V1[:, :, :], bank[7][0:K, :].rearrange("p (b d) -> p b d", b=B)))
                dve.sem_inc(s1_evac, 1)

            def attention1_softmax(g):
                columns = slice(g * GT * K, (g + 1) * GT * K)
                sc = PR[:, 0, columns].rearrange("p (t k) -> p t k", k=K)
                pr = PR[:, 1, columns].rearrange("p (t k) -> p t k", k=K)
                top, total = l1_max[:, 0:GT], l1_sum[:, 0:GT]
                dve.wait_ge(a1_s, g + 1)
                link(dve.tensor_tensor(PR[:, 1, columns].rearrange("p (b t k) -> p b t k", b=GB, t=BT),
                                       bank[0][:, columns].rearrange("p (b t k) -> p b t k", b=GB, t=BT),
                                       r1[:, g * GB:(g + 1) * GB, :].unsqueeze(2).broadcast_to([P, GB, BT, K]), ALU.add))
                link(dve.tensor_reduce(top, pr, AX.X, ALU.max))
                dve.tensor_tensor(sc, pr, top.unsqueeze(2).broadcast_to([P, GT, K]), ALU.subtract).then_inc(a1_sub, 1)
                if g == 0:
                    ternary_weights()
                dve.wait_ge(a1_exp, g + 1)
                link(dve.tensor_reduce(total, sc, AX.X, ALU.add))
                link(dve.reciprocal(total, total))
                dve.tensor_tensor(pr, sc, total.unsqueeze(2).broadcast_to([P, GT, K]), ALU.mult).then_inc(a1_p, 1)

            def attention1_add(g):
                batches = range(g * GB, (g + 1) * GB)
                for b in batches:
                    dve.wait_ge(a1_o, b + 1)
                    xv = X[:, b * BT:(b + 1) * BT, :]
                    dve.tensor_tensor(xv, xv, bank[4 + b][:, :].rearrange("p (t d) -> p t d", d=D),
                                      ALU.add).then_inc(a1_added, 1)
                dve.wait_ge(a1_added, batches[-1] + 1)

            def mean_value():
                dve.wait_ge(s2_mm, 5)
                dve.tensor_copy(vo[:, :], bank[4][:, 0:D]).then_inc(s2_evac, 1)

            def masked_result():
                dve.wait_ge(s2_mm, 6)
                dve.tensor_copy(U[:, :, :], bank[5][:, :].rearrange("p (b d) -> p b d", b=B)).then_inc(s2_evac, 1)

            def quantise_x(first, count):
                def of_batches(a):
                    return a.rearrange("p (b t) d -> p b t d", b=B)[:, :, first:first + count, :]

                tiles = [b * BT + i for b in range(B) for i in range(first, first + count)]
                nt = len(tiles)
                top, scale, inv = amax[:, 0:nt], qscale[:, 0:nt], qinv[:, 0:nt]
                ln_stats(tiles)
                ln_aggregate(tiles)
                ln_rstd(nt)
                for j, t in enumerate(tiles):
                    ins = dve.tensor_scalar(XQ[:, t, :], X[:, t, :], mv[:, j, 0:1], rstd[:, j:j + 1], ALU.subtract, ALU.mult)
                link(ins)
                link(dve.tensor_reduce(top.rearrange("p (b t) -> p b t", b=B), of_batches(XQ[:, :, :]), AX.X, ALU.max,
                                       apply_absolute_value=True))
                link(dve.tensor_scalar(top, top, 1e-5, None, ALU.max))
                link(dve.reciprocal(scale, top))
                dve.tensor_scalar(inv, top, 1.0 / 127.0, None, ALU.mult)
                link(dve.tensor_scalar(scale, scale, 127.0, None, ALU.mult))
                for j, t in enumerate(tiles):
                    ins = dve.tensor_scalar(XQ[:, t, :], XQ[:, t, :], qscale[:, j:j + 1], ROUND, ALU.mult, ALU.add)
                link(ins)
                for j, t in enumerate(tiles):
                    dve.tensor_scalar(XQ[:, t, :], XQ[:, t, :], ROUND, qinv[:, j:j + 1], ALU.subtract, ALU.mult).then_inc(f2_xq, 1)

            def xattn2():
                layer_norm([b * BT for b in range(B)], XNR[:, 0:B, :], x2_n)
                query_bias_rows()
                values(1)
                dve.wait_ge(x2_q, 1)
                for c in range(2):
                    ins = dve.tensor_tensor(kq[:, c * 512:(c + 1) * 512], kall[:, c * 512:(c + 1) * 512], bank[c][:, :], ALU.mult)
                link(ins)
                link(dve.tensor_reduce(s16[:, :], kq.rearrange("p (h d) -> p h d", h=HL), AX.X, ALU.add))
                link(dve.tensor_scalar(s16[:, :], s16[:, :], float(DL) ** -0.5, None, ALU.mult))
                link(dve.tensor_scalar(m16[:, :], s16[:, :], NEG, None, ALU.max))
                dve.tensor_tensor(e16[:, 0, :], s16[:, :], m16[:, :], ALU.subtract)
                dve.tensor_scalar(e16[:, 1, :], m16[:, :], -1.0, NEG, ALU.mult, ALU.add).then_inc(x2_m, 1)
                dve.wait_ge(x2_e, 1)
                link(dve.scalar_tensor_tensor(out=sum16[:, :], in0=e16[:, 1, :], scalar=float(K - 1),
                                              in1=e16[:, 0, :], op0=ALU.mult, op1=ALU.add))
                link(dve.reciprocal(sum16[:, :], sum16[:, :]))
                link(dve.tensor_tensor(e16[:, :, :], e16[:, :, :],
                                       sum16[:, :].unsqueeze(1).broadcast_to([P, 2, HL]), ALU.mult))
                link(dve.tensor_tensor(s16[:, :], e16[:, 0, :], e16[:, 1, :], ALU.subtract))

                def heads(a):
                    return a.rearrange("p (h d) -> p h d", h=HL)

                dve.tensor_tensor(heads(attn2[:, :]), heads(vall[:, :]),
                                  s16[:, :].unsqueeze(2).broadcast_to([P, HL, DL]), ALU.mult)
                link(dve.tensor_tensor(heads(kq), heads(vsum[:, :]),
                                       e16[:, 1, :].unsqueeze(2).broadcast_to([P, HL, DL]), ALU.mult))
                dve.tensor_tensor(attn2[:, :], attn2[:, :], kq, ALU.add).then_inc(x2_o, 1)
                for b in range(B):
                    t = b * BT
                    dve.tensor_tensor(X[:, t + 1:t + BT, :], X[:, t + 1:t + BT, :],
                                      U[:, b, :].unsqueeze(1).broadcast_to([P, BT - 1, D]), ALU.add)
                    ins = dve.scalar_tensor_tensor(out=X[:, t, :], in0=U[:, b, :], scalar=late[:, :], in1=X[:, t, :],
                                                   op0=ALU.mult, op1=ALU.add)
                link(ins)
                dve.wait_ge(rows_out, 16)
                quantise_x(1, BT - 1)
                dve.wait_ge(x2_mm, 1)
                xv = X[0:K, :, :].rearrange("p (b t) d -> p b t d", b=B)[:, :, 0, :]
                dve.tensor_tensor(xv, xv, bank[5][0:K, :].rearrange("p (b d) -> p b d", b=B), ALU.add).then_inc(x2_added, 1)
                dve.wait_ge(x2_added, 1)

            def weight_sums():
                dve.wait_ge(in_ff2, 64)
                dve.tensor_reduce(wmean[:, 0, 0:1], w1_s[:, :], AX.X, ALU.add, apply_absolute_value=True)
                dve.tensor_reduce(wmean[:, 0, 1:2], w2_s[:, :, :], AX.XY, ALU.add, apply_absolute_value=True).then_inc(fs_sum, 1)

            def ternary_weights():
                dve.wait_ge(fs_mm, 1)
                mean, scale = wmean[:, 1, 0:2], wmean[:, 1, 2:4]
                dve.tensor_scalar(mean, bank[0][:, GT * K:GT * K + 2], 1.0 / (D * F2), 1e-5, ALU.mult, ALU.max).then_inc(fs_read, 1)
                dve.wait_ge(fs_read, 1)
                link(dve.reciprocal(scale, mean))
                w2v = w2_s[:, :, :]
                dve.tensor_scalar(w2v, w2v, scale[:, 1:2], ROUND, ALU.mult, ALU.add)
                link(dve.tensor_scalar(w1_s[:, :], w1_s[:, :], scale[:, 0:1], ROUND, ALU.mult, ALU.add))
                dve.tensor_scalar(w2v, w2v, ROUND, 1.0, ALU.subtract, ALU.min)
                link(dve.tensor_scalar(w1_s[:, :], w1_s[:, :], ROUND, 1.0, ALU.subtract, ALU.min))
                dve.tensor_scalar(w2q[:, :, :], w2v, -1.0, None, ALU.max)
                link(dve.tensor_scalar(w1_s[:, :], w1_s[:, :], -1.0, mean[:, 0:1], ALU.max, ALU.mult))
                dve.wait_ge(fs_taps, 1)
                for j in range(TAPS):
                    ins = dve.tensor_tensor(Z[:, j, :], w1_s[:, :], bank[1 + j][:, :], ALU.mult)
                link(ins)

            def split_taps():
                link(dve.tensor_copy(w1c_h[:, :, :], Z[:, 0:TAPS, :]))
                dve.tensor_tensor(w1c_l[:, :, :], Z[:, 0:TAPS, :], w1c_h[:, :, :].bitcast(F32), ALU.subtract).then_inc(fs_ready, 1)

            def ffn2():
                for t in (xqh, xql):
                    dve.memset(t[:, :, 0:1].bitcast(F32), 0.0)
                    dve.memset(t[:, :, S + 1:S + 2].bitcast(F32), 0.0)

                def x_low(b):
                    dve.wait_ge(f2_xh, b + 1)
                    dve.tensor_tensor(xql[:, b % 2, 1:S + 1], bank[6][:, :], xqh[:, b % 2, 1:S + 1].bitcast(F32),
                                      ALU.subtract).then_inc(f2_xl, 1)

                def quantise(p):
                    dve.wait_ge(f2_z, 2 * p + 2)
                    z = Z[:, 2 * p % ZBUFS:2 * p % ZBUFS + 2, :]
                    link(dve.tensor_reduce(zmax[:, :], z, AX.X, ALU.max, apply_absolute_value=True))
                    link(dve.tensor_scalar(zmax[:, :], zmax[:, :], 1e-5, None, ALU.max))
                    link(dve.reciprocal(zscale[:, :], zmax[:, :]))
                    dve.tensor_scalar(zinv[:, 2 * p:2 * p + 2], zmax[:, :], 1.0 / 127.0, wmean[:, 1, 1:2], ALU.mult, ALU.mult)
                    link(dve.tensor_scalar(zscale[:, :], zscale[:, :], 127.0, None, ALU.mult))
                    for i in range(2):
                        ins = dve.tensor_scalar(z[:, i, :], z[:, i, :], zscale[:, i:i + 1], ROUND, ALU.mult, ALU.add)
                    link(ins)
                    if p:
                        dve.wait_ge(f2_qt, 2 * p)
                    for i in range(2):
                        dve.tensor_scalar(zq[:, i, :], z[:, i, :], ROUND, 127.0, ALU.subtract, ALU.min).then_inc(f2_zq, 1)

                def add(p):
                    dve.wait_ge(f2_dn, p + 1)
                    for i in (2 * p, 2 * p + 1):
                        dve.scalar_tensor_tensor(out=X[:, i, :], in0=bank[7][:, i % 2 * D:(i % 2 + 1) * D], scalar=zinv[:, i:i + 1],
                                                 in1=X[:, i, :], op0=ALU.mult, op1=ALU.add).then_inc(f2_added, 1)

                quantise_x(0, 1)
                x_low(0)

                def pair_stats(p):
                    for i in (2 * p, 2 * p + 1):
                        ins = dve.bn_stats(stats[:, i, :], X[:, i, :])
                    return ins

                for p in range(TILES // 2 + 2):
                    if p % 2 == 0 and p // 2 + 1 < B:
                        x_low(p // 2 + 1)
                    if p >= 2:
                        add(p - 2)
                    if p < TILES // 2:
                        quantise(p)
                    if p == 2:
                        dve.wait_ge(in_mask3, 16)
                        link(dve.tensor_scalar(mfill[:, :], mask3_i, 0, FILL, ALU.is_equal, ALU.mult))
                        dve.memset(mfill[0:PARTS, :], 1.0).then_inc(mrow_ready, 1)
                    if p >= 3:
                        dve.wait_ge(f2_added, 2 * p - 4)
                        pair_stats(p - 3)
                dve.wait_ge(f2_added, TILES)
                link(pair_stats(TILES // 2 - 1))
                ln_aggregate(everything)
                ln_rstd(TILES)
                ln_scale(everything, XNR[:, :, :], xn_ready)

            dve.wait_ge(in_x[0], 16)
            for t in half(0):
                dve.bn_stats(stats[:, t, :], X[:, t, :])
            dve.wait_ge(in_w0, 16)
            dve.wait_ge(const_ready, 1)
            keys(0)
            dve.tensor_copy(ctx4[:, :, :, :], ctxT.rearrange("p (b k) -> p b k", b=B).unsqueeze(2)
                            .broadcast_to([P, B, HPC, K])).then_inc(ctx4_ready, 1)
            dve.wait_ge(in_x[1], 16)
            for t in half(1):
                ins = dve.bn_stats(stats[:, t, :], X[:, t, :])
            link(ins)
            ln_aggregate(everything)
            mask_row()
            ln_rstd(TILES)
            ln_scale(everything, XNR[:, :, :], xn_ready)
            values(0)
            split_biases()
            attention(0)
            dve.wait_ge(const_ready, 2)
            for g in range(GROUPS):
                router(0, g)
            setup1()
            experts(0)
            XN0, XN1 = XNR[:, 0:GT, :], XNR[:, GT:TILES, :]
            combine(0)
            layer_norm(half(0), XN0, xn_ready)
            weight_sums()
            attention1_softmax(0)
            combine(1)
            attention1_add(0)
            layer_norm(everything, XNR[:, :, :], xn_ready)
            router(1, 0)
            attention1_softmax(1)
            attention1_add(1)
            layer_norm(half(1), XN1, xn_ready)
            router(1, 1)
            experts(1)
            combine(GROUPS)
            keys(1)
            mean_value()
            masked_result()
            dve.wait_ge(s2_evac, 2)
            split_taps()
            combine(GROUPS + 1)
            xattn2()
            ffn2()
            attention(1)
            for g in range(GROUPS):
                router(2, g)
            experts(2)
            for g in range(GROUPS):
                combine(2 * GROUPS + g)

        @block.tensor
        def _(pe):
            def keys(wk):
                pe.matmul(bank[0][:, 0:P], wk, ctxT, start=True, stop=True).then_inc(setup_mm, 1)

            def setup(i, wq, wv):
                ev = i * (B + 1)
                for b in range(B):
                    batch_keys = kbd[:, b, :, :].rearrange("p h k -> p (h k)")
                    pe.wait_ge(setup_evac, ev + b + 1)
                    if b >= 2:
                        pe.wait_ge(m_evac, i * B + b - 1)
                    pe.matmul(bank[1 + b % 2][:, :], wq, batch_keys, start=True, stop=True).then_inc(setup_mm, 1)
                    if i:
                        ins = pe.matmul(bank[4][0:B, :], bq_cols[:, b, :], batch_keys, start=(b == 0), stop=(b == B - 1))
                        if b == B - 1:
                            ins.then_inc(r_mm, 1)
                pe.wait_ge(ctx4_ready, 1)
                for b in range(B):
                    dst = bank[3][:, b * P:(b + 1) * P]
                    ins = pe.matmul(dst, ctx4[:, b, :, :].rearrange("p h k -> p (h k)"), wv, start=True, stop=(i == 0))
                    if i:
                        ins = pe.matmul(dst, ones_row[:, :], bv3, start=False, stop=True)
                ins.then_inc(setup_mm, 1)

            def setup1():
                pe.wait_ge(in_w1, 16)
                pe.wait_ge(in_col, 16)
                pe.wait_ge(in_row, 16)
                pe.matmul(bank[6][:, 0:P], wk1, ctxT, start=True, stop=True).then_inc(s1_mm, 1)
                pe.wait_ge(s1_evac, 1)
                keys = kT[:, :, :].rearrange("p b k -> p (b k)")
                pe.matmul(bank[4][:, 0:P], wq1, keys, start=True, stop=True).then_inc(s1_mm, 1)
                pe.matmul(bank[5][:, 0:P], bq1.broadcast_to([P, P]), keys, start=True, stop=True)
                pe.matmul(bank[5][:, P:P + E], ones_row[:, :], br1, start=True, stop=True).then_inc(s1_mm, 1)
                for b in range(B):
                    dst = bank[7][0:K, b * D:(b + 1) * D]
                    pe.matmul(dst, ctxT[:, b * K:(b + 1) * K], wv1, start=True, stop=False)
                    ins = pe.matmul(dst, ones_row[:, 0:K], bv1, start=False, stop=True)
                ins.then_inc(s1_mm, 1)

            def attention1_scores(n, g):
                if g == 1:
                    pe.wait_ge(fs_read, 1)
                for j in range(g * GT, (g + 1) * GT):
                    b = j // BT
                    pe.wait_ge(xt_ready, turn_of(n, b) + 1)
                    ins = pe.matmul(bank[0][:, j * K:(j + 1) * K], XT[:, j, :], M1[:, b, :], start=True, stop=True)
                ins.then_inc(a1_s, 1)

            def attention1_values(g):
                batches = range(g * GB, (g + 1) * GB)
                pe.wait_ge(a1_p, g + 1)
                for b in batches:
                    for j in range(BT):
                        t = b * BT + j
                        ins = pe.transpose(bank[b % 4][0:K, j * P:(j + 1) * P], PR[:, 1, t * K:(t + 1) * K], ident[:, :])
                    ins.then_inc(a1_pt, 1)
                for b in batches:
                    pe.wait_ge(a1_ptc, b + 1)
                    for j in range(BT):
                        ins = pe.matmul(bank[4 + b][:, j * D:(j + 1) * D], PT1[:, b * BT + j, :], V1[:, b, :],
                                        start=True, stop=True)
                    ins.then_inc(a1_o, 1)

            def setup2():
                pe.wait_ge(ex_y, 2 * SLOTS)
                pe.wait_ge(in_l2, 48)
                for i in range(2):
                    for c in range(2):
                        ins = pe.matmul(bank[4 + 2 * i + c][:, :], ctxT, wkv_s[:, i * INNER + c * 512:i * INNER + (c + 1) * 512],
                                        start=True, stop=True)
                    ins.then_inc(s2_mm, 1)
                for c in range(2):
                    pe.wait_ge(s2_act, 3 + c)
                    ins = pe.matmul(bank[4 + c][:, :], batch_mask[:, :], vall[:, c * 512:(c + 1) * 512], start=True, stop=True)
                ins.then_inc(s2_mm, 1)
                for c in range(IC):
                    pe.wait_ge(s2_act, 5 + c // 4)
                    ins = pe.transpose(bank[6 + c // 4][:, c % 4 * P:(c % 4 + 1) * P], vsum[:, c * P:(c + 1) * P], ident[:, :])
                ins.then_inc(s2_mm, 1)
                for c in range(IC):
                    pe.wait_ge(s2_act, 7 + c // 4)
                    ins = pe.matmul(bank[4][:, 0:D], attn2[:, c * P:(c + 1) * P], wout_s[:, c, :], start=(c == 0), stop=(c == IC - 1))
                ins.then_inc(s2_mm, 1)

            def masked_result():
                pe.wait_ge(s2_evac, 1)
                for b in range(B):
                    dst = bank[5][:, b * D:(b + 1) * D]
                    pe.matmul(dst, ident[:, b * K:b * K + 1].broadcast_to([P, P]), vo[:, :], start=True, stop=False)
                    ins = pe.matmul(dst, ones_row[:, :], bout2, start=False, stop=True)
                ins.then_inc(s2_mm, 1)

            def xattn2():
                for b in range(B):
                    pe.wait_ge(x2_n, b + 1)
                    ins = pe.transpose(bank[6][:, b * K:(b + 1) * K], XNR[0:K, b, :], ident[0:K, 0:K])
                ins.then_inc(x2_t, 1)
                pe.wait_ge(x2_xl, 1)
                pe.wait_ge(m_evac, 2 * B)
                for c in range(2):
                    ins = pe.matmul(bank[c][:, :], XL[:, :], wq_s[:, c * 512:(c + 1) * 512], start=True, stop=True)
                ins.then_inc(x2_q, 1)
                pe.wait_ge(x2_o, 1)
                pe.wait_ge(setup_evac, 2 * (B + 1))
                pe.wait_ge(r_evac, 1)
                for c in range(IC):
                    ins = pe.transpose(bank[2 + c // 4][:, c % 4 * P:(c % 4 + 1) * P], attn2[:, c * P:(c + 1) * P], ident[:, :])
                    if c % 4 == 3:
                        ins.then_inc(x2_ot, 1)
                dst = bank[4][:, 0:B * K]
                for c in range(IC):
                    pe.wait_ge(x2_otc, c // 4 + 1)
                    pe.matmul(dst, wout_s[:, c, :], oT[:, c, :], start=(c == 0), stop=False)
                pe.matmul(dst, bout2, ones_row[:, :], start=False, stop=True).then_inc(x2_y, 1)
                pe.wait_ge(x2_yc, 1)
                pe.wait_ge(s2_evac, 2)
                for b in range(B):
                    ins = pe.transpose(bank[5][0:K, b * D:(b + 1) * D], XL[:, b * K:(b + 1) * K], ident[:, :])
                ins.then_inc(x2_mm, 1)

            def taps():
                pe.wait_ge(in_ff2, 64)
                for j in range(TAPS):
                    ins = pe.matmul(bank[1 + j][:, :], ident[0:TAPS, j:j + 1].broadcast_to([TAPS, P]), cw_s[:, :],
                                    start=True, stop=True)
                ins.then_inc(fs_taps, 1)

            def means():
                pe.wait_ge(fs_sum, 1)
                pe.matmul(bank[0][:, GT * K:GT * K + 2], ones_f[:, :], wmean[:, 0, 0:2], start=True, stop=True).then_inc(fs_mm, 1)

            def ffn2():
                def turn_x(b):
                    if b:
                        pe.wait_ge(f2_xl, b)
                    pe.wait_ge(f2_xq, TILES - B + b + 1)
                    for j in range(BT):
                        ins = pe.transpose(bank[6][:, j * P:(j + 1) * P], XQ[:, b * BT + j, :], ident[:, :])
                    ins.then_inc(f2_xt, 1)

                def up(i):
                    b, at = i // BT, i % BT * P
                    pe.wait_ge(f2_xl, b + 1)
                    if i >= 4:
                        pe.wait_ge(f2_z, i - 3)
                    dst = bank[i % 4][:, :]
                    for j in range(TAPS):
                        for k, (v, w) in enumerate(((xqh, w1c_h), (xqh, w1c_l), (xql, w1c_h))):
                            pe.matmul(dst, v[:, b % 2, at + j:at + j + P], w[:, j, :], start=(j == 0 and k == 0), stop=False)
                    pe.matmul(dst, ones_bf[0:PARTS, :], cb[:, :], start=False, stop=True).then_inc(f2_h, 1)

                def turn(i):
                    pe.wait_ge(f2_zq, i + 1)
                    if i >= 2:
                        pe.wait_ge(f2_qtc, i - 1)
                    zb = bank[4 + i % 2][:, 0:F2 // 2].bitcast(BF16)
                    for c in range(F2C):
                        ins = pe.transpose(zb[:, c * P:(c + 1) * P], zq[:, i % 2, c * P:(c + 1) * P], ident_bf[:, :])
                    ins.then_inc(f2_qt, 1)

                def down(p):
                    if p:
                        pe.wait_ge(f2_added, 2 * p)
                    for i in (2 * p, 2 * p + 1):
                        pe.wait_ge(f2_qtc, i + 1)
                        for c in range(F2C):
                            ins = pe.matmul(bank[7][:, i % 2 * D:(i % 2 + 1) * D], zqT[:, i % 2, c, :], w2q[:, c, :],
                                            start=(c == 0), stop=(c == F2C - 1))
                    ins.then_inc(f2_dn, 1)

                pe.wait_ge(fs_ready, 1)
                pe.wait_ge(const_ready, 2)
                turn_x(0)
                for p in range(TILES // 2 + 2):
                    if p % 2 == 0 and p // 2 + 1 < B:
                        turn_x(p // 2 + 1)
                    if p < TILES // 2:
                        up(2 * p)
                    if p >= 2:
                        down(p - 2)
                    if p < TILES // 2:
                        up(2 * p + 1)
                    if 1 <= p <= TILES // 2:
                        turn(2 * p - 2)
                        turn(2 * p - 1)

            def transposes(n, batches=range(B)):
                for q in batches:
                    for j in range(BT):
                        pe.wait_ge(xn_ready, turn_of(n, q) * BT + j + 1)
                        ins = pe.transpose(bank[4 + q][:, j * P:(j + 1) * P], XNR[:, q * BT + j, :], ident[:, :])
                    ins.then_inc(xt_mm, 1)

            def attention(a, n):
                def tokens_out(q):
                    pe.wait_ge(xt_ready, turn_of(n, q) + 1)

                def scores(s):
                    b = s // BT
                    tokens_out(b)
                    if s >= 2:
                        pe.wait_ge(s_sub, a * TILES + s - 1)
                    pe.matmul(bank[s % 2][:, :], XT[:, s, :], M[:, b, :], start=True, stop=False)
                    if a == 0:
                        ins = pe.matmul(bank[s % 2][:, :], ones_row_bf[:, :], mrow[:, b, :, :].rearrange("p h k -> p (h k)"),
                                        start=False, stop=True)
                    else:
                        ins = pe.matmul(bank[s % 2][:, :], mfill[:, s * P:(s + 1) * P], score_rows[:, b, :], start=False, stop=True)
                    ins.then_inc(s_mm, 1)

                pe.wait_ge(m_evac, (a + 1) * B)
                scores(0)
                for s in range(TILES + 5):
                    j = s - 1
                    if j == 0:
                        pe.wait_ge(setup_evac, (a + 1) * (B + 1))
                    if 0 <= j < TILES:
                        pe.wait_ge(s_exp, a * TILES + j + 1)
                        if j >= 2:
                            pe.wait_ge(pt_ready, a * TILES + j - 1)
                        for c in range(HC):
                            ins = pe.transpose(bank[2 + j % 2][:, c * P:(c + 1) * P], PR[:, j % 2, c * P:(c + 1) * P], ident[:, :])
                        ins.then_inc(pt_mm, 1)
                    j = s - 2
                    if 0 <= j < TILES:
                        b = j // BT
                        pe.wait_ge(pt_ready, a * TILES + j + 1)
                        if j < 2:
                            tokens_out(j)
                        else:
                            pe.wait_ge(o_norm, a * TILES + j - 1)
                        for c in range(HC):
                            ins = pe.matmul(bank[4 + j % 2][:, c * VW:(c + 1) * VW], PT[:, j % 2, c, :], VB[:, b, c, :],
                                            start=True, stop=True)
                        ins.then_inc(o_mm, 1)
                    if s + 1 < TILES:
                        scores(s + 1)
                    j = s - 3
                    if 0 <= j < TILES:
                        pe.wait_ge(o_norm, a * TILES + j + 1)
                        if j:
                            pe.wait_ge(ot_ready, a * TILES + j)
                        else:
                            tokens_out(2)
                        pe.transpose(bank[6][:, 0:P], ON[:, j % 2, :], ident[:, :]).then_inc(ot_mm, 1)
                    j = s - 4
                    if 0 <= j < TILES:
                        pe.wait_ge(ot_ready, a * TILES + j + 1)
                        if j:
                            pe.wait_ge(x_added, a * TILES + j)
                        else:
                            tokens_out(3)
                        if a == 0:
                            ins = pe.matmul(bank[7][:, 0:D], OT[:, j % 2, :], wo0, start=True, stop=True)
                        else:
                            pe.matmul(bank[7][:, 0:D], OT[:, j % 2, :], wo3, start=True, stop=False)
                            ins = pe.matmul(bank[7][:, 0:D], ones_bf[0:PARTS, :], bo_rows[:, :], start=False, stop=True)
                        ins.then_inc(wo_mm, 1)

            def logits(n, g, gate_w):
                transposes(n, range(g * GB, (g + 1) * GB))
                for j in range(GT):
                    t = g * GT + j
                    pe.wait_ge(xt_ready, turn_of(n, t // BT) + 1)
                    ins = pe.matmul(bank[2 * g][:, j * E:(j + 1) * E], XT[:, t, :], gate_w, start=True, stop=True)
                ins.then_inc(lg_mm, 1)

            def ranks(layer, g):
                pe.wait_ge(both_ready, layer * GROUPS + g + 1)
                rank, count = bank[2 * g + 1][:, 0:GT * E], bank[2 * g + 1][:, GT * E:(GT + 1) * E]
                pe.matmul(rank, before_bf[:, :], both[:, g, :, :].rearrange("p t e -> p (t e)"), start=True, stop=False)
                pe.matmul(rank, ones_bf[:, :], ahead_a[:, g, PAD - 1:-1, :].rearrange("p t e -> p (t e)"),
                          start=False, stop=True)
                pe.matmul(count, ones_bf[:, :], ahead_a[:, g, PAD + GT - 1, :], start=True, stop=True).then_inc(rank_mm, 1)

            def router(layer, n, gate_w):
                for g in range(GROUPS):
                    logits(n, g, gate_w)
                for g in range(GROUPS):
                    ranks(layer, g)

            def experts(layer, up, dn):
                L = MOE[layer]
                f, fu = L["f"], L["up"]
                nc_f = f // P
                base = layer * SLOTS
                y_banks = y_banks_of(L)

                def tr_x(t, s4, turn):
                    pe.wait_ge(x_loaded[s4], 16 * (layer * uses(SLOTS, s4)) + 16 * (turn + 1))
                    if layer or not isinstance(t, int) or t:
                        pe.wait_ge(ex_xl, t + base)
                    pe.transpose(bank[6][:, 0:P], xrow[s4][:, :], ident[:, :]).then_inc(ex_t, 1)

                def up_mm(t, s, e, waited=False):
                    if not waited:
                        pe.wait_ge(ex_xl, t + base + 1)
                    for k in range(fu // f):
                        wh, wl = (up[k][:, bass.ds(e, 1), i, 0:f].rearrange("p a f -> p (a f)") for i in range(2))
                        dst = bank[2 * k + s][:, 0:f]
                        pe.matmul(dst, xh[s][:, :], wh, start=True, stop=False)
                        pe.matmul(dst, xh[s][:, :], wl, start=False, stop=False)
                        ins = pe.matmul(dst, xl[s][:, :], wh, start=False, stop=not L["bias"])
                        if L["bias"]:
                            ins = pe.matmul(dst, ones_bf[0:PARTS, :], bias1[:, bass.ds(e, 1), :].rearrange("p a f -> p (a f)"),
                                            start=False, stop=True)
                    ins.then_inc(ex_up, 1)

                def tr_h(t, s):
                    if fu > f:
                        pe.wait_ge(ex_mul, t + 1)
                    else:
                        pe.wait_ge(ex_act, t + base + 1)
                    for c in range(nc_f):
                        ins = pe.transpose(bank[4 + s][:, c * P:(c + 1) * P], hb[s][:, c * P:(c + 1) * P], ident[:, :])
                    ins.then_inc(ex_ht, 1)

                def dn_mm(t, s, e):
                    pe.wait_ge(ex_hl, t + base + 1)
                    if layer or not isinstance(t, int) or t >= len(y_banks):
                        pe.wait_ge(ex_y, t + (base + 1 - len(y_banks)))
                    y = y_banks[s % len(y_banks)][:, 0:2 * D]
                    for c in range(nc_f):
                        w = dn[:, bass.ds(e, 1), :, c * P:(c + 1) * P].rearrange("p a k d -> p (a k) d")
                        pe.matmul(y, hh[s][:, c, :], w, start=(c == 0), stop=False, skip_group_check=True)
                        ins = pe.matmul(y, hl[s][:, c, :], w, start=False, stop=(c == nc_f - 1), skip_group_check=True)
                    if L["bias"]:
                        ins = pe.matmul(y[:, 0:D], ones_bf[0:PARTS, :], bias2[:, bass.ds(e, 1), :].rearrange("p a f -> p (a f)"),
                                        start=False, stop=True, skip_group_check=True)
                    ins.then_inc(ex_dn, 1)

                def experts_of(t, count):
                    _, values = nc.values_load_multi_w_load_instructions(
                        eid_i[0:1, bass.ds(t, count)], engines=[mybir.EngineType.PE], min_val=0, max_val=E - 1,
                        skip_runtime_bounds_check_because="the numbers are clamped where they are made", bass_reorder=False)
                    return values

                pe.wait_ge(experts_known, GROUPS * (layer + 1))
                e0, e1 = experts_of(0, 2)
                tr_x(0, 0, 0)
                tr_x(1, 1, 0)
                up_mm(0, 0, e0)
                tr_x(2, 2, 0)
                up_mm(1, 1, e1)
                tr_h(0, 0)

                def step(i, u, ids):
                    t = RING * i + u
                    tr_x(t + 3, (u + 3) % RING, i + (u + 3) // RING)
                    up_mm(t + 2, u % 2, ids[u + 2], waited=True)
                    tr_h(t + 1, (u + 1) % 2)
                    dn_mm(t, u % 2, ids[u])

                ids = experts_of(0, RING + 2)
                for u in range(RING):
                    step(0, u, ids)
                with pe.Fori(1, ROUNDS) as i:
                    ids = experts_of(RING * i, RING + 2)
                    for u in range(RING):
                        step(i, u, ids)
                ids = experts_of(ROUNDS * RING, SLOTS - ROUNDS * RING)
                for u in range(STEPS % RING):
                    step(ROUNDS, u, ids)
                up_mm(SLOTS - 1, (SLOTS - 1) % 2, ids[-1])
                tr_h(SLOTS - 2, (SLOTS - 2) % 2)
                dn_mm(SLOTS - 3, (SLOTS - 3) % 2, ids[-3])
                tr_h(SLOTS - 1, (SLOTS - 1) % 2)
                dn_mm(SLOTS - 2, (SLOTS - 2) % 2, ids[-2])
                dn_mm(SLOTS - 1, (SLOTS - 1) % 2, ids[-1])

            pe.wait_ge(const_ready, 1)
            pe.wait_ge(in_w0, 16)
            keys(wk0)
            setup(0, wq0, wv0)
            transposes(0)
            pe.wait_ge(mrow_ready, 1)
            attention(0, 0)
            router(0, 1, gate0)
            setup1()
            pe.wait_ge(w_split, 2 * E)
            experts(0, [WA], WB)
            taps()
            pe.wait_ge(s1_evac, 2)
            transposes(2, range(GB))
            means()
            attention1_scores(2, 0)
            attention1_values(0)
            logits(3, 0, gate1)
            transposes(2, range(GB, B))
            ranks(1, 0)
            attention1_scores(2, 1)
            attention1_values(1)
            logits(3, 1, gate1)
            ranks(1, 1)
            pe.wait_ge(in_rows, 32)
            pe.wait_ge(w_split, 4 * E)
            experts(1, [WC[:, :, :, 0:256]], WC[:, :, :, 256:512])
            pe.wait_ge(in_w3, 16)
            keys(wk3)
            setup2()
            masked_result()
            setup(1, wq3, wv3)
            xattn2()
            ffn2()
            transposes(4)
            pe.wait_ge(in_key_rows, 16)
            pe.wait_ge(mrow_ready, 2)
            attention(1, 4)
            router(2, 5, gate3)
            pe.wait_ge(w_split, 7 * E)
            experts(2, [WC, WA], WB)


def kernel(**inputs):
    import numpy as _np
    import concourse.bacc as _bacc
    from concourse import mybir as _mybir
    from concourse.bass_utils import run_bass_kernel_spmd as _run

    a = {k: _np.asarray(v) for k, v in inputs.items()}
    ctxT = a["ctx_1024"].reshape(-1, 128).T
    columns = [a[k][:, None] for k in ("L1_xattn_bq", "L1_xattn_bk", "L3_xattn_bq", "L3_xattn_bk")]
    arrays = {
        "p0": _np.concatenate([ctxT, a["L0_xattn_Wk"].T, a["L0_xattn_Wq"], a["L0_xattn_Wv"].T, a["L0_xattn_Wo"].T,
                               a["L0_ffn_gate_w"]], axis=1),
        "p1": _np.concatenate([a["L1_xattn_Wk"].T, a["L1_xattn_Wq"], a["L1_xattn_Wv"].T, a["L1_ffn_Wr"]], axis=1),
        "p3": _np.concatenate([a["L3_xattn_Wk"], a["L3_xattn_Wq"].T, a["L3_xattn_Wv"], a["L3_xattn_Wo"],
                               a["L3_ffn_w_gate"]], axis=1),
        "cols": _np.concatenate(columns, axis=1),
        "rows": _np.concatenate([a["L1_xattn_bv"], a["L3_xattn_bv"], a["L2_xattn_bout"],
                                 a["L1_ffn_br"]])[None],
        "bias": _np.concatenate([a["L1_ffn_b1"].reshape(-1), a["L1_ffn_b2"].reshape(-1),
                                 a["L2_ffn_conv_b"], a["L3_xattn_bo"]]).reshape(128, -1),
        "x": a["x"].reshape(-1, 128),
        "mask0": a["mask_Bx1xS2_if1"].reshape(1, 4, 32),
        "mask3": a["mask_BxSxS2_if1"].reshape(-1, 32).T,
        "fc0": a["L0_ffn_fc_w"],
        "pj0": a["L0_ffn_proj_w"],
        "fc1": a["L1_ffn_W1"],
        "pj1": a["L1_ffn_W2"],
        "fc3": a["L3_ffn_w_gate_up"],
        "pj3": a["L3_ffn_w_down"],
        "wkv": a["L2_xattn_Wkv"],
        "wq2": a["L2_xattn_Wq"],
        "wout2": a["L2_xattn_Wout"],
        "w1t": a["L2_ffn_w1"].T,
        "w2t": a["L2_ffn_w2"].T,
        "cw": a["L2_ffn_conv_w"][:, 0, :].T,
    }
    nc = _bacc.Bacc("TRN2", target_bir_lowering=False, num_devices=1)
    args, maps = [], {}
    for name, v in arrays.items():
        v = _np.ascontiguousarray(v)
        maps[f"in_{name}_dram"] = v
        args.append(nc.dram_tensor(f"in_{name}_dram", v.shape, _mybir.dt.from_np(v.dtype), kind="ExternalInput").ap())
    out = nc.dram_tensor("out_dram", (2048, 128), _mybir.dt.float32, kind="ExternalOutput").ap()
    build(nc, *args, out)
    r = _run(nc, [maps], core_ids=[0])
    return r.results[0]["out_dram"].reshape(4, 512, 128)
```
